# Optimizing a Trainium2 kernel written in Bass

```python
import numpy as np
import jax
import jax.numpy as jnp

def _softmax(x, axis=-1):
    return jax.nn.softmax(x, axis=axis)

def _gelu(x):
    return jax.nn.gelu(x, approximate=True)

def _silu(x):
    return jax.nn.silu(x)

def _sigmoid(x):
    return jax.nn.sigmoid(x)

def _layernorm(x, axis=-1, eps=1e-05):
    m = jnp.mean(x, axis=axis, keepdims=True)
    v = jnp.var(x, axis=axis, keepdims=True)
    return (x - m) / jnp.sqrt(v + eps)

def _scatter_add(tgt, idx, src, axis=0):
    return tgt.at[idx].add(src)

def _segment_sum(src, seg, n):
    return jax.ops.segment_sum(src, seg, n)
kernel_name = 'mk_vit_tower_d2_tok_img1024_r4_3082a7'

def setup_inputs(seed: int=0):
    np.random.seed(seed)
    _w = jnp.asarray

    def _rec_inputs():
        import jax
        import jax.numpy as jnp
        _rk = jax.random.key(seed)
        x = -0.00016672 + 0.999947 * jax.random.normal(jax.random.fold_in(_rk, 1), (64, 3, 128, 128), jnp.float32)
        return x
    x = _rec_inputs()

    def _L0_tok_setup():
        import jax, jax.numpy as jnp
        import numpy as np
        B, C, H, W_IMG = (64, 3, 96, 96)
        P = 16
        EMBED = 256
        PATCH_DIM = C * P * P
        key = jax.random.key(seed)
        k1, k2 = jax.random.split(key)
        x = jax.random.normal(k1, (B, C, H, W_IMG), dtype=jnp.float32)
        W = jax.random.normal(k2, (PATCH_DIM, EMBED), dtype=jnp.float32) * (1.0 / np.sqrt(PATCH_DIM))
        b = jnp.zeros((EMBED,), dtype=jnp.float32)
        return {'x': x, 'W': W, 'b': b}
    _L0_tok_all = _L0_tok_setup()
    _L0_tok_in = {k: v for k, v in _L0_tok_all.items() if k in ('W', 'b')}
    del _L0_tok_all

    def _L0_attn_setup():
        import jax, jax.numpy as jnp
        import numpy as np
        B, L, E, H = (4, 256, 256, 16)
        D = E // H
        SPARSITY = 0.4
        NEG_INF = jnp.float32(-1e+30)
        key = jax.random.key(seed)
        ks = jax.random.split(key, 8)
        s = 0.02
        return {'hidden_states': jax.random.normal(ks[0], (B, L, E), jnp.float32), 'qkv_w': jax.random.normal(ks[1], (3 * E, E), jnp.float32) * s, 'qkv_b': jax.random.normal(ks[2], (3 * E,), jnp.float32) * s, 'r_w1': jax.random.normal(ks[3], (E // 4, E), jnp.float32) * s, 'r_b1': jax.random.normal(ks[4], (E // 4,), jnp.float32) * s, 'r_w2': jax.random.normal(ks[5], (H, E // 4), jnp.float32) * s, 'r_b2': jax.random.normal(ks[6], (H,), jnp.float32) * s}
    _L0_attn_all = _L0_attn_setup()
    _L0_attn_in = {k: v for k, v in _L0_attn_all.items() if k in ('qkv_w', 'qkv_b', 'r_w1', 'r_b1', 'r_w2', 'r_b2')}
    del _L0_attn_all

    def _L0_ffn_setup():
        import jax, jax.numpy as jnp
        import numpy as np
        E = 8
        G = 4
        LG = 2
        TOPK = 2
        ROUTE_SCALE = 1.0

        def _grouped_mm(x, w, counts):
            counts = counts.astype(jnp.int32)
            if hasattr(jax.lax, 'ragged_dot'):
                return jax.lax.ragged_dot(x, w, counts)
            offs = jnp.cumsum(counts)
            eid = jnp.searchsorted(offs, jnp.arange(x.shape[0]), side='right')
            oh = jax.nn.one_hot(eid, w.shape[0], dtype=x.dtype)
            return jnp.einsum('nd,ne,edh->nh', x, oh, w)
        key = jax.random.key(seed)
        ks = jax.random.split(key, 8)
        bs, slen, dim, hid, shid = (2, 512, 256, 128, 256)
        std = 0.02
        return {'x': jax.random.normal(ks[0], (bs, slen, dim), jnp.float32), 'w_gate': jax.random.normal(ks[1], (E, dim), jnp.float32) * std, 'w1': jax.random.normal(ks[2], (E, dim, hid), jnp.float32) * std, 'w2': jax.random.normal(ks[3], (E, hid, dim), jnp.float32) * std, 'w3': jax.random.normal(ks[4], (E, dim, hid), jnp.float32) * std, 'sw1': jax.random.normal(ks[5], (shid, dim), jnp.float32) * std, 'sw2': jax.random.normal(ks[6], (dim, shid), jnp.float32) * std, 'sw3': jax.random.normal(ks[7], (shid, dim), jnp.float32) * std, 'expert_bias': jnp.zeros((E,), jnp.float32)}
    _L0_ffn_all = _L0_ffn_setup()
    _L0_ffn_in = {k: v for k, v in _L0_ffn_all.items() if k in ('w_gate', 'w1', 'w2', 'w3', 'sw1', 'sw2', 'sw3', 'expert_bias')}
    del _L0_ffn_all

    def _L1_attn_setup():
        import math
        import jax, jax.numpy as jnp
        import numpy as np
        N_HEAD = 16
        X_INT = -100.0
        Y_INT = 1.0
        POWER = 2
        DIVISOR = 1000.0

        def polymax(x):
            m = Y_INT / X_INT
            lin_cond = (x >= X_INT) & (x <= 0)
            x_lin = jnp.where(lin_cond, x, 0.0)
            lin = jnp.where(lin_cond, m * x_lin + Y_INT, 0.0)
            pos_cond = x > 0
            x_pos = jnp.where(pos_cond, x, 0.0)
            poly = jnp.where(pos_cond, x_pos ** POWER + Y_INT, 0.0)
            return (poly + lin) / DIVISOR
        key = jax.random.key(seed)
        k1, k2, k3 = jax.random.split(key, 3)
        B, T, C = (2, 512, 256)
        x = jax.random.normal(k1, (B, T, C), dtype=jnp.float32)
        W_attn = jax.random.normal(k2, (C, 3 * C), dtype=jnp.float32) * (1.0 / math.sqrt(C))
        W_proj = jax.random.normal(k3, (C, C), dtype=jnp.float32) * (1.0 / math.sqrt(C))
        return {'x': x, 'W_attn': W_attn, 'W_proj': W_proj}
    _L1_attn_all = _L1_attn_setup()
    _L1_attn_in = {k: v for k, v in _L1_attn_all.items() if k in ('W_attn', 'W_proj')}
    del _L1_attn_all

    def _L1_ffn_setup():
        import jax, jax.numpy as jnp
        import numpy as np
        EPS = 1e-08

        def _ternary_linear(x, w):
            alpha = jnp.mean(jnp.abs(w))
            w_t = jnp.sign(w) * (jnp.abs(w) > 0.5 * alpha).astype(w.dtype)
            w_q = w + jax.lax.stop_gradient(w_t - w)
            d = x.shape[-1]
            rms = jnp.sqrt(jnp.sum(x * x, axis=-1, keepdims=True)) / jnp.sqrt(jnp.asarray(d, x.dtype))
            x_norm = x / (rms + EPS)
            return jnp.einsum('bsd,fd->bsf', x_norm, w_q)
        key = jax.random.key(seed)
        k1, k2, k3 = jax.random.split(key, 3)
        d_model, d_ff = (256, 1024)
        B, S = (4, 1024)
        x = jax.random.normal(k1, (B, S, d_model), dtype=jnp.float32)
        w_up = jax.random.normal(k2, (d_ff, d_model), dtype=jnp.float32) * 0.02
        w_down = jax.random.normal(k3, (d_model, d_ff), dtype=jnp.float32) * 0.02
        return {'x': x, 'w_up': w_up, 'w_down': w_down}
    _L1_ffn_all = _L1_ffn_setup()
    _L1_ffn_in = {k: v for k, v in _L1_ffn_all.items() if k in ('w_up', 'w_down')}
    del _L1_ffn_all
    return {'x': x, 'L0_tok_W': _L0_tok_in['W'], 'L0_tok_b': _L0_tok_in['b'], 'L0_attn_qkv_w': _L0_attn_in['qkv_w'], 'L0_attn_qkv_b': _L0_attn_in['qkv_b'], 'L0_attn_r_w1': _L0_attn_in['r_w1'], 'L0_attn_r_b1': _L0_attn_in['r_b1'], 'L0_attn_r_w2': _L0_attn_in['r_w2'], 'L0_attn_r_b2': _L0_attn_in['r_b2'], 'L0_ffn_w_gate': _L0_ffn_in['w_gate'], 'L0_ffn_w1': _L0_ffn_in['w1'], 'L0_ffn_w2': _L0_ffn_in['w2'], 'L0_ffn_w3': _L0_ffn_in['w3'], 'L0_ffn_sw1': _L0_ffn_in['sw1'], 'L0_ffn_sw2': _L0_ffn_in['sw2'], 'L0_ffn_sw3': _L0_ffn_in['sw3'], 'L0_ffn_expert_bias': _L0_ffn_in['expert_bias'], 'L1_attn_W_attn': _L1_attn_in['W_attn'], 'L1_attn_W_proj': _L1_attn_in['W_proj'], 'L1_ffn_w_up': _L1_ffn_in['w_up'], 'L1_ffn_w_down': _L1_ffn_in['w_down']}

def reference(x, L0_tok_W, L0_tok_b, L0_attn_qkv_w, L0_attn_qkv_b, L0_attn_r_w1, L0_attn_r_b1, L0_attn_r_w2, L0_attn_r_b2, L0_ffn_w_gate, L0_ffn_w1, L0_ffn_w2, L0_ffn_w3, L0_ffn_sw1, L0_ffn_sw2, L0_ffn_sw3, L0_ffn_expert_bias, L1_attn_W_attn, L1_attn_W_proj, L1_ffn_w_up, L1_ffn_w_down):
    import jax
    import jax.numpy as jnp

    def _L0_tok_ref(x, W, b):
        import jax, jax.numpy as jnp
        import numpy as np
        B, C, H, W_IMG = (64, 3, 96, 96)
        P = 16
        EMBED = 256
        PATCH_DIM = C * P * P
        Bn, Cn, Hn, Wn = x.shape
        gh, gw = (Hn // P, Wn // P)
        patches = x.reshape(Bn, Cn, gh, P, gw, P)
        patches = patches.transpose(0, 2, 4, 1, 3, 5)
        patches = patches.reshape(Bn, gh * gw, Cn * P * P)
        return jnp.einsum('bnd,de->bne', patches, W) + b

    def _L0_attn_ref(hidden_states, qkv_w, qkv_b, r_w1, r_b1, r_w2, r_b2):
        import jax, jax.numpy as jnp
        import numpy as np
        B, L, E, H = (4, 256, 256, 16)
        D = E // H
        SPARSITY = 0.4
        NEG_INF = jnp.float32(-1e+30)
        bsz, tgt_len, embed_dim = hidden_states.shape
        qkv = (hidden_states @ qkv_w.T + qkv_b).reshape(bsz, tgt_len, 3, H, D)
        qkv = jnp.transpose(qkv, (2, 0, 3, 1, 4))
        q, k, v = (qkv[0], qkv[1], qkv[2])
        h1 = jax.nn.relu(hidden_states @ r_w1.T + r_b1)
        routing_logits = jax.nn.sigmoid(h1 @ r_w2.T + r_b2)
        routing_scores = jax.nn.sigmoid(routing_logits)
        attn = jnp.einsum('bhqd,bhkd->bhqk', q, k) / jnp.sqrt(jnp.float32(D))
        k_keep = max(1, int(tgt_len * SPARSITY))
        rs_t = jnp.transpose(routing_scores, (0, 2, 1))
        _, top_idx = jax.lax.top_k(rs_t, k_keep)
        keep = jnp.zeros((bsz, H, tgt_len), dtype=bool)
        keep = keep.at[jnp.arange(bsz)[:, None, None], jnp.arange(H)[None, :, None], top_idx].set(True)
        sparse = jnp.where(keep[:, :, None, :], attn, NEG_INF)
        w = jax.nn.softmax(sparse.astype(jnp.float32), axis=-1).astype(q.dtype)
        out = jnp.einsum('bhqk,bhkd->bhqd', w, v)
        out = jnp.transpose(out, (0, 2, 1, 3)).reshape(bsz, tgt_len, embed_dim)
        return out

    def _L0_ffn_ref(x, w_gate, w1, w2, w3, sw1, sw2, sw3, expert_bias):
        import jax, jax.numpy as jnp
        import numpy as np
        E = 8
        G = 4
        LG = 2
        TOPK = 2
        ROUTE_SCALE = 1.0

        def _grouped_mm(x, w, counts):
            counts = counts.astype(jnp.int32)
            if hasattr(jax.lax, 'ragged_dot'):
                return jax.lax.ragged_dot(x, w, counts)
            offs = jnp.cumsum(counts)
            eid = jnp.searchsorted(offs, jnp.arange(x.shape[0]), side='right')
            oh = jax.nn.one_hot(eid, w.shape[0], dtype=x.dtype)
            return jnp.einsum('nd,ne,edh->nh', x, oh, w)
        bs, slen, dim = x.shape
        xf = x.reshape(-1, dim)
        N = xf.shape[0]
        logits = xf @ w_gate.T
        scores = jax.nn.softmax(logits.astype(jnp.float32), axis=-1)
        original = scores
        s = (scores + expert_bias).reshape(N, G, E // G)
        group_scores = jax.lax.top_k(s, 2)[0].sum(-1)
        top_groups = jax.lax.top_k(group_scores, LG)[1]
        keep = jnp.zeros((N, G), bool).at[jnp.arange(N)[:, None], top_groups].set(True)
        masked = jnp.where(keep[:, :, None], s, -jnp.inf).reshape(N, E)
        topk_idx = jax.lax.top_k(masked, TOPK)[1]
        weights = (jnp.take_along_axis(original, topk_idx, axis=1) * ROUTE_SCALE).astype(x.dtype)
        counts = jnp.bincount(topk_idx.reshape(-1), length=E)
        flat_idx = topk_idx.reshape(-1)
        routed_in = xf[flat_idx]
        routed_in = (routed_in.astype(jnp.float32) * weights.reshape(-1, 1)).astype(x.dtype)
        h = jax.nn.silu(_grouped_mm(routed_in, w1, counts)) * _grouped_mm(routed_in, w3, counts)
        routed_out = _grouped_mm(h, w2, counts)
        shared = jax.nn.silu(xf @ sw1.T) * (xf @ sw3.T) @ sw2.T
        out = shared.at[flat_idx].add(routed_out)
        return out.reshape(bs, slen, dim)

    def _L1_attn_ref(x, W_attn, W_proj):
        import math
        import jax, jax.numpy as jnp
        import numpy as np
        N_HEAD = 16
        X_INT = -100.0
        Y_INT = 1.0
        POWER = 2
        DIVISOR = 1000.0

        def polymax(x):
            m = Y_INT / X_INT
            lin_cond = (x >= X_INT) & (x <= 0)
            x_lin = jnp.where(lin_cond, x, 0.0)
            lin = jnp.where(lin_cond, m * x_lin + Y_INT, 0.0)
            pos_cond = x > 0
            x_pos = jnp.where(pos_cond, x, 0.0)
            poly = jnp.where(pos_cond, x_pos ** POWER + Y_INT, 0.0)
            return (poly + lin) / DIVISOR
        B, T, C = x.shape
        H = N_HEAD
        hd = C // H
        qkv = x @ W_attn
        q, k, v = jnp.split(qkv, 3, axis=-1)
        q = q.reshape(B, T, H, hd).transpose(0, 2, 1, 3)
        k = k.reshape(B, T, H, hd).transpose(0, 2, 1, 3)
        v = v.reshape(B, T, H, hd).transpose(0, 2, 1, 3)
        att = jnp.einsum('bhid,bhjd->bhij', q, k) * (1.0 / math.sqrt(hd))
        causal = jnp.tril(jnp.ones((T, T), dtype=bool))
        att = jnp.where(causal[None, None], att, -jnp.inf)
        att = polymax(att)
        y = jnp.einsum('bhij,bhjd->bhid', att, v)
        y = y.transpose(0, 2, 1, 3).reshape(B, T, C)
        return y @ W_proj

    def _L1_ffn_ref(x, w_up, w_down):
        import jax, jax.numpy as jnp
        import numpy as np
        EPS = 1e-08

        def _ternary_linear(x, w):
            alpha = jnp.mean(jnp.abs(w))
            w_t = jnp.sign(w) * (jnp.abs(w) > 0.5 * alpha).astype(w.dtype)
            w_q = w + jax.lax.stop_gradient(w_t - w)
            d = x.shape[-1]
            rms = jnp.sqrt(jnp.sum(x * x, axis=-1, keepdims=True)) / jnp.sqrt(jnp.asarray(d, x.dtype))
            x_norm = x / (rms + EPS)
            return jnp.einsum('bsd,fd->bsf', x_norm, w_q)
        h = jax.nn.gelu(_ternary_linear(x, w_up), approximate=False)
        return _ternary_linear(h, w_down)
    h = _L0_tok_ref(x, L0_tok_W, L0_tok_b)
    h = h + _L0_attn_ref(_layernorm(h, axis=-1), L0_attn_qkv_w, L0_attn_qkv_b, L0_attn_r_w1, L0_attn_r_b1, L0_attn_r_w2, L0_attn_r_b2)
    h = h + _L0_ffn_ref(_layernorm(h, axis=-1), L0_ffn_w_gate, L0_ffn_w1, L0_ffn_w2, L0_ffn_w3, L0_ffn_sw1, L0_ffn_sw2, L0_ffn_sw3, L0_ffn_expert_bias)
    h = h + _L1_attn_ref(_layernorm(h, axis=-1), L1_attn_W_attn, L1_attn_W_proj)
    h = h + _L1_ffn_ref(_layernorm(h, axis=-1), L1_ffn_w_up, L1_ffn_w_down)
    return h

_drawn_inputs = setup_inputs


def setup_inputs(seed=0):
    import zlib

    import numpy as np

    out = dict(_drawn_inputs(seed))
    spreads = {'L0_tok_b': (0.0, 0.1), 'L0_ffn_expert_bias': (0.0, 0.696)}
    factors = {'L0_attn_qkv_b': 2.693,
     'L0_attn_r_b1': 4.347,
     'L0_ffn_w_gate': 8.0,
     'L0_ffn_w1': 5.468,
     'L0_ffn_w2': 5.026,
     'L0_ffn_w3': 4.73,
     'L0_ffn_sw1': 3.636,
     'L0_ffn_sw2': 3.607,
     'L0_ffn_sw3': 3.601,
     'L1_attn_W_attn': 4.519,
     'L1_attn_W_proj': 4.489}
    for name, (base, spread) in spreads.items():
        noise = np.random.default_rng([zlib.crc32(name.encode()), seed]).standard_normal(out[name].shape)
        drawn = base * np.exp(spread * noise) if base else spread * noise
        out[name] = jnp.asarray(drawn.astype(out[name].dtype))
    for name, factor in factors.items():
        out[name] = (out[name] * factor).astype(out[name].dtype)
    return out
```

```python
from contextlib import ExitStack

import numpy as np

import concourse.bass as bass
from concourse import mybir

ALU = mybir.AluOpType
ACT = mybir.ActivationFunctionType
AX = mybir.AxisListType
F32 = mybir.dt.float32
BF16 = mybir.dt.bfloat16

P = 128
SLOTS = 8
IMGS = 8
L = 64
TILES = 4
TOK = IMGS * L
E = 256
C = E // P
NH = 16
HD = E // NH
HP = NH // 2
KEEP = int(L * 0.4)
KP = 6
NX = 8
HID = 128
FF = 1024
NF = FF // P
NEG = -1e30
EPS = 1e-5
VW = HD + 1
BIG = 3e38
PV0 = 7 * 512 - 4 * 4 * VW
SETUP_V = 10
TOP = 2 * (KEEP // 8) + 4
TAKEN = -4.0


def build(nc, x, tokW, tokb, wqkv, bqk, bv, rW1, rb1, rW2, rb2, gateW, eb, w1, w3, w2, s1, s3, s2,
          wat, wpr, wup, wdn, ident, par, sel, delta, rev64, cmask, ridx, iota64, rev8, out):
    with ExitStack() as ctx:
        def sb(name, shape, dt=F32):
            return ctx.enter_context(nc.sbuf_tensor(name, shape, dt))

        def sem(name):
            return ctx.enter_context(nc.semaphore(name))

        PS = ctx.enter_context(nc.psum_tensor("PS", [P, 8, 512], F32))
        PF = PS[:, :, :].rearrange("p b n -> p (b n)")

        tokW_s = sb("tokW_s", [P, KP, E]); tokb_s = sb("tokb_s", [P, E])
        wqkv_s = sb("wqkv_s", [P, C, 3 * E]); bqk_s = sb("bqk_s", [P, 4]); bv_s = sb("bv_s", [P, E])
        rW1_s = sb("rW1_s", [P, C, 64]); rb1_s = sb("rb1_s", [64, 1])
        rW2_s = sb("rW2_s", [64, IMGS, P]); rb2_s = sb("rb2_s", [P, 1]); rb2h = sb("rb2h", [P, 1])
        gateW_s = sb("gateW_s", [P, C, NX]); eb_s = sb("eb_s", [P, NX])
        s1_s = sb("s1_s", [P, C, E]); s3_s = sb("s3_s", [P, C, E]); s2_s = sb("s2_s", [P, C, E])
        w1_s = sb("w1_s", [P, NX, C, HID]); w3_s = sb("w3_s", [P, NX, C, HID]); w2_s = sb("w2_s", [P, NX, E])
        wat_s = sb("wat_s", [P, C, 3 * E]); wpr_s = sb("wpr_s", [P, C, E])
        wup_s = sb("wup_s", [P, C, FF]); wdn_s = sb("wdn_s", [P, NF, E])
        ident_s = sb("ident_s", [P, P]); identb = sb("identb", [P, P], BF16)
        par_s = sb("par_s", [P, 4])
        self_ = sb("self_", [P, TILES, P]); selb = sb("selb", [P, TILES, P], BF16)
        delta_s = sb("delta_s", [P, NH]); rev64_s = sb("rev64_s", [P, L])
        cmask_s = sb("cmask_s", [P, 4, L]); cmaskb = sb("cmaskb", [P, 4, L], BF16)
        ridx_s = sb("ridx_s", [P, 64]); iota_s = sb("iota_s", [P, 64]); rev8_s = sb("rev8_s", [P, NX])
        ones = sb("ones", [P, P]); mhalf = sb("mhalf", [P, 4]); phalf = sb("phalf", [P, 4])

        H = sb("H", [P, SLOTS * TILES, E])
        work = sb("work", [P, NF, TOK])
        patch = work[:, 0:KP, :]
        G = work
        st = sb("st", [P, TILES, 6]); mv = sb("mv", [P, TILES, 2])
        st2 = sb("st2", [P, TILES, 6]); mv2 = sb("mv2", [P, TILES, 2])
        ve = sb("ve", [P, TILES]); rstd = sb("rstd", [P, TILES])
        ve2 = sb("ve2", [P, TILES]); rstd2 = sb("rstd2", [P, TILES])
        xn1 = sb("xn1", [P, TILES, E]); xn2 = sb("xn2", [P, TILES, E])
        xT1 = sb("xT1", [P, C, TOK + L]); xT2 = sb("xT2", [P, C, TOK])
        qT = sb("qT", [P, C, TOK]); kM = sb("kM", [P, C, 2, TOK])
        vbuf = sb("vbuf", [P, TILES * HP * 2 * 2 * VW])
        Vb = vbuf[:, :].rearrange("p (t hp b e v) -> p t hp b e v", t=TILES, hp=HP, b=2, e=2)
        V2 = vbuf[:, 0:TILES * NH * 2 * HD].rearrange("p (t h b d) -> p t h b d", t=TILES, h=NH, b=2)
        h1T = sb("h1T", [64, TOK])
        t1 = sb("t1", [P, L]); sg1 = sb("sg1", [P, L]); t2 = sb("t2", [P, L]); sg2 = sb("sg2", [P, L])
        wk = [sb(f"wk{i}", [P, L]) for i in range(3)]
        m8 = [sb(f"m8_{i}", [P, 8]) for i in range(5)]
        cand = sb("cand", [P, L]); selk = sb("selk", [P, L]); keep = sb("keep", [P, L]); bias = sb("bias", [P, L])
        mb = sb("mb", [P, NH, L], BF16)
        mx = sb("mx", [P, 2, NH])
        Pm = sb("Pm", [P, 2, NH * L]); PT = sb("PT", [P, 2, HP, P])
        rden = sb("rden", [P, NH]); yn = sb("yn", [P, E])
        th = sb("th", [P, C * TOK]); u = sb("u", [P, C * TOK]); hs = sb("hs", [P, C * TOK])
        sabs = sb("sabs", [P, 2]); thr = sb("thr", [P, 2]); nthr = sb("nthr", [P, 2])
        vr = sb("vr", [P, TILES]); rq = sb("rq", [P, TILES]); rr = sb("rr", [P, TILES]); r4 = sb("r4", [P, TILES])
        msq = sb("msq", [P, TILES]); rg = sb("rg", [P, TILES]); rge = sb("rge", [P, TILES]); rgi = sb("rgi", [P, TILES])
        lg = sb("lg", [P, SLOTS * TILES, NX])


        NT = SLOTS * TILES
        flat = Pm[:, :, :].rearrange("p a n -> p (a n)")
        rs = {n: flat[:, k * NT * NX:(k + 1) * NT * NX]
              for k, n in enumerate(("ex", "pr", "s", "m", "a", "b", "oh1", "oh2"))}
        r3 = {n: v[:, :].rearrange("p (t e) -> p t e", e=NX) for n, v in rs.items()}
        rsm = {n: sb("rv_" + n, [P, NT]) for n in ("mx", "sum", "inv", "m1", "c1", "m2", "c2")}
        gs, wins, gk, gd = (th[:, k * NT * 4:(k + 1) * NT * 4].rearrange("p (t g) -> p t g", g=4) for k in range(4))
        cmp = sb("cmp", [P, NT])
        wt = sb("wt", [P, 2 * NT]); ei = sb("ei", [P, 2 * NT]); gg = sb("gg", [P, 2 * NT])
        code = sb("code", [P, 2 * NT])
        cnt = sb("cnt", [P, NX]); off = sb("off", [P, NX])
        AC = [sb("AT", [P, 64]), sb("CT", [P, 64])]
        tabA = sb("tabA", [64, HID]); tabC = sb("tabC", [64, HID])
        ow = work[:, 0, :].rearrange("p (b n r) -> p b n r", b=2, n=4)
        owT = work[0:64, 1:3, :]
        tz, sz = work[:, 3:5, :], work[:, 5:7, :]
        racc = sb("racc", [64, HID]); gm = sb("gm", [64, HID]); gT = sb("gT", [P, 64])
        QUADS = 2 * NT // 4

        kT = qT
        qM = kM
        F = Pm
        relu_s = (th, hs)
        lin = (u, w1_s[:, :, :, :].rearrange("p e c h -> p (e c h)")[:, 0:NH * L])
        sqt = (PT[:, 0, 0:4, :], PT[:, 0, 4:8, :])
        sqa = PT[:, 1, 0:4, :]

        def sems(names):
            return (sem(n) for n in names.split())

        Bk_mm, Bk_out, Bq_mm, Bq_out, Bs_mm, Bv_mm = sems("Bk_mm Bk_out Bq_mm Bq_out Bs_mm Bv_mm")
        Bv_out, V2_zero, Y_mm, Y_out, a_mm, abs_mm = sems("Bv_out V2_zero Y_mm Y_out a_mm abs_mm")
        abs_ok, acc_mm, b_mm, bias_ok, cnt_mm, cnt_ok = sems("abs_ok acc_mm b_mm bias_ok cnt_mm cnt_ok")
        dn_mm, embed_out, embed_mm, f0_ok, f2_ok, gT_mm = sems("dn_mm embed_out embed_mm f0_ok f2_ok gT_mm")
        gT_ok, g_ok, gate_mm, gex_ok, gl_ok, gm_ok = sems("gT_ok g_ok gate_mm gex_ok gl_ok gm_ok")
        h1_mm, h1_out, h2_ok, h3_ok, h4_ok, h5_ok, hs_ok = sems("h1_mm h1_out h2_ok h3_ok h4_ok h5_ok hs_ok")
        k_mm, k_out, keep_ok, lg_ok, lin_ok, loaded = sems("k_mm k_out keep_ok lg_ok lin_ok loaded")
        mb_ok, msq_ok, owT_mm, owT_ok, ow_ok, p_exp = sems("mb_ok msq_ok owT_mm owT_ok ow_ok p_exp")
        p_sub, patch_in, pr_mm, pt_mm, pt_out, pv_mm = sems("p_sub patch_in pr_mm pt_mm pt_out pv_mm")
        q_mm, q_out, quad_ok, r4_step, r8_mm, r8_ok = sems("q_mm q_out quad_ok r4_step r8_mm r8_ok")
        racc_ok, rden_ok, relu_ok, rg_ok, rg_step, rl_mm = sems("racc_ok rden_ok relu_ok rg_ok rg_step rl_mm")
        routed_step, rsg1, rstd1_ok, rstd2_ok, rstd3_ok, rstd4_ok = sems("routed_step rsg1 rstd1_ok rstd2_ok rstd3_ok rstd4_ok")
        rt1, rt2, rw2_zero, s_mm, selk_ok, setup_v = sems("rt1 rt2 rw2_zero s_mm selk_ok setup_v")
        sh_mm, smax, sq_ok, sqa_ok, ss_mm, stored, sz_ok = sems("sh_mm smax sq_ok sqa_ok ss_mm stored sz_ok")
        tabT_ok, tab_mm, tab_ok, tab_t, th_neg, th_ok = sems("tabT_ok tab_mm tab_ok tab_t th_neg th_ok")
        th_set, thr_ok, top_step, tz_ok, u_ok, up_mm = sems("th_set thr_ok top_step tz_ok u_ok up_mm")
        v_mm, v_out, ve1_mv, ve1_ok, ve1_st, ve2_mv = sems("v_mm v_out ve1_mv ve1_ok ve1_st ve2_mv")
        ve2_ok, ve2_st, ve3_mv, ve3_ok, ve3_st, ve4_mv = sems("ve2_ok ve2_st ve3_mv ve3_ok ve3_st ve4_mv")
        ve4_ok, ve4_st, x3T_a, x3T_mm, x3T_v, x4T_a = sems("ve4_ok ve4_st x3T_a x3T_mm x3T_v x4T_a")
        x4T_mm, x4T_v, xT1_a, xT1_mm, xT1_v, xT2_a = sems("x4T_mm x4T_v xT1_a xT1_mm xT1_v xT2_a")
        xT2_mm, xT2_v, xn1_ok, xn2_ok, xn3_ok, xn4_ok = sems("xT2_mm xT2_v xn1_ok xn2_ok xn3_ok xn4_ok")
        yT_mm, yT_out, y_out, z_mm = sems("yT_mm yT_out y_out z_mm")

        def first(g):
            return isinstance(g, int) and g == 0

        def in_reg(eng, value):
            return value if isinstance(value, int) else eng.to_reg(value)

        steps = {}

        def after(chain, n=1):
            steps[chain] = steps.get(chain, 0) + n
            return steps[chain]

        loads = [(tokW_s, tokW), (tokb_s, tokb), (wqkv_s, wqkv), (bqk_s, bqk), (bv_s, bv), (rW1_s, rW1),
                 (rb1_s, rb1), (rb2_s, rb2), (gateW_s, gateW), (eb_s, eb), (s1_s, s1), (s3_s, s3), (s2_s, s2),
                 (w1_s, w1), (w3_s, w3), (w2_s, w2), (wat_s, wat), (wpr_s, wpr), (wup_s, wup), (wdn_s, wdn),
                 (ident_s, ident), (par_s, par), (self_, sel), (delta_s, delta), (rev64_s, rev64),
                 (cmask_s, cmask), (ridx_s, ridx), (iota_s, iota64), (rev8_s, rev8)]
        N_LOADED = 16 * (len(loads) + IMGS)
        LAST = SLOTS - 1
        block = ctx.enter_context(nc.Block())

        @block.sync
        def _(sp):
            def load_patches(g):
                sp.dma_start(patch, x[g, :, :, :]).then_inc(patch_in, 16)

            load_patches(0)
            sp.wait_ge(rw2_zero, 1)
            for j in range(IMGS):
                sp.dma_start(rW2_s[:, j, NH * j:NH * (j + 1)], rW2).then_inc(loaded, 16)
            for dst, src in loads:
                sp.dma_start(dst[:], src).then_inc(loaded, 16)
            with sp.Fori(0, LAST) as i:
                sp.wait_ge(embed_mm, TILES * i + TILES)
                load_patches(i + 1)
            with sp.Fori(0, SLOTS) as i:
                sp.wait_ge(h5_ok, TILES * i + TILES + 1)
                sp.dma_start(out[i, :, :, :], H[:, bass.ds(TILES * i, TILES), :]).then_inc(stored, 16)
            sp.wait_ge(stored, 16 * SLOTS)

        @block.tensor
        def _(pe):
            def embed(g):
                pe.wait_ge(patch_in, 16 * g + 16)
                for t in range(TILES):
                    for k in range(KP):
                        m = pe.matmul(PS[:, 4 + t // 2, (t % 2) * E:(t % 2 + 1) * E],
                                      patch[:, k, t * P:(t + 1) * P], tokW_s[:, k, :],
                                      start=(k == 0), stop=(k == KP - 1))
                    m.then_inc(embed_mm, 1)

            def transpose_in(g, xn, banks, ready, done):
                banks = banks if isinstance(banks, tuple) else (banks, banks + 1)
                for c in range(C):
                    for t in range(TILES):
                        if c == 0:
                            pe.wait_ge(ready, TILES * g + t + 1)
                        m = pe.transpose(PS[:, banks[c], t * P:(t + 1) * P], xn[:, t, c * P:(c + 1) * P],
                                         ident_s[:, :])
                    m.then_inc(done, 1)

            def proj_T(bank, w, col, xT, done, cols=P):
                for c in range(C):
                    m = pe.matmul(PS[0:cols, bank, :], w[:, c, col:col + cols], xT[:, c, 0:TOK],
                                  start=(c == 0), stop=(c == C - 1))
                m.then_inc(done, 1)

            def A2(g):
                transpose_in(g, xn1, 4, xn1_ok, xT1_mm)
                pe.wait_ge(xT1_a, 2 * g + 2)
                pe.wait_ge(xT1_v, 2 * g + 2)
                if not first(g):
                    pe.wait_ge(y_out, 2 * TILES * g)
                for c in range(C):
                    proj_T(6 + c, wqkv_s, c * P, xT1, q_mm)
                if not first(g):
                    pe.wait_ge(p_sub, TILES * g)
                for c in range(C):
                    proj_T(c, wqkv_s, E + c * P, xT1, k_mm)
                proj_T(4, rW1_s, 0, xT1, h1_mm, 64)
                for n in range(TILES):
                    value_rows(2 + n // 2, n % 2, n * P)
                pe.wait_ge(h1_out, g + 1)
                for j in range(IMGS):
                    m = pe.matmul(PS[:, 5, 0:L], rW2_s[:, j, :], h1T[:, j * L:(j + 1) * L],
                                  start=(j == 0), stop=(j == IMGS - 1))
                m.then_inc(rl_mm, 1)
                pe.wait_ge(k_out, 4 * g + 4)
                for n in range(TILES):
                    value_rows(n // 2, n % 2, n * P + L)

            def value_rows(bank, half, at):
                for c in range(C):
                    m = pe.matmul(PS[:, bank, half * E:(half + 1) * E], xT1[:, c, at:at + P],
                                  wqkv_s[:, c, 2 * E:3 * E], start=(c == 0), stop=(c == C - 1))
                m.then_inc(v_mm, 1)

            def image_scores(t, left, right, hb):
                for b in range(2):
                    for c in range(C):
                        for i in range(4):
                            at, r = t * P + b * L, slice(32 * i, 32 * i + 32)
                            m = pe.matmul(PS[b * L:(b + 1) * L, i, hb + c * P:hb + (c + 1) * P],
                                          left[r, c, at:at + L], right[r, c, :, at:at + L],
                                          start=False, stop=True, tile_position=(32 * i, b * L),
                                          skip_group_check=True)
                return m

            def scores(g, pair):
                if pair == 0:
                    pe.wait_ge(mb_ok, g + 1)
                    pe.wait_ge(q_out, 2 * g + 2)
                    pe.wait_ge(v_out, 5 * g + 5)
                else:
                    pe.wait_ge(p_sub, TILES * g + 2)
                for t in (2 * pair, 2 * pair + 1):
                    hb = (t % 2) * 256
                    for i in range(4):
                        pe.matmul(PS[:, i, hb:hb + 256], selb[:, t, :], mb[:, 4 * i:4 * i + 4, :],
                                  start=True, stop=False, skip_group_check=True)
                    image_scores(t, qT, kM, hb).then_inc(s_mm, 1)

            def weights_T(g, t):
                pe.wait_ge(p_exp, TILES * g + t + 1)
                if t == 2:
                    pe.wait_ge(embed_out, embedded[0])
                elif t:
                    pe.wait_ge(pt_out, TILES * g + t)
                for hp in range(HP):
                    m = pe.transpose(PS[:, 4 + hp // 4, (hp % 4) * P:(hp % 4 + 1) * P],
                                     Pm[:, t % 2, hp * P:(hp + 1) * P], ident_s[:, :])
                m.then_inc(pt_mm, 1)

            def values(g, t):
                pe.wait_ge(pt_out, TILES * g + t + 1)
                if t:
                    pe.wait_ge(y_out, 2 * (TILES * g + t))
                for hp in range(HP):
                    at = PV0 + hp * 4 * VW
                    m = pe.matmul(PF[:, at:at + 4 * VW], PT[:, t % 2, hp, :], Vb[:, t, hp, :, :, :],
                                  start=True, stop=True)
                m.then_inc(pv_mm, 1)

            embedded = [0]

            def attend(g, pair):
                for t in (2 * pair, 2 * pair + 1):
                    weights_T(g, t)
                    values(g, t)

            def A4(g, last):
                if last:
                    pe.wait_ge(y_out, 2 * TILES * (g + 1))
                else:
                    pe.wait_ge(q_out, 2 * g + 4)
                transpose_in(g, xn2, 6, xn2_ok, xT2_mm)
                pe.wait_ge(xT2_a, g + 1)
                pe.wait_ge(xT2_v, g + 1)
                if last:
                    pe.wait_ge(pt_out, TILES * (g + 1))
                else:
                    pe.wait_ge(h1_out, g + 2)
                for t in range(TILES):
                    for c in range(C):
                        m = pe.matmul(PS[:, 4, t * NX:(t + 1) * NX], xT2[:, c, t * P:(t + 1) * P],
                                      gateW_s[:, c, :], start=(c == 0), stop=(c == C - 1))
                m.then_inc(gate_mm, 1)
                if not last:
                    pe.wait_ge(rt1, g + 2)
                proj_T(5, s1_s, 0, xT2, a_mm)
                proj_T(6, s3_s, 0, xT2, b_mm)
                proj_T(7, s1_s, P, xT2, a_mm)
                pe.wait_ge(lg_ok, g + 1)
                proj_T(4, s3_s, P, xT2, b_mm)
                if not last:
                    scores(g + 1, 0)
                pe.wait_ge(hs_ok, 2 * g + 2)
                for t in range(TILES):
                    for c in range(C):
                        m = pe.matmul(PS[:, 5 + t // 2, (t % 2) * E:(t % 2 + 1) * E],
                                      hs[:, c * TOK + t * P:c * TOK + (t + 1) * P], s2_s[:, c, :],
                                      start=(c == 0), stop=(c == C - 1))
                    m.then_inc(sh_mm, 1)

            pe.wait_ge(loaded, N_LOADED)
            pe.wait_ge(setup_v, SETUP_V)
            pe.wait_ge(abs_ok, 2)
            pe.matmul(PS[:, 0, 0:2], ones[:, :], sabs[:, :], start=True, stop=True).then_inc(abs_mm, 1)
            pe.wait_ge(thr_ok, 2)
            embed(0)
            A2(0)
            scores(0, 0)
            with pe.Fori(0, LAST) as i:
                scores(i, 1)
                pe.wait_ge(h3_ok, 2 * i + 1)
                attend(i, 0)
                pe.wait_ge(pt_out, TILES * i + 2)
                embed(i + 1)
                embedded[0] = 2 * i + 4
                attend(i, 1)
                A2(i + 1)
                A4(i, False)
            scores(LAST, 1)
            pe.wait_ge(h3_ok, 2 * LAST + 1)
            attend(LAST, 0)
            embedded[0] = 2 * SLOTS
            pe.wait_ge(pt_out, TILES * LAST + 2)
            attend(LAST, 1)
            A4(LAST, True)

            pe.wait_ge(h3_ok, 2 * SLOTS + 1)
            for n, w in enumerate((w1_s, w3_s)):
                for e in range(NX):
                    for c in range(C):
                        m = pe.matmul(PS[:, n, e * NX:(e + 1) * NX], w[:, e, c, :], xT2[:, c, 0:NX],
                                      start=(c == 0), stop=(c == C - 1))
                m.then_inc(tab_mm, 1)
            for n in range(2):
                pe.wait_ge(tabT_ok, n + 1)
                pe.transpose(PS[0:64, 2 + n, 0:P], AC[n][:, :], ident_s[:, :]).then_inc(tab_t, 1)
            pe.wait_ge(cnt_ok, 1)
            pe.matmul(PS[:, 4, 0:NX], ones[:, :], cnt[:, :], start=True, stop=True).then_inc(cnt_mm, 1)
            pe.wait_ge(tab_ok, 2)

            def quad_in(q, b):
                count = in_reg(pe, 4 * q + 4)
                pe.wait_ge(setup_v, SETUP_V)
                pe.wait_ge(ow_ok, count)
                for n in range(4):
                    m = pe.transpose(PS[0:64, b, n * P:(n + 1) * P], ow[:, b, n, :], ident_s[:, :])
                m.then_inc(owT_mm, 1)
                pe.wait_ge(owT_ok, q + 1)
                for n in range(4):
                    m = pe.matmul(PS[:, 2 + b, n * P:(n + 1) * P], owT[:, b, n * P:(n + 1) * P], tabA[:, :],
                                  start=True, stop=True)
                m.then_inc(z_mm, 1)

            def quad_out(q, b):
                pe.wait_ge(sz_ok, q + 1)
                for n in range(4):
                    m = pe.matmul(PS[0:64, 4 + b, 0:HID], ow[:, b, n, :], sz[:, b, n * P:(n + 1) * P],
                                  start=(n == 0), stop=(n == 3))
                m.then_inc(acc_mm, 1)

            with pe.Fori(0, QUADS // 2) as i:
                pe.wait_ge(racc_ok, 2 * i + 1)
                for b in range(2):
                    quad_in(2 * i + b, b)
                for b in range(2):
                    quad_out(2 * i + b, b)
            pe.wait_ge(gm_ok, 1)
            pe.transpose(PS[:, 6, 0:64], gm[:, :], ident_s[0:64, 0:64]).then_inc(gT_mm, 1)
            pe.wait_ge(gT_ok, 1)
            for e in range(NX):
                m = pe.matmul(PS[0:NX, 7, 0:E], gT[:, e * NX:(e + 1) * NX], w2_s[:, e, :],
                              start=(e == 0), stop=(e == NX - 1))
            m.then_inc(r8_mm, 1)
            pe.wait_ge(r8_ok, 1)

            def B1_qk(g):
                if not first(g):
                    pe.wait_ge(Y_out, 2 * (TILES * g - 2))
                transpose_in(g, xn1, 4, xn3_ok, x3T_mm)
                pe.wait_ge(x3T_a, g + 1)
                pe.wait_ge(x3T_v, g + 1)
                if not first(g):
                    pe.wait_ge(h4_ok, 2 * g - 1)
                for c in range(C):
                    proj_T(6 + c, wat_s, c * P, xT1, Bq_mm)
                for c in range(C):
                    proj_T(4 + c, wat_s, E + c * P, xT1, Bk_mm)

            def B1_v(g):
                pe.wait_ge(Bk_out, 2 * g + 2)
                for t in range(TILES):
                    for c in range(C):
                        m = pe.matmul(PS[:, (5, 0)[t // 2], (t % 2) * E:(t % 2 + 1) * E],
                                      xT1[:, c, t * P:(t + 1) * P], wat_s[:, c, 2 * E:3 * E],
                                      start=(c == 0), stop=(c == C - 1))
                    m.then_inc(Bv_mm, 1)

            def B2_scores(g, pair):
                if pair == 0:
                    pe.wait_ge(Bq_out, 4 * g + 4)
                    pe.wait_ge(Bk_out, 2 * g + 2)
                    pe.wait_ge(Bv_out, 8 * g + 8)
                else:
                    pe.wait_ge(f2_ok, TILES * g + 2)
                for t in (2 * pair, 2 * pair + 1):
                    hb = (t % 2) * 256
                    for i in range(4):
                        pe.matmul(PS[:, i, hb:hb + 256], identb[:, :], cmaskb[:, :, :], start=True, stop=False,
                                  skip_group_check=True)
                    image_scores(t, kT, qM, hb).then_inc(Bs_mm, 1)

            def B2_values(g, pair, banks):
                for t in (2 * pair, 2 * pair + 1):
                    pe.wait_ge(f2_ok, TILES * g + t + 1)
                    for hp in range(HP):
                        m = pe.matmul(PS[:, banks[t % 2], hp * L:(hp + 1) * L], F[:, t % 2, hp * P:(hp + 1) * P],
                                      V2[:, t, 2 * hp:2 * hp + 2, :, :], start=True, stop=True)
                    m.then_inc(Y_mm, 1)

            def B2_turn(g, pair, bank):
                for t in (2 * pair, 2 * pair + 1):
                    pe.wait_ge(Y_out, 2 * (TILES * g + t + 1))
                    for b in range(2):
                        m = pe.transpose(PS[:, bank, (t % 2) * E + b * P:(t % 2) * E + (b + 1) * P],
                                         xn2[:, t, b * P:(b + 1) * P], ident_s[:, :])
                m.then_inc(yT_mm, 1)

            def B2_proj(g, pair, bank):
                pe.wait_ge(yT_out, 2 * g + pair + 1)
                for t in (2 * pair, 2 * pair + 1):
                    for e in range(2):
                        m = pe.matmul(PS[:, bank, (t % 2) * E:(t % 2 + 1) * E], xT2[:, e, t * P:(t + 1) * P],
                                      wpr_s[:, e, :], start=(e == 0), stop=(e == 1))
                m.then_inc(pr_mm, 1)

            UP_BANKS = (5, 6, 7, 4, 5, 6, 7, 4)

            def B3(g):
                transpose_in(g, xn2, (7, 4), xn4_ok, x4T_mm)
                pe.wait_ge(x4T_a, g + 1)
                pe.wait_ge(x4T_v, g + 1)
                for f in range(NF):
                    if f >= 4:
                        pe.wait_ge(g_ok, NF * g + f - 3)
                    proj_T(UP_BANKS[f], wup_s, f * P, xT2, up_mm)
                pe.wait_ge(g_ok, NF * g + NF)
                for t in range(TILES):
                    for f in range(NF):
                        m = pe.matmul(PS[:, 5 + t // 2, (t % 2) * E:(t % 2 + 1) * E], G[:, f, t * P:(t + 1) * P],
                                      wdn_s[:, f, :], start=(f == 0), stop=(f == NF - 1))
                    m.then_inc(dn_mm, 1)
                pe.wait_ge(sqa_ok, NF * g + NF)
                for t in range(TILES):
                    m = pe.matmul(PS[:, 7, t:t + 1], sqa[:, t, :], ones[:, 0:1], start=True, stop=True)
                m.then_inc(ss_mm, 1)

            def B2_first(g):
                B2_scores(g, 1)
                pe.wait_ge(h5_ok, TILES * g + 1)
                B2_values(g, 0, (4, 5))
                B2_turn(g, 0, 6)
                B2_proj(g, 0, 7)

            B1_qk(0)
            B1_v(0)
            B2_scores(0, 0)
            with pe.Fori(0, LAST) as i:
                B2_first(i)
                B1_qk(i + 1)
                pe.wait_ge(Bq_out, 4 * i + 8)
                B2_values(i, 1, (6, 7))
                pe.wait_ge(Bk_out, 2 * i + 3)
                B2_turn(i, 1, 4)
                B1_v(i + 1)
                B2_proj(i, 1, 6)
                B2_scores(i + 1, 0)
                B3(i)
            B2_first(LAST)
            pe.wait_ge(h4_ok, 2 * LAST + 1)
            B2_values(LAST, 1, (6, 7))
            B2_turn(LAST, 1, 4)
            B2_proj(LAST, 1, 6)
            B3(LAST)

        @block.scalar
        def _(act):
            def a_A2(g):
                act.wait_ge(xT1_mm, 2 * g + 1)
                act.activation(xT1[:, 0, 0:TOK], PS[:, 4, :], ACT.Copy).then_inc(xT1_a, 1)
                act.activation(xT1[:, 0, TOK:TOK + L], PS[:, 4, 0:L], ACT.Copy).then_inc(xT1_a, 1)
                for c in range(C):
                    act.wait_ge(q_mm, 2 * g + c + 1)
                    act.activation(qT[:, c, :], PS[:, 6 + c, :], ACT.Identity, bias=bqk_s[:, c:c + 1])\
                       .then_inc(q_out, 1)
                act.wait_ge(h1_mm, g + 1)
                act.activation(h1T[:, :], PS[0:64, 4, :], ACT.Relu, bias=rb1_s[:, :]).then_inc(h1_out, 1)
                act.wait_ge(rl_mm, g + 1)
                act.activation(t1[:, :], PS[:, 5, 0:L], ACT.Tanh, bias=rb2h[:, :], scale=0.5).then_inc(rt1, 1)
                act.wait_ge(rsg1, g + 1)
                act.activation(t2[:, :], sg1[:, :], ACT.Tanh, scale=0.5).then_inc(rt2, 1)

            def exps(g, pair):
                for t in (2 * pair, 2 * pair + 1):
                    act.wait_ge(p_sub, TILES * g + t + 1)
                    act.activation(Pm[:, t % 2, :], Pm[:, t % 2, :], ACT.Exp, scale=HD ** -0.5)\
                       .then_inc(p_exp, 1)

            def turns(g, pair):
                for t in (2 * pair, 2 * pair + 1):
                    act.wait_ge(pt_mm, TILES * g + t + 1)
                    act.activation(PT[:, t % 2, :, :], PF[:, 4 * 512:6 * 512], ACT.Copy).then_inc(pt_out, 1)

            def a_A4(g):
                act.wait_ge(xT2_mm, 2 * g + 1)
                act.activation(xT2[:, 0, :], PS[:, 6, :], ACT.Copy).then_inc(xT2_a, 1)
                for c in range(C):
                    act.wait_ge(a_mm, 2 * g + c + 1)
                    act.activation(th[:, c * TOK:(c + 1) * TOK], PS[:, (5, 7)[c], :], ACT.Tanh, scale=0.5)\
                       .then_inc(th_ok, 1)

            act.wait_ge(loaded, N_LOADED)
            act.wait_ge(setup_v, SETUP_V)
            act.activation(Pm[:, :, :], wup_s[:, :, :], ACT.Abs, accum_out=sabs[:, 0:1]).then_inc(abs_ok, 1)
            act.activation(PT[:, :, :, :], wdn_s[:, :, :], ACT.Abs, accum_out=sabs[:, 1:2]).then_inc(abs_ok, 1)
            a_A2(0)
            exps(0, 0)
            with act.Fori(0, LAST) as i:
                turns(i, 0)
                exps(i, 1)
                turns(i, 1)
                a_A2(i + 1)
                a_A4(i)
                exps(i + 1, 0)
            turns(LAST, 0)
            exps(LAST, 1)
            turns(LAST, 1)
            a_A4(LAST)

            for n in range(2):
                act.wait_ge(tab_mm, n + 1)
                act.activation(AC[n][:, :], PS[:, n, 0:64], ACT.Copy).then_inc(tabT_ok, 1)
            for n in range(2):
                act.wait_ge(tab_t, n + 1)
                act.activation((tabA, tabC)[n][:, :], PS[0:64, 2 + n, 0:P], ACT.Copy).then_inc(tab_ok, 1)
            act.wait_ge(gl_ok, 1)
            act.activation(rs["ex"][:, :], rs["a"][:, :], ACT.Exp).then_inc(gex_ok, 1)
            with act.Fori(0, QUADS // 2) as i:
                for b in range(2):
                    act.wait_ge(owT_mm, 2 * i + b + 1)
                    act.activation(owT[:, b, :], PS[0:64, b, :], ACT.Copy).then_inc(owT_ok, 1)
                    act.wait_ge(z_mm, 2 * i + b + 1)
                    act.activation(tz[:, b, :], PS[:, 2 + b, :], ACT.Tanh, scale=0.5).then_inc(tz_ok, 1)
            act.wait_ge(gT_mm, 1)
            act.activation(gT[:, :], PS[:, 6, 0:64], ACT.Copy).then_inc(gT_ok, 1)

            def a_B1_k(g):
                act.wait_ge(x3T_mm, 2 * g + 1)
                act.activation(xT1[:, 0, 0:TOK], PS[:, 4, :], ACT.Copy).then_inc(x3T_a, 1)
                for c in range(C):
                    act.wait_ge(Bk_mm, 2 * g + c + 1)
                    act.activation(kT[:, c, :], PS[:, 4 + c, :], ACT.Copy).then_inc(Bk_out, 1)

            def a_B1_v(g):
                for t in range(TILES):
                    if t % 2 == 0:
                        act.wait_ge(Bv_mm, TILES * g + t + 2)
                    for b in range(2):
                        r = slice(b * L, (b + 1) * L)
                        act.activation(V2[r, t, :, b, :], PS[r, (5, 0)[t // 2], (t % 2) * E:(t % 2 + 1) * E]
                                       .rearrange("p (h d) -> p h d", d=HD), ACT.Copy).then_inc(Bv_out, 1)

            def parts(g, t):
                hb = (t % 2) * 256
                act.wait_ge(Bs_mm, TILES * g + 2 * (t // 2) + 2)
                sc = PS[:, 0:4, hb:hb + 256]
                act.activation(relu_s[t % 2][:, :], sc, ACT.Relu).then_inc(relu_ok, 1)
                act.activation(lin[t % 2][:, :], sc, ACT.Relu, scale=-0.01).then_inc(lin_ok, 1)

            def outs(g, pair, banks):
                for t in (2 * pair, 2 * pair + 1):
                    act.wait_ge(Y_mm, TILES * g + t + 1)
                    y = PS[:, banks[t % 2], :].rearrange("p (hp e b d) -> p hp e b d", hp=HP, e=2, b=2)
                    for e in range(2):
                        r = slice(e * L, (e + 1) * L)
                        act.activation(xn2[r, t, :].rearrange("p (b hp d) -> p b hp d", b=2, hp=HP),
                                       y[r, :, e, :, :].rearrange("p hp b d -> p b hp d"), ACT.Copy, scale=1e-3)\
                           .then_inc(Y_out, 1)

            def a_B3(g, ahead):
                act.wait_ge(x4T_mm, 2 * g + 1)
                act.activation(xT2[:, 0, :], PS[:, 7, :], ACT.Copy).then_inc(x4T_a, 1)
                for f in range(NF):
                    if f == 0 or f == 2:
                        ahead(f // 2)
                    act.wait_ge(up_mm, NF * g + f + 1)
                    act.activation(G[:, f, :], PS[:, (5, 6, 7, 4)[f % 4], :], ACT.Gelu).then_inc(g_ok, 1)

            act.wait_ge(V2_zero, 1)
            a_B1_k(0)
            a_B1_v(0)
            parts(0, 0)
            parts(0, 1)
            with act.Fori(0, LAST) as i:
                outs(i, 0, (4, 5))
                parts(i, 2)
                parts(i, 3)
                a_B1_k(i + 1)
                outs(i, 1, (6, 7))
                a_B1_v(i + 1)
                a_B3(i, lambda n: parts(i + 1, n))
            outs(LAST, 0, (4, 5))
            parts(LAST, 2)
            parts(LAST, 3)
            outs(LAST, 1, (6, 7))
            a_B3(LAST, lambda n: None)

        @block.gpsimd
        def _(pool):
            def p_rstd(var_ok, n, src, dst, done):
                pool.wait_ge(var_ok, n)
                pool.tensor_tensor(dst[:, :], src[:, :], mhalf[:, :], ALU.pow).then_inc(done, 1)

            def p_mask(g):
                pool.wait_ge(bias_ok, g + 1)
                if not first(g):
                    pool.wait_ge(s_mm, TILES * g)
                pool.tensor_tensor(mb[:, :, :], bias[:, :].unsqueeze(1).broadcast_to([P, NH, L]),
                                   delta_s[:, :].unsqueeze(2).broadcast_to([P, NH, L]), ALU.mult)\
                    .then_inc(mb_ok, 1)

            pool.wait_ge(loaded, N_LOADED)
            pool.wait_ge(setup_v, SETUP_V)
            p_rstd(ve1_ok, 1, ve, rstd, rstd1_ok)
            p_mask(0)
            with pool.Fori(0, LAST) as i:
                p_rstd(ve1_ok, i + 2, ve, rstd, rstd1_ok)
                p_rstd(ve2_ok, i + 1, ve2, rstd2, rstd2_ok)
                p_mask(i + 1)
            p_rstd(ve2_ok, SLOTS, ve2, rstd2, rstd2_ok)

            def quads(g, t):
                pool.wait_ge(relu_ok, TILES * g + t + 1)
                v = relu_s[t % 2][:, :]
                pool.tensor_tensor(v, v, v, ALU.mult).then_inc(quad_ok, 1)

            def p_ln4(g):
                pool.wait_ge(ve4_ok, 2 * g + 2)
                pool.tensor_tensor(rstd2[:, :], ve2[:, :], mhalf[:, :], ALU.pow).then_inc(rstd4_ok, 1)
                pool.tensor_tensor(rq[:, :], vr[:, :], phalf[:, :], ALU.pow).then_inc(rstd4_ok, 1)

            def p_B3(g, ahead):
                for f in range(NF):
                    if f == 0 or f == 2:
                        ahead(f // 2)
                    pool.wait_ge(g_ok, NF * g + f + 1)
                    gf = G[:, f, :].rearrange("p (t n) -> p t n", n=P)
                    if f == 0:
                        pool.tensor_tensor(sqa, gf, gf, ALU.mult).then_inc(sqa_ok, 1)
                        continue
                    pool.tensor_tensor(sqt[f % 2], gf, gf, ALU.mult).then_inc(sq_ok, 1)
                    pool.wait_ge(sq_ok, (NF - 1) * g + f)
                    pool.wait_ge(sqa_ok, NF * g + f)
                    pool.tensor_tensor(sqa, sqa, sqt[f % 2], ALU.add).then_inc(sqa_ok, 1)
                pool.wait_ge(msq_ok, g + 1)
                pool.tensor_tensor(rg[:, :], msq[:, :], phalf[:, :], ALU.pow).then_inc(rg_ok, 1)

            p_rstd(ve3_ok, 1, ve, rstd, rstd3_ok)
            quads(0, 0)
            quads(0, 1)
            with pool.Fori(0, LAST) as i:
                p_rstd(ve3_ok, i + 2, ve, rstd, rstd3_ok)
                quads(i, 2)
                quads(i, 3)
                p_ln4(i)
                p_B3(i, lambda n: quads(i + 1, n))
            quads(LAST, 2)
            quads(LAST, 3)
            p_ln4(LAST)
            p_B3(LAST, lambda n: None)

        @block.vector
        def _(dve):
            dve.memset(rW2_s[:, :, :], 0.0).then_inc(rw2_zero, 1)
            n_setup = 0
            for buf, v in ((ones, 1.0), (mhalf, -0.5), (phalf, 0.5), (vbuf, 0.0)):
                dve.memset(buf[:], v).then_inc(setup_v, 1)
                n_setup += 1
            dve.wait_ge(setup_v, n_setup)
            for e in range(2):
                r = slice(e * L, (e + 1) * L)
                dve.memset(Vb[r, :, :, :, e, HD:VW], 1.0).then_inc(setup_v, 1)
                n_setup += 1
            dve.wait_ge(loaded, N_LOADED)
            for dst, src in ((identb[:, :], ident_s[:, :]), (selb[:, :, :], self_[:, :, :]),
                             (cmaskb[:, :, :], cmask_s[:, :, :])):
                dve.tensor_copy(dst, src).then_inc(setup_v, 1)
                n_setup += 1
            dve.tensor_scalar(rb2h[:, :], rb2_s[:, :], 0.5, None, ALU.mult).then_inc(setup_v, 1)
            n_setup += 1
            assert n_setup == SETUP_V
            dve.wait_ge(abs_mm, 1)
            dve.tensor_scalar(thr[:, :], PS[:, 0, 0:2], 0.5 / (E * FF), None, ALU.mult).then_inc(th_set, 1)
            dve.tensor_scalar(nthr[:, :], PS[:, 0, 0:2], -0.5 / (E * FF), None, ALU.mult).then_inc(th_set, 1)
            dve.wait_ge(th_set, 2)
            for n, (w, tmp) in enumerate(((wup_s[:, :, :].rearrange("p c n -> p (c n)"),
                                           Pm[:, :, :].rearrange("p c n -> p (c n)")),
                                          (wdn_s[:, :, :].rearrange("p c n -> p (c n)"),
                                           PT[:, :, :, :].rearrange("p a b n -> p (a b n)")))):
                dve.tensor_scalar(tmp, w, nthr[:, n:n + 1], None, ALU.is_lt).then_inc(th_neg, 1)
                dve.wait_ge(th_neg, n + 1)
                dve.scalar_tensor_tensor(out=w, in0=w, scalar=thr[:, n:n + 1], in1=tmp, op0=ALU.is_gt,
                                         op1=ALU.subtract).then_inc(thr_ok, 1)
            dve.memset(msq[:, :], 0.0).then_inc(h3_ok, 1)
            dve.memset(rg[:, :], 0.0).then_inc(h5_ok, 1)

            def stats(g, st_, mv_, ve_, in_st, in_mv, in_ve):
                for t in range(TILES):
                    dve.bn_stats(st_[:, t, :], H[:, TILES * g + t, :]).then_inc(in_st, 1)
                for t in range(TILES):
                    count = in_reg(dve, TILES * g + t + 1)
                    dve.wait_ge(setup_v, SETUP_V)
                    dve.wait_ge(in_st, count)
                    dve.bn_aggr(mv_[:, t, :], st_[:, t, :]).then_inc(in_mv, 1)
                dve.wait_ge(in_mv, TILES * g + TILES)
                dve.tensor_scalar(ve_[:, :], mv_[:, :, 1], EPS, None, ALU.add).then_inc(in_ve, 1)

            def normalize(g, xn, mv_, scale, done):
                for t in range(TILES):
                    dve.tensor_scalar(xn[:, t, :], H[:, TILES * g + t, :], mv_[:, t, 0:1], scale[:, t:t + 1],
                                      ALU.subtract, ALU.mult).then_inc(done, 1)

            def embed_h(g):
                for p in range(2):
                    dve.wait_ge(embed_mm, TILES * g + 2 * p + 2)
                    at = TILES * g + 2 * p
                    dve.tensor_tensor(H[:, bass.ds(at, 2), :], PS[:, 4 + p, :].rearrange("p (t n) -> p t n", t=2),
                                      tokb_s[:, :].unsqueeze(1).broadcast_to([P, 2, E]), ALU.add)\
                       .then_inc(embed_out, 1)
                count = in_reg(dve, 2 * g + 2)
                dve.wait_ge(setup_v, SETUP_V)
                dve.wait_ge(embed_out, count)
                stats(g, st, mv, ve, ve1_st, ve1_mv, ve1_ok)

            def norm1(g):
                dve.wait_ge(rstd1_ok, g + 1)
                normalize(g, xn1, mv, rstd, xn1_ok)

            def v_A2_first(g):
                dve.wait_ge(xT1_mm, 2 * g + 2)
                dve.tensor_copy(xT1[:, 1, 0:TOK], PS[:, 5, :]).then_inc(xT1_v, 1)
                dve.tensor_copy(xT1[:, 1, TOK:TOK + L], PS[:, 5, 0:L]).then_inc(xT1_v, 1)

            def keys_in(g):
                for c in range(C):
                    dve.wait_ge(k_mm, 2 * g + c + 1)
                    for e in range(2):
                        dve.tensor_scalar(kM[:, c, e, :], PS[:, c, :], bqk_s[:, 2 + c:3 + c],
                                          par_s[:, e:e + 1], ALU.add, ALU.mult).then_inc(k_out, 1)

            def router_sigmoid(g):
                dve.wait_ge(rt1, g + 1)
                dve.tensor_scalar(sg1[:, :], t1[:, :], 0.5, 0.5, ALU.mult, ALU.add).then_inc(rsg1, 1)

            def values_to_blocks(g):
                bv3 = bv_s[:, :].rearrange("p (hp e d) -> p hp e d", e=2, d=HD)
                vp = PF[:, 0:8 * E].rearrange("p (n hp e d) -> p n hp e d", n=8, e=2, d=HD)

                def values_in(r, tiles, b, e, n0, n1):
                    n = n1 - n0
                    dve.tensor_tensor(Vb[r, tiles, :, b, e, 0:HD], vp[r, n0:n1, :, e, :],
                                      bv3[r, :, e, :].unsqueeze(1).broadcast_to([L, n, HP, HD]), ALU.add)\
                       .then_inc(v_out, 1)

                lo, hi = slice(0, L), slice(L, P)
                dve.wait_ge(v_mm, 8 * g + 4)
                values_in(lo, slice(0, 4), 0, 0, 4, 8)
                values_in(hi, slice(0, 4), 1, 1, 4, 8)
                dve.wait_ge(v_mm, 8 * g + 8)
                values_in(lo, slice(0, 4), 1, 0, 0, 4)
                values_in(hi, slice(1, 4), 0, 1, 0, 3)
                values_in(hi, slice(0, 1), 0, 1, 3, 4)

            def top_keys(g):
                dve.wait_ge(rt2, g + 1)
                dve.tensor_scalar(wk[0][:, :], t2[:, :], 0.5, 0.5, ALU.mult, ALU.add).then_inc(top_step, 1)
                for r in range(KEEP // 8):
                    count = in_reg(dve, TOP * g + 2 * r + 1)
                    dve.wait_ge(setup_v, SETUP_V)
                    dve.wait_ge(top_step, count)
                    dve.max(m8[r][:, :], wk[r % 3][:, :]).then_inc(top_step, 1)
                    count = in_reg(dve, TOP * g + 2 * r + 2)
                    dve.wait_ge(setup_v, SETUP_V)
                    dve.wait_ge(top_step, count)
                    dve.match_replace(wk[(r + 1) % 3][:, :], m8[r][:, :], wk[r % 3][:, :], TAKEN)\
                       .then_inc(top_step, 1)
                left = wk[(KEEP // 8) % 3]
                count = in_reg(dve, TOP * g + TOP - 3)
                dve.wait_ge(setup_v, SETUP_V)
                dve.wait_ge(top_step, count)
                dve.max(m8[3][:, :], left[:, :]).then_inc(top_step, 1)
                dve.wait_ge(top_step, TOP * g + TOP - 2)
                dve.scalar_tensor_tensor(out=cand[:, :], in0=left[:, :], scalar=m8[3][:, 0:1], in1=rev64_s[:, :],
                                         op0=ALU.is_equal, op1=ALU.mult).then_inc(top_step, 1)
                count = in_reg(dve, TOP * g + TOP - 1)
                dve.wait_ge(setup_v, SETUP_V)
                dve.wait_ge(top_step, count)
                dve.max(m8[4][:, :], cand[:, :]).then_inc(top_step, 1)
                dve.wait_ge(top_step, TOP * g + TOP)
                dve.tensor_scalar(selk[:, :], cand[:, :], m8[4][:, 0:1], None, ALU.is_equal)\
                   .then_inc(selk_ok, 1)
                dve.wait_ge(selk_ok, g + 1)
                dve.scalar_tensor_tensor(out=keep[:, :], in0=left[:, :], scalar=TAKEN, in1=selk[:, :],
                                         op0=ALU.is_equal, op1=ALU.add).then_inc(keep_ok, 1)
                dve.wait_ge(keep_ok, g + 1)
                if not first(g):
                    dve.wait_ge(mb_ok, g)
                dve.tensor_scalar(bias[:, :], keep[:, :], -1.0, -NEG, ALU.add, ALU.mult)\
                   .then_inc(bias_ok, 1)

            def soft(g, t):
                hb = (t % 2) * 256
                dve.wait_ge(s_mm, TILES * g + 2 * (t // 2) + 2)
                dve.tensor_reduce(mx[:, t % 2, :].rearrange("p (i h) -> p i h", i=4),
                                  PS[:, 0:4, hb:hb + 256].rearrange("p i (h k) -> p i h k", k=L), AX.X, ALU.max)\
                   .then_inc(smax, 1)
                dve.wait_ge(smax, TILES * g + t + 1)
                if not (first(g) and t < 2):
                    dve.wait_ge(pt_mm, TILES * g + t - 1)
                dve.tensor_tensor(Pm[:, t % 2, :].rearrange("p (i h k) -> p i h k", i=4, k=L),
                                  PS[:, 0:4, hb:hb + 256].rearrange("p i (h k) -> p i h k", k=L),
                                  mx[:, t % 2, :].rearrange("p (i h) -> p i h", i=4).unsqueeze(3)
                                  .broadcast_to([P, 4, 4, L]), ALU.subtract).then_inc(p_sub, 1)

            def attend(g, t):
                dve.wait_ge(pv_mm, TILES * g + t + 1)
                o = PF[:, PV0:PV0 + HP * 4 * VW].rearrange("p (hp b e v) -> p hp b e v", hp=HP, b=2, e=2)
                for b in range(2):
                    r = slice(b * L, (b + 1) * L)
                    dve.reciprocal(rden[r, :].rearrange("p (hp e) -> p hp e", e=2), o[r, :, b, :, HD])\
                       .then_inc(rden_ok, 1)
                for b in range(2):
                    r = slice(b * L, (b + 1) * L)
                    dve.wait_ge(rden_ok, 2 * (TILES * g + t) + b + 1)
                    dve.tensor_tensor(yn[r, :].rearrange("p (hp e d) -> p hp e d", hp=HP, e=2),
                                      o[r, :, b, :, 0:HD],
                                      rden[r, :].rearrange("p (hp e) -> p hp e", e=2).unsqueeze(3)
                                      .broadcast_to([L, HP, 2, HD]), ALU.mult).then_inc(y_out, 1)
                dve.wait_ge(y_out, 2 * (TILES * g + t + 1))
                dve.tensor_tensor(H[:, TILES * g + t, :], H[:, TILES * g + t, :], yn[:, :], ALU.add)\
                   .then_inc(h2_ok, 1)

            def stats2(g):
                count = in_reg(dve, TILES * g + TILES)
                dve.wait_ge(setup_v, SETUP_V)
                dve.wait_ge(h2_ok, count)
                stats(g, st2, mv2, ve2, ve2_st, ve2_mv, ve2_ok)

            def norm2(g):
                dve.wait_ge(rstd2_ok, g + 1)
                normalize(g, xn2, mv2, rstd2, xn2_ok)

            def v_A4(g):
                dve.wait_ge(xT2_mm, 2 * g + 2)
                dve.tensor_copy(xT2[:, 1, :], PS[:, 7, :]).then_inc(xT2_v, 1)
                dve.wait_ge(gate_mm, g + 1)
                dve.tensor_copy(lg[:, bass.ds(TILES * g, TILES), :], PS[:, 4, 0:TILES * NX]
                                .rearrange("p (t e) -> p t e", e=NX)).then_inc(lg_ok, 1)
                for c in range(C):
                    cols = slice(c * TOK, (c + 1) * TOK)
                    dve.wait_ge(th_ok, 2 * g + c + 1)
                    dve.scalar_tensor_tensor(out=u[:, cols], in0=th[:, cols], scalar=1.0, in1=PS[:, (5, 7)[c], :],
                                             op0=ALU.add, op1=ALU.mult).then_inc(u_ok, 1)
                    dve.wait_ge(u_ok, 2 * g + c + 1)
                    dve.wait_ge(b_mm, 2 * g + c + 1)
                    dve.tensor_tensor(hs[:, cols], u[:, cols], PS[:, (6, 4)[c], :], ALU.mult)\
                       .then_inc(hs_ok, 1)

            def v_shared(g):
                for p in range(2):
                    dve.wait_ge(sh_mm, TILES * g + 2 * p + 2)
                    rows2 = H[:, bass.ds(TILES * g + 2 * p, 2), :]
                    dve.scalar_tensor_tensor(out=rows2, in0=PS[:, 5 + p, :].rearrange("p (t n) -> p t n", t=2),
                                             scalar=0.5, in1=rows2, op0=ALU.mult, op1=ALU.add)\
                       .then_inc(h3_ok, 1)

            def slot_in(g, between):
                v_A2_first(g)
                between()
                keys_in(g)
                router_sigmoid(g)
                top_keys(g)
                values_to_blocks(g)

            embed_h(0)
            norm1(0)
            slot_in(0, lambda: None)
            soft(0, 0)
            soft(0, 1)
            with dve.Fori(0, LAST) as i:
                attend(i, 0)
                soft(i, 2)
                attend(i, 1)
                soft(i, 3)
                embed_h(i + 1)
                norm1(i + 1)
                attend(i, 2)
                attend(i, 3)
                stats2(i)
                slot_in(i + 1, lambda: norm2(i))
                v_A4(i)
                soft(i + 1, 0)
                soft(i + 1, 1)
                v_shared(i)
            for t in range(2):
                attend(LAST, t)
                soft(LAST, 2 + t)
            attend(LAST, 2)
            attend(LAST, 3)
            stats2(LAST)
            norm2(LAST)
            v_A4(LAST)
            v_shared(LAST)
            dve.wait_ge(h3_ok, 2 * SLOTS + 1)

            lg2 = lg[:, :, :].rearrange("p t e -> p (t e)")

            def each(v):
                return v[:, :].unsqueeze(2).broadcast_to([P, NT, NX])

            def experts(v):
                return v[:, :].unsqueeze(1).broadcast_to([P, NT, NX])

            dve.tensor_reduce(rsm["mx"][:, :], lg[:, :, :], AX.X, ALU.max).then_inc(routed_step, 1)
            dve.wait_ge(routed_step, after("routed"))
            dve.tensor_tensor(r3["a"], lg[:, :, :], each(rsm["mx"]), ALU.subtract).then_inc(gl_ok, 1)
            dve.wait_ge(gex_ok, 1)
            dve.tensor_reduce(rsm["sum"][:, :], r3["ex"], AX.X, ALU.add).then_inc(routed_step, 1)
            dve.wait_ge(routed_step, after("routed"))
            dve.reciprocal(rsm["inv"][:, :], rsm["sum"][:, :]).then_inc(routed_step, 1)
            dve.wait_ge(routed_step, after("routed"))
            dve.tensor_tensor(r3["pr"], r3["ex"], each(rsm["inv"]), ALU.mult).then_inc(routed_step, 1)
            dve.wait_ge(routed_step, after("routed"))
            dve.tensor_tensor(r3["s"], r3["pr"], experts(eb_s), ALU.add).then_inc(routed_step, 1)
            dve.wait_ge(routed_step, after("routed"))
            s4 = rs["s"][:, :].rearrange("p (t g x) -> p t g x", g=4, x=2)
            dve.tensor_tensor(gs[:, :, :], s4[:, :, :, 0], s4[:, :, :, 1], ALU.add).then_inc(routed_step, 1)
            dve.wait_ge(routed_step, after("routed"))
            for a in range(4):
                dve.memset(wins[:, :, a], float(a)).then_inc(routed_step, 1)
                dve.wait_ge(routed_step, after("routed"))
            for a in range(4):
                for b in range(a + 1, 4):
                    dve.tensor_tensor(cmp[:, :], gs[:, :, a], gs[:, :, b], ALU.is_ge).then_inc(routed_step, 1)
                    dve.wait_ge(routed_step, after("routed"))
                    dve.tensor_tensor(wins[:, :, a], wins[:, :, a], cmp[:, :], ALU.add).then_inc(routed_step, 1)
                    dve.wait_ge(routed_step, after("routed"))
                    dve.tensor_tensor(wins[:, :, b], wins[:, :, b], cmp[:, :], ALU.subtract).then_inc(routed_step, 1)
                    dve.wait_ge(routed_step, after("routed"))
            dve.tensor_scalar(gk[:, :, :], wins[:, :, :], 2.0, None, ALU.is_ge).then_inc(routed_step, 1)
            dve.wait_ge(routed_step, after("routed"))
            dve.tensor_scalar(gd[:, :, :], gk[:, :, :], -1.0, BIG, ALU.add, ALU.mult).then_inc(routed_step, 1)
            dve.wait_ge(routed_step, after("routed"))
            m4 = rs["m"][:, :].rearrange("p (t g x) -> p t g x", g=4, x=2)
            for xx in range(2):
                dve.tensor_tensor(m4[:, :, :, xx], s4[:, :, :, xx], gk[:, :, :], ALU.mult).then_inc(routed_step, 1)
                dve.wait_ge(routed_step, after("routed"))
                dve.tensor_tensor(m4[:, :, :, xx], m4[:, :, :, xx], gd[:, :, :], ALU.add).then_inc(routed_step, 1)
                dve.wait_ge(routed_step, after("routed"))
            for k, (src, oh, mxk, ck) in enumerate((("m", "oh1", "m1", "c1"), ("b", "oh2", "m2", "c2"))):
                dve.tensor_reduce(rsm[mxk][:, :], r3[src], AX.X, ALU.max).then_inc(routed_step, 1)
                dve.wait_ge(routed_step, after("routed"))
                dve.tensor_tensor(r3["a"], r3[src], each(rsm[mxk]), ALU.is_equal).then_inc(routed_step, 1)
                dve.wait_ge(routed_step, after("routed"))
                dve.tensor_tensor(r3["a"], r3["a"], experts(rev8_s), ALU.mult).then_inc(routed_step, 1)
                dve.wait_ge(routed_step, after("routed"))
                dve.tensor_reduce(rsm[ck][:, :], r3["a"], AX.X, ALU.max).then_inc(routed_step, 1)
                dve.wait_ge(routed_step, after("routed"))
                dve.tensor_tensor(r3[oh], r3["a"], each(rsm[ck]), ALU.is_equal).then_inc(routed_step, 1)
                dve.wait_ge(routed_step, after("routed"))
                if k == 0:
                    dve.scalar_tensor_tensor(out=rs["b"][:, :], in0=rs[oh][:, :], scalar=-BIG,
                                             in1=rs["m"][:, :], op0=ALU.mult, op1=ALU.add).then_inc(routed_step, 1)
                    dve.wait_ge(routed_step, after("routed"))
                cols = slice(k * NT, (k + 1) * NT)
                dve.tensor_scalar(ei[:, cols], rsm[ck][:, :], -1.0, float(NX), ALU.mult, ALU.add)\
                   .then_inc(routed_step, 1)
                dve.wait_ge(routed_step, after("routed"))
                dve.tensor_tensor(r3["a"], r3[oh], r3["pr"], ALU.mult).then_inc(routed_step, 1)
                dve.wait_ge(routed_step, after("routed"))
                dve.tensor_reduce(wt[:, cols], r3["a"], AX.X, ALU.add).then_inc(routed_step, 1)
                dve.wait_ge(routed_step, after("routed"))
            dve.tensor_tensor(rs["a"][:, :], rs["oh1"][:, :], rs["oh2"][:, :], ALU.add).then_inc(routed_step, 1)
            dve.wait_ge(routed_step, after("routed"))
            dve.tensor_reduce(cnt[:, :], rs["a"][:, :].rearrange("p (t e) -> p e t", e=NX), AX.X, ALU.add)\
               .then_inc(cnt_ok, 1)
            dve.wait_ge(cnt_mm, 1)
            dve.tensor_copy(off[:, :], PS[:, 4, 0:NX]).then_inc(routed_step, 1)
            dve.wait_ge(routed_step, after("routed"))
            for e in range(1, NX):
                dve.tensor_tensor(off[:, e:e + 1], off[:, e:e + 1], off[:, e - 1:e], ALU.add).then_inc(routed_step, 1)
                dve.wait_ge(routed_step, after("routed"))
            dve.tensor_scalar(gg[:, :], ridx_s[:, :], off[:, 0:1], None, ALU.is_ge).then_inc(routed_step, 1)
            dve.wait_ge(routed_step, after("routed"))
            for e in range(1, NX - 1):
                dve.scalar_tensor_tensor(out=gg[:, :], in0=ridx_s[:, :], scalar=off[:, e:e + 1],
                                         in1=gg[:, :], op0=ALU.is_ge, op1=ALU.add).then_inc(routed_step, 1)
                dve.wait_ge(routed_step, after("routed"))
            dve.scalar_tensor_tensor(out=code[:, :], in0=gg[:, :], scalar=float(NX), in1=ei[:, :],
                                     op0=ALU.mult, op1=ALU.add).then_inc(routed_step, 1)
            dve.wait_ge(routed_step, after("routed"))
            dve.memset(racc[:, :], 0.0).then_inc(racc_ok, 1)

            def quad_ow(q, b):
                for n in range(4):
                    at = 4 * q + n
                    dve.tensor_scalar(ow[:, b, n, :], iota_s[:, :], code[:, bass.ds(at, 1)],
                                      wt[:, bass.ds(at, 1)], ALU.is_equal, ALU.mult).then_inc(ow_ok, 1)

            with dve.Fori(0, QUADS // 2) as i:
                for b in range(2):
                    quad_ow(2 * i + b, b)
                for b in range(2):
                    dve.wait_ge(tz_ok, 2 * i + b + 1)
                    dve.scalar_tensor_tensor(out=sz[:, b, :], in0=tz[:, b, :], scalar=1.0, in1=PS[:, 2 + b, :],
                                             op0=ALU.add, op1=ALU.mult).then_inc(sz_ok, 1)
                for b in range(2):
                    dve.wait_ge(acc_mm, 2 * i + b + 1)
                    dve.wait_ge(racc_ok, 2 * i + b + 1)
                    dve.tensor_tensor(racc[:, :], racc[:, :], PS[0:64, 4 + b, 0:HID], ALU.add)\
                       .then_inc(racc_ok, 1)
            dve.wait_ge(racc_ok, QUADS + 1)
            dve.wait_ge(tab_ok, 2)
            dve.scalar_tensor_tensor(out=gm[:, :], in0=racc[:, :], scalar=0.5, in1=tabC[:, :], op0=ALU.mult,
                                     op1=ALU.mult).then_inc(gm_ok, 1)
            dve.wait_ge(r8_mm, 1)
            dve.tensor_tensor(H[0:NX, TILES * LAST, :], H[0:NX, TILES * LAST, :], PS[0:NX, 7, 0:E], ALU.add)\
               .then_inc(r8_ok, 1)
            dve.wait_ge(r8_ok, 1)

            def norm3(g):
                dve.wait_ge(rstd3_ok, g + 1)
                normalize(g, xn1, mv, rstd, xn3_ok)

            def v_B1(g):
                for c in range(C):
                    dve.wait_ge(Bq_mm, 2 * g + c + 1)
                    for e in range(2):
                        dve.tensor_scalar(qM[:, c, e, :], PS[:, 6 + c, :], par_s[:, 2 + e:3 + e], None, ALU.mult)\
                           .then_inc(Bq_out, 1)

            def v_x3T(g):
                dve.wait_ge(x3T_mm, 2 * g + 2)
                dve.tensor_copy(xT1[:, 1, 0:TOK], PS[:, 5, :]).then_inc(x3T_v, 1)

            def poly(g, t):
                hb = (t % 2) * 256
                dve.wait_ge(lin_ok, TILES * g + 2 * (t // 2) + 2)
                dve.wait_ge(quad_ok, TILES * g + t + 1)
                dve.scalar_tensor_tensor(out=lin[t % 2][:, :], in0=lin[t % 2][:, :], scalar=1.0,
                                         in1=relu_s[t % 2][:, :], op0=ALU.add,
                                         op1=ALU.add).then_inc(f0_ok, 1)
                dve.wait_ge(f0_ok, TILES * g + t + 1)
                if not (first(g) and t < 2):
                    dve.wait_ge(Y_mm, TILES * g + t - 1)
                Fv = F[:, t % 2, :].rearrange("p (i n) -> p i n", i=4)
                dve.scalar_tensor_tensor(out=Fv, in0=PS[:, 0:4, hb:hb + 256], scalar=-100.0,
                                         in1=lin[t % 2][:, :].rearrange("p (i n) -> p i n", i=4), op0=ALU.is_ge,
                                         op1=ALU.mult).then_inc(f2_ok, 1)

            def turned(g, pair, bank):
                dve.wait_ge(yT_mm, 2 * g + pair + 1)
                for t in (2 * pair, 2 * pair + 1):
                    m = dve.tensor_copy(xT2[:, :, t * P:(t + 1) * P].rearrange("p e (b q) -> p e b q", b=2),
                                        PS[:, bank, (t % 2) * E:(t % 2 + 1) * E]
                                        .rearrange("p (b e q) -> p e b q", b=2, e=2))
                m.then_inc(yT_out, 1)

            def projected(g, pair, bank):
                dve.wait_ge(pr_mm, 2 * g + pair + 1)
                rows2 = H[:, bass.ds(TILES * g + 2 * pair, 2), :]
                dve.tensor_tensor(rows2, rows2, PS[:, bank, :].rearrange("p (t n) -> p t n", t=2), ALU.add)\
                   .then_inc(h4_ok, 1)

            def stats4(g):
                count = in_reg(dve, 2 * g + 2)
                dve.wait_ge(setup_v, SETUP_V)
                dve.wait_ge(h4_ok, count)
                stats(g, st2, mv2, ve2, ve4_st, ve4_mv, ve4_ok)
                dve.tensor_copy(vr[:, :], mv2[:, :, 1]).then_inc(ve4_ok, 1)

            def norm4(g):
                dve.wait_ge(rstd4_ok, 2 * g + 2)
                dve.tensor_tensor(rr[:, :], rq[:, :], rstd2[:, :], ALU.mult).then_inc(r4_step, 1)
                dve.wait_ge(r4_step, 4 * g + 1)
                dve.tensor_scalar(rr[:, :], rr[:, :], 1e-8, None, ALU.add).then_inc(r4_step, 1)
                dve.wait_ge(r4_step, 4 * g + 2)
                dve.reciprocal(rr[:, :], rr[:, :]).then_inc(r4_step, 1)
                dve.wait_ge(r4_step, 4 * g + 3)
                dve.tensor_tensor(r4[:, :], rr[:, :], rstd2[:, :], ALU.mult).then_inc(r4_step, 1)
                dve.wait_ge(r4_step, 4 * g + 4)
                normalize(g, xn2, mv2, r4, xn4_ok)

            def v_x4T(g):
                dve.wait_ge(x4T_mm, 2 * g + 2)
                dve.tensor_copy(xT2[:, 1, :], PS[:, 4, :]).then_inc(x4T_v, 1)

            def v_B3(g):
                dve.wait_ge(ss_mm, g + 1)
                dve.tensor_scalar(msq[:, :], PS[:, 7, 0:TILES], 1.0 / FF, None, ALU.mult).then_inc(msq_ok, 1)
                dve.wait_ge(rg_ok, g + 1)
                dve.tensor_scalar(rge[:, :], rg[:, :], 1e-8, None, ALU.add).then_inc(rg_step, 1)
                dve.wait_ge(rg_step, 2 * g + 1)
                dve.reciprocal(rgi[:, :], rge[:, :]).then_inc(rg_step, 1)
                dve.wait_ge(rg_step, 2 * g + 2)
                for t in range(TILES):
                    dve.wait_ge(dn_mm, TILES * g + 2 * (t // 2) + 2)
                    at = TILES * g + t
                    dve.scalar_tensor_tensor(out=H[:, at, :], in0=PS[:, 5 + t // 2, (t % 2) * E:(t % 2 + 1) * E],
                                             scalar=rgi[:, t:t + 1], in1=H[:, at, :], op0=ALU.mult, op1=ALU.add)\
                       .then_inc(h5_ok, 1)

            def stats3(g):
                stats(g, st, mv, ve, ve3_st, ve3_mv, ve3_ok)

            dve.memset(vbuf[:], 0.0).then_inc(V2_zero, 1)
            stats3(0)
            norm3(0)
            v_x3T(0)
            v_B1(0)
            poly(0, 0)
            poly(0, 1)
            with dve.Fori(0, LAST) as i:
                stats3(i + 1)
                norm3(i + 1)
                turned(i, 0, 6)
                poly(i, 2)
                projected(i, 0, 7)
                poly(i, 3)
                v_x3T(i + 1)
                v_B1(i + 1)
                turned(i, 1, 4)
                projected(i, 1, 6)
                stats4(i)
                norm4(i)
                v_x4T(i)
                poly(i + 1, 0)
                poly(i + 1, 1)
                v_B3(i)
            turned(LAST, 0, 6)
            poly(LAST, 2)
            projected(LAST, 0, 7)
            poly(LAST, 3)
            turned(LAST, 1, 4)
            projected(LAST, 1, 6)
            stats4(LAST)
            norm4(LAST)
            v_x4T(LAST)
            v_B3(LAST)


def _layout(inputs):
    a = {k: np.asarray(v) for k, v in inputs.items()}

    def chunks(w):
        return w.reshape(-1, P, w.shape[1]).transpose(1, 0, 2)

    def rows(v):
        return np.broadcast_to(v[None, :], (P, v.shape[0]))

    x = a["x"].reshape(SLOTS, IMGS, 3, 8, 16, 8, 16).transpose(0, 2, 4, 6, 1, 3, 5).reshape(SLOTS, KP, P, TOK)
    x = np.roll(x, -1, axis=0).transpose(0, 2, 1, 3)
    order = np.concatenate([np.arange(HD) + HD * (4 * i + 2 * c + e)
                            for c in range(C) for i in range(4) for e in range(2)])
    qkv = a["L0_attn_qkv_w"].T
    qkv = np.concatenate([qkv[:, order], qkv[:, E + order], qkv[:, 2 * E:]], axis=1)
    qb = a["L0_attn_qkv_b"]
    bqk = np.stack([qb[order][:P], qb[order][P:], qb[E + order][:P], qb[E + order][P:]], axis=1)
    wat = a["L1_attn_W_attn"]
    wat = np.concatenate([wat[:, order], wat[:, E + order], wat[:, 2 * E:]], axis=1)
    wpr = a["L1_attn_W_proj"].reshape(HP, 2, HD, E).transpose(0, 2, 1, 3).reshape(P, 2, E)

    def hid(w):
        return w.reshape(NX, C, P, HID).transpose(2, 0, 1, 3)

    ident = np.eye(P)
    f = np.arange(P)
    even = ((f // HD) % 2 == 0).astype(np.float32)
    par = np.stack([even, 1 - even, HD ** -0.5 * even, HD ** -0.5 * (1 - even)], axis=1)
    sel = (f[:, None, None] // NH == 2 * np.arange(TILES)[None, :, None] + f[None, None, :] // L)
    delta = f[:, None] % NH == np.arange(NH)[None, :]
    rev64 = rows(np.arange(L, 0, -1))
    cm = np.where(f[:, None] % L > np.arange(L)[None, :], NEG, 0.0)
    cmask = np.broadcast_to(cm[:, None, :], (P, 4, L))
    slot = np.arange(SLOTS * TILES)
    tile0 = ((slot // TILES + 1) % SLOTS) * TILES + slot % TILES
    token = tile0[None, :] * P + f[:, None]
    ridx = np.concatenate([2 * token, 2 * token + 1], axis=1)
    maps = dict(
        x=x, tokW=chunks(a["L0_tok_W"]), tokb=rows(a["L0_tok_b"]), wqkv=chunks(qkv), bqk=bqk, bv=rows(qb[2 * E:]),
        rW1=chunks(a["L0_attn_r_w1"].T), rb1=a["L0_attn_r_b1"][:, None], rW2=a["L0_attn_r_w2"].T,
        rb2=np.tile(a["L0_attn_r_b2"], IMGS)[:, None], gateW=chunks(a["L0_ffn_w_gate"].T),
        eb=rows(a["L0_ffn_expert_bias"]), w1=hid(a["L0_ffn_w1"]), w3=hid(a["L0_ffn_w3"]),
        w2=a["L0_ffn_w2"].transpose(1, 0, 2), s1=chunks(a["L0_ffn_sw1"].T), s3=chunks(a["L0_ffn_sw3"].T),
        s2=chunks(a["L0_ffn_sw2"].T), wat=chunks(wat), wpr=wpr, wup=chunks(a["L1_ffn_w_up"].T),
        wdn=chunks(a["L1_ffn_w_down"].T), ident=ident, par=par, sel=sel, delta=delta, rev64=rev64, cmask=cmask,
        ridx=ridx, iota64=rows(np.arange(64)), rev8=rows(np.arange(NX, 0, -1)))
    consts = ("ident", "par", "sel", "delta", "rev64", "cmask", "ridx", "iota64", "rev8")
    return {k: np.ascontiguousarray(v.astype(np.float32) if k in consts else v) for k, v in maps.items()}


def kernel(**inputs):
    import concourse.bacc as _bacc
    from concourse.bass_utils import run_bass_kernel_spmd as _run

    nc = _bacc.Bacc("TRN2", target_bir_lowering=False, num_devices=1)
    arrays = _layout(inputs)
    args = {n: nc.dram_tensor("in_" + n, v.shape, F32, kind="ExternalInput").ap() for n, v in arrays.items()}
    out = nc.dram_tensor("out_0", (SLOTS, P, TILES, E), F32, kind="ExternalOutput").ap()
    build(nc, out=out, **args)
    r = _run(nc, [{"in_" + n: v for n, v in arrays.items()}], core_ids=[0])
    got = np.roll(np.asarray(r.results[0]["out_0"]), 1, axis=0)
    return np.ascontiguousarray(got.transpose(0, 2, 1, 3)).reshape(SLOTS * IMGS, L, E)
```

```python
from contextlib import ExitStack

import numpy as np

import concourse.bass as bass
from concourse import mybir

ALU = mybir.AluOpType
ACT = mybir.ActivationFunctionType
AX = mybir.AxisListType
F32 = mybir.dt.float32
BF16 = mybir.dt.bfloat16
F16 = mybir.dt.float16

P = 128
SLOTS = 8
IMGS = 8
L = 64
TILES = 4
TOK = IMGS * L
E = 256
C = E // P
NH = 16
HD = E // NH
HP = NH // 2
KEEP = int(L * 0.4)
KP = 6
NX = 8
HID = 128
FF = 1024
NF = FF // P
NEG = -1e30
EPS = 1e-5
VW = HD + 1
BIG = 3e38
PV0 = 7 * 512 - 4 * 4 * VW
SETUP_V = 9 + IMGS + 2
TOP = 2 * (KEEP // 8) + 4
TAKEN = -4.0


def build(nc, x, tokW, tokb, wqkv, bqk, bv, rW1, rb1, rW2, rb2, gateW, eb, w1, w3, w2, s1, s3, s2,
          wat, wpr, wup, wdn, ident, par, sel, delta, rev64, cmask, ridx, iota64, rev8, out):
    with ExitStack() as ctx:
        def sb(name, shape, dt=F32):
            return ctx.enter_context(nc.sbuf_tensor(name, shape, dt))

        def sem(name):
            return ctx.enter_context(nc.semaphore(name))

        PS = ctx.enter_context(nc.psum_tensor("PS", [P, 8, 512], F32))
        PF = PS[:, :, :].rearrange("p b n -> p (b n)")

        tokW_s = sb("tokW_s", [P, KP, E]); tokb_s = sb("tokb_s", [P, E])
        wqkv_s = sb("wqkv_s", [P, C, 3 * E]); bqk_s = sb("bqk_s", [P, 4]); bv_s = sb("bv_s", [P, E])
        rW1_s = sb("rW1_s", [P, C, 64]); rb1_s = sb("rb1_s", [64, 1])
        rW2_s = sb("rW2_s", [64, IMGS, P]); rW2c = sb("rW2c", [64, NH]); rb2_s = sb("rb2_s", [P, 1]); rb2h = sb("rb2h", [P, 1])
        gateW_s = sb("gateW_s", [P, C, NX]); eb_s = sb("eb_s", [P, NX])
        s1_s = sb("s1_s", [P, C, E]); s3_s = sb("s3_s", [P, C, E]); s2_s = sb("s2_s", [P, C, E])
        w1_s = sb("w1_s", [P, NX, C, HID]); w3_s = sb("w3_s", [P, NX, C, HID]); w2_s = sb("w2_s", [P, NX, E])
        wat_s = sb("wat_s", [P, C, 3 * E]); wpr_s = sb("wpr_s", [P, C, E])
        wup_s = sb("wup_s", [P, C, FF]); wdn_s = sb("wdn_s", [P, NF, E])
        ident_s = sb("ident_s", [P, P]); identb = sb("identb", [P, P], BF16)
        par_s = sb("par_s", [P, 4])
        self_ = sb("self_", [P, TILES, P]); selb = sb("selb", [P, TILES, P], BF16)
        delta_s = sb("delta_s", [P, NH]); rev64_s = sb("rev64_s", [P, L])
        cmask_s = sb("cmask_s", [P, 4, L]); cmaskb = sb("cmaskb", [P, 4, L], BF16)
        ridx_s = sb("ridx_s", [P, 64]); iota_s = sb("iota_s", [P, 64]); rev8_s = sb("rev8_s", [P, NX])
        ones = sb("ones", [P, P]); mhalf = sb("mhalf", [P, 4]); phalf = sb("phalf", [P, 4])

        H = sb("H", [P, SLOTS * TILES, E])
        work = sb("work", [P, NF, TOK])
        patch = work[:, 0:KP, :]
        st = sb("st", [P, TILES, 6]); mv = sb("mv", [P, TILES, 2])
        st2 = sb("st2", [P, TILES, 6]); mv2 = sb("mv2", [P, TILES, 2])
        ve = sb("ve", [P, TILES]); rstd = sb("rstd", [P, TILES])
        ve2 = sb("ve2", [P, TILES]); rstd2 = sb("rstd2", [P, TILES])
        xn1 = sb("xn1", [P, TILES, E]); xn2 = sb("xn2", [P, TILES, E])
        xT1 = sb("xT1", [P, C, TOK + L]); xT2 = sb("xT2", [P, C, TOK])
        qT = sb("qT", [P, C, TOK]); kM = sb("kM", [P, C, 2, TOK])
        vbuf = sb("vbuf", [P, TILES * HP * 2 * 2 * VW])
        Vb = vbuf[:, :].rearrange("p (t hp b e v) -> p t hp b e v", t=TILES, hp=HP, b=2, e=2)
        V2 = vbuf[:, 0:TILES * NH * 2 * HD].rearrange("p (t h b d) -> p t h b d", t=TILES, h=NH, b=2)
        h1T = sb("h1T", [64, TOK])
        t1 = sb("t1", [P, L]); sg1 = sb("sg1", [P, L]); t2 = sb("t2", [P, L]); sg2 = sb("sg2", [P, L])
        wk = [sb(f"wk{i}", [P, L]) for i in range(3)]
        m8 = [sb(f"m8_{i}", [P, 8]) for i in range(5)]
        cand = sb("cand", [P, L]); selk = sb("selk", [P, L]); keep = sb("keep", [P, L]); bias = sb("bias", [P, L])
        mb = sb("mb", [P, NH, L], BF16)
        mx = sb("mx", [P, 2, NH])
        Pm = sb("Pm", [P, 2, NH * L]); PT = sb("PT", [P, 2, HP, P])
        rden = sb("rden", [P, NH]); yn = sb("yn", [P, E])
        th = sb("th", [P, C * TOK]); u = sb("u", [P, C * TOK]); hs = sb("hs", [P, C * TOK])
        sabs = sb("sabs", [P, 2]); thr = sb("thr", [P, 2]); nthr = sb("nthr", [P, 2])
        vr = sb("vr", [P, 2, TILES]); rq = sb("rq", [P, 2, TILES]); pq = sb("pq", [P, 2, TILES]); rr = sb("rr", [P, TILES]); r4 = sb("r4", [P, TILES])
        msq = sb("msq", [P, TILES]); rg = sb("rg", [P, TILES]); rge = sb("rge", [P, TILES]); rgi = sb("rgi", [P, TILES])
        lg = sb("lg", [P, SLOTS * TILES, NX])


        NT = SLOTS * TILES
        flat = Pm[:, :, :].rearrange("p a n -> p (a n)")
        rs = {n: flat[:, k * NT * NX:(k + 1) * NT * NX]
              for k, n in enumerate(("ex", "pr", "s", "m", "a", "b", "oh1", "oh2"))}
        r3 = {n: v[:, :].rearrange("p (t e) -> p t e", e=NX) for n, v in rs.items()}
        rsm = {n: sb("rv_" + n, [P, NT]) for n in ("mx", "sum", "inv", "m1", "c1", "m2", "c2")}
        gs, wins, gk, gd = (th[:, k * NT * 4:(k + 1) * NT * 4].rearrange("p (t g) -> p t g", g=4) for k in range(4))
        cmp = sb("cmp", [P, NT])
        wt = sb("wt", [P, 2 * NT]); ei = sb("ei", [P, 2 * NT]); gg = sb("gg", [P, 2 * NT])
        code = sb("code", [P, 2 * NT])
        cnt = sb("cnt", [P, NX]); off = sb("off", [P, NX])
        AC = [sb("AT", [P, 64]), sb("CT", [P, 64])]
        tabA = sb("tabA", [64, HID]); tabC = sb("tabC", [64, HID])
        ow = work[:, 0, :].rearrange("p (b n r) -> p b n r", b=2, n=4)
        owT = work[0:64, 1:3, :]
        tz, sz = work[:, 3:5, :], work[:, 5:7, :]
        racc = sb("racc", [64, HID]); gm = sb("gm", [64, HID]); gT = sb("gT", [P, 64])
        QUADS = 2 * NT // 4
        UP_BANKS = (4, 5, 6, 7)

        spare = work[:, 0:NF, :].rearrange("p (n k) t -> p n (k t)", n=2)
        wup_f = wup_s[:, :, :].rearrange("p c n -> p (c n)")
        wdn_f = wdn_s[:, :, :].rearrange("p f n -> p (f n)")
        half_q = wqkv_s[:, :, :].rearrange("p c n -> p (c n)")[:, 0:C * FF // 2].bitcast(F16)
        half_t = tokW_s[:, :, :].rearrange("p k n -> p (k n)")[:, 0:NF * E // 2].bitcast(F16)
        wup_t, wdn_t = half_q, half_t
        wup_h = half_q.rearrange("p (c n) -> p c n", c=C)
        wdn_h = half_t.rearrange("p (f n) -> p f n", f=NF)

        kT = qT
        qM = kM
        F = Pm
        relu_s = (th, hs)
        lin = (u, w1_s[:, :, :, :].rearrange("p e c h -> p (e c h)")[:, 0:NH * L])
        sqt = (PT[:, 0, 0:4, :], PT[:, 0, 4:8, :])
        sqa = PT[:, 1, 0:4, :]
        Gb = work[:, :, :].bitcast(F16)
        G_hi, G_lo = Gb[:, :, 0:TOK], Gb[:, :, TOK:2 * TOK]
        x4b = xT2[:, :, :].bitcast(F16)
        x4_hi, x4_lo = x4b[:, :, 0:TOK], x4b[:, :, TOK:2 * TOK]
        g32 = w3_s[:, :, :, :].rearrange("p e c h -> p (e c h)").rearrange("p (k n) -> p k n", k=4)

        def sems(names):
            return (sem(n) for n in names.split())

        a_mm, abs_mm, abs_ok, acc_mm, b_mm, bias_ok, Bk_mm = sems("a_mm abs_mm abs_ok acc_mm b_mm bias_ok Bk_mm")
        Bk_out, Bq_mm, Bq_out, Bs_mm, Bv_mm, Bv_out = sems("Bk_out Bq_mm Bq_out Bs_mm Bv_mm Bv_out")
        cnt_mm, cnt_ok, dn_mm, embed_mm, embed_out, f0_ok = sems("cnt_mm cnt_ok dn_mm embed_mm embed_out f0_ok")
        f2_ok, g_ok, gate_mm, gex_ok, gh_out, gl_ok = sems("f2_ok g_ok gate_mm gex_ok gh_out gl_ok")
        gl_out, gm_ok, gT_mm, gT_ok, h1_mm, h1_out, h2_ok = sems("gl_out gm_ok gT_mm gT_ok h1_mm h1_out h2_ok")
        h3_ok, h4_ok, h5_ok, hs_ok, k_mm, k_out, keep_ok = sems("h3_ok h4_ok h5_ok hs_ok k_mm k_out keep_ok")
        lg_ok, lin_ok, loaded_A, loaded_B, loaded_embed = sems("lg_ok lin_ok loaded_A loaded_B loaded_embed")
        mb_ok, msq_ok, ow_ok, owT_mm, owT_ok, p_exp, p_sub = sems("mb_ok msq_ok ow_ok owT_mm owT_ok p_exp p_sub")
        patch_in, pr_mm, pt_mm, pt_out, pv_mm, q_mm, q_out = sems("patch_in pr_mm pt_mm pt_out pv_mm q_mm q_out")
        quad_even, quad_odd, r4_step, r8_mm, r8_ok = sems("quad_even quad_odd r4_step r8_mm r8_ok")
        racc_ok, rden_ok, relu_ok, rg_ok, rg_step, rl_mm = sems("racc_ok rden_ok relu_ok rg_ok rg_step rl_mm")
        routed_step, rsg1, rstd1_ok, rstd2_ok, rstd3_ok = sems("routed_step rsg1 rstd1_ok rstd2_ok rstd3_ok")
        rstd4_ok, rt1, rt2, s_mm, selk_ok, setup_b = sems("rstd4_ok rt1 rt2 s_mm selk_ok setup_b")
        setup_v, sh_mm, smax, sq_ok, sqa_ok, ss_mm, stored = sems("setup_v sh_mm smax sq_ok sqa_ok ss_mm stored")
        sz_ok, tab_mm, tab_ok, tab_t, tabT_ok, th_neg = sems("sz_ok tab_mm tab_ok tab_t tabT_ok th_neg")
        th_ok, th_set, thr_ok, top_step, tz_ok, u_ok = sems("th_ok th_set thr_ok top_step tz_ok u_ok")
        up_mm, V2_zero, v_mm, v_out, ve1_mv, ve1_ok = sems("up_mm V2_zero v_mm v_out ve1_mv ve1_ok")
        ve1_st, ve2_mv, ve2_ok, ve2_st, ve3_mv, ve3_ok = sems("ve1_st ve2_mv ve2_ok ve2_st ve3_mv ve3_ok")
        ve3_st, ve4_mv, ve4_ok, ve4_st, x3T_a, x3T_mm = sems("ve3_st ve4_mv ve4_ok ve4_st x3T_a x3T_mm")
        x3T_v, x4T_a, x4T_mm, x4T_v, xn1_ok, xn2_ok = sems("x3T_v x4T_a x4T_mm x4T_v xn1_ok xn2_ok")
        xn3_ok, xn4_ok, xT1_a, xT1_mm, xT2_a, xT2_mm, Y_mm = sems("xn3_ok xn4_ok xT1_a xT1_mm xT2_a xT2_mm Y_mm")
        Y_out, y_out, yT_mm, yT_out, z_mm = sems("Y_out y_out yT_mm yT_out z_mm")

        def first(g):
            return isinstance(g, int) and g == 0

        def in_reg(eng, value):
            return value if isinstance(value, int) else eng.to_reg(value)

        steps = {}

        def after(chain, n=1):
            steps[chain] = steps.get(chain, 0) + n
            return steps[chain]

        loads_embed = [(tokW_s, tokW), (ident_s, ident), (tokb_s, tokb)]
        loads_A = [(wqkv_s, wqkv), (bqk_s, bqk), (par_s, par), (rW1_s, rW1), (rb1_s, rb1), (rW2c, rW2), (rb2_s, rb2),
                   (rev64_s, rev64), (bv_s, bv), (delta_s, delta), (self_, sel), (gateW_s, gateW), (s1_s, s1),
                   (s3_s, s3), (s2_s, s2)]
        loads_B = [(wup_s, wup), (wdn_s, wdn), (cmask_s, cmask), (w1_s, w1), (w3_s, w3), (w2_s, w2), (eb_s, eb),
                   (rev8_s, rev8), (ridx_s, ridx), (iota_s, iota64), (wat_s, wat), (wpr_s, wpr)]
        LAST = SLOTS - 1
        block = ctx.enter_context(nc.Block())

        @block.sync
        def _(sp):
            def load_patches(g):
                sp.dma_start(patch, x[g, :, :, :]).then_inc(patch_in, 16)

            load_patches(0)
            for dst, src in loads_embed:
                sp.dma_start(dst[:], src).then_inc(loaded_embed, 16)
            for dst, src in loads_A:
                sp.dma_start(dst[:], src).then_inc(loaded_A, 16)
            for dst, src in loads_B:
                sp.dma_start(dst[:], src).then_inc(loaded_B, 16)
            with sp.Fori(0, LAST) as i:
                sp.wait_ge(embed_mm, TILES * i + TILES)
                load_patches(i + 1)
            with sp.Fori(0, SLOTS) as i:
                sp.wait_ge(h5_ok, TILES * i + TILES)
                sp.dma_start(out[i, :, :, :], H[:, bass.ds(TILES * i, TILES), :]).then_inc(stored, 16)
            sp.wait_ge(stored, 16 * SLOTS)

        @block.tensor
        def _(pe):
            def embed(g):
                pe.wait_ge(patch_in, 16 * g + 16)
                for t in range(TILES):
                    for k in range(KP):
                        m = pe.matmul(PS[:, 4 + t // 2, (t % 2) * E:(t % 2 + 1) * E],
                                      patch[:, k, t * P:(t + 1) * P], tokW_s[:, k, :],
                                      start=(k == 0), stop=(k == KP - 1))
                    m.then_inc(embed_mm, 1)

            def transpose_in(g, xn, banks, ready, done):
                banks = banks if isinstance(banks, tuple) else (banks, banks + 1)
                for c in range(C):
                    for t in range(TILES):
                        if c == 0:
                            pe.wait_ge(ready, TILES * g + t + 1)
                        m = pe.transpose(PS[:, banks[c], t * P:(t + 1) * P], xn[:, t, c * P:(c + 1) * P],
                                         ident_s[:, :])
                    m.then_inc(done, 1)

            def proj_T(bank, w, col, xT, done, cols=P):
                for c in range(C):
                    m = pe.matmul(PS[0:cols, bank, :], w[:, c, col:col + cols], xT[:, c, 0:TOK],
                                  start=(c == 0), stop=(c == C - 1))
                m.then_inc(done, 1)

            def A2(g):
                transpose_in(g, xn1, 4, xn1_ok, xT1_mm)
                pe.wait_ge(xT1_a, 4 * g + 4)
                if not first(g):
                    pe.wait_ge(y_out, 2 * TILES * g)
                for c in range(C):
                    proj_T(6 + c, wqkv_s, c * P, xT1, q_mm)
                if not first(g):
                    pe.wait_ge(p_sub, TILES * g)
                for c in range(C):
                    proj_T(c, wqkv_s, E + c * P, xT1, k_mm)
                proj_T(4, rW1_s, 0, xT1, h1_mm, 64)
                for n in range(TILES):
                    value_rows(2 + n // 2, n % 2, n * P)
                pe.wait_ge(h1_out, g + 1)
                for j in range(IMGS):
                    m = pe.matmul(PS[:, 5, 0:L], rW2_s[:, j, :], h1T[:, j * L:(j + 1) * L],
                                  start=(j == 0), stop=(j == IMGS - 1))
                m.then_inc(rl_mm, 1)
                pe.wait_ge(k_out, 4 * g + 4)
                for n in range(TILES):
                    value_rows(n // 2, n % 2, n * P + L)

            def value_rows(bank, half, at):
                for c in range(C):
                    m = pe.matmul(PS[:, bank, half * E:(half + 1) * E], xT1[:, c, at:at + P],
                                  wqkv_s[:, c, 2 * E:3 * E], start=(c == 0), stop=(c == C - 1))
                m.then_inc(v_mm, 1)

            def image_scores(t, left, right, hb):
                for b in range(2):
                    for c in range(C):
                        for i in range(4):
                            at, r = t * P + b * L, slice(32 * i, 32 * i + 32)
                            m = pe.matmul(PS[b * L:(b + 1) * L, i, hb + c * P:hb + (c + 1) * P],
                                          left[r, c, at:at + L], right[r, c, :, at:at + L],
                                          start=False, stop=True, tile_position=(32 * i, b * L),
                                          skip_group_check=True)
                return m

            def scores(g, pair):
                if pair == 0:
                    pe.wait_ge(mb_ok, g + 1)
                    pe.wait_ge(q_out, 2 * g + 2)
                    pe.wait_ge(v_out, 5 * g + 5)
                else:
                    pe.wait_ge(p_sub, TILES * g + 2)
                for t in (2 * pair, 2 * pair + 1):
                    hb = (t % 2) * 256
                    for i in range(4):
                        pe.matmul(PS[:, i, hb:hb + 256], selb[:, t, :], mb[:, 4 * i:4 * i + 4, :],
                                  start=True, stop=False, skip_group_check=True)
                    image_scores(t, qT, kM, hb).then_inc(s_mm, 1)

            def weights_T(g, t, half):
                if half == 0:
                    pe.wait_ge(p_exp, TILES * g + t + 1)
                if t % 2:
                    pe.wait_ge(pt_out, 2 * (TILES * g + t) + half - 1)
                for hp in range(4):
                    at = (4 * half + hp) * P
                    m = pe.transpose(PS[:, 4 + half, hp * P:(hp + 1) * P], Pm[:, t % 2, at:at + P], ident_s[:, :])
                m.then_inc(pt_mm, 1)

            def values(g, t, half):
                pe.wait_ge(pt_out, 2 * (TILES * g + t) + half + 1)
                if t and half == 0:
                    pe.wait_ge(y_out, 2 * (TILES * g + t))
                for hp in range(4 * half, 4 * half + 4):
                    at = PV0 + hp * 4 * VW
                    m = pe.matmul(PF[:, at:at + 4 * VW], PT[:, t % 2, hp, :], Vb[:, t, hp, :, :, :],
                                  start=True, stop=True)
                m.then_inc(pv_mm, 1)

            def attend(g, pair):
                t = 2 * pair
                weights_T(g, t, 0)
                weights_T(g, t, 1)
                values(g, t, 0)
                weights_T(g, t + 1, 0)
                values(g, t, 1)
                weights_T(g, t + 1, 1)
                values(g, t + 1, 0)
                values(g, t + 1, 1)

            def A4(g, last):
                if last:
                    pe.wait_ge(y_out, 2 * TILES * (g + 1))
                else:
                    pe.wait_ge(q_out, 2 * g + 4)
                transpose_in(g, xn2, 6, xn2_ok, xT2_mm)
                pe.wait_ge(xT2_a, 2 * g + 2)
                if last:
                    pe.wait_ge(pt_out, 2 * TILES * (g + 1))
                else:
                    pe.wait_ge(h1_out, g + 2)
                for t in range(TILES):
                    for c in range(C):
                        m = pe.matmul(PS[:, 4, t * NX:(t + 1) * NX], xT2[:, c, t * P:(t + 1) * P],
                                      gateW_s[:, c, :], start=(c == 0), stop=(c == C - 1))
                m.then_inc(gate_mm, 1)
                if not last:
                    pe.wait_ge(rt1, g + 2)
                proj_T(5, s1_s, 0, xT2, a_mm)
                proj_T(6, s3_s, 0, xT2, b_mm)
                proj_T(7, s1_s, P, xT2, a_mm)
                pe.wait_ge(lg_ok, g + 1)
                proj_T(4, s3_s, P, xT2, b_mm)
                if not last:
                    scores(g + 1, 0)
                pe.wait_ge(hs_ok, 2 * g + 2)
                for t in range(TILES):
                    for c in range(C):
                        m = pe.matmul(PS[:, 5 + t // 2, (t % 2) * E:(t % 2 + 1) * E],
                                      hs[:, c * TOK + t * P:c * TOK + (t + 1) * P], s2_s[:, c, :],
                                      start=(c == 0), stop=(c == C - 1))
                    m.then_inc(sh_mm, 1)

            pe.wait_ge(loaded_embed, 16 * len(loads_embed))
            embed(0)
            pe.wait_ge(loaded_A, 16 * len(loads_A))
            pe.wait_ge(setup_v, SETUP_V)
            A2(0)
            scores(0, 0)
            with pe.Fori(0, LAST) as i:
                scores(i, 1)
                pe.wait_ge(h3_ok, 2 * i + 1)
                attend(i, 0)
                pe.wait_ge(pt_out, 2 * (TILES * i + 2))
                embed(i + 1)
                pe.wait_ge(embed_out, 2 * i + 4)
                attend(i, 1)
                A2(i + 1)
                A4(i, False)
            scores(LAST, 1)
            pe.wait_ge(h3_ok, 2 * LAST + 1)
            pe.wait_ge(abs_ok, 2)
            pe.wait_ge(h3_ok, 2 * LAST + 1)
            pe.matmul(PS[:, 4, 0:2], ones[:, :], sabs[:, :], start=True, stop=True).then_inc(abs_mm, 1)
            pe.wait_ge(th_set, 2)
            attend(LAST, 0)
            pe.wait_ge(pt_out, 2 * (TILES * LAST + 2))
            attend(LAST, 1)
            A4(LAST, True)

            pe.wait_ge(h3_ok, 2 * SLOTS + 1)
            for n, w in enumerate((w1_s, w3_s)):
                for e in range(NX):
                    for c in range(C):
                        m = pe.matmul(PS[:, n, e * NX:(e + 1) * NX], w[:, e, c, :], xT2[:, c, 0:NX],
                                      start=(c == 0), stop=(c == C - 1))
                m.then_inc(tab_mm, 1)
            for n in range(2):
                pe.wait_ge(tabT_ok, n + 1)
                pe.transpose(PS[0:64, 2 + n, 0:P], AC[n][:, :], ident_s[:, :]).then_inc(tab_t, 1)
            pe.wait_ge(cnt_ok, 1)
            pe.matmul(PS[:, 4, 0:NX], ones[:, :], cnt[:, :], start=True, stop=True).then_inc(cnt_mm, 1)
            pe.wait_ge(tab_ok, 2)

            def quad_in(q, b):
                count = in_reg(pe, 4 * q + 4)
                pe.wait_ge(setup_v, 1)
                pe.wait_ge(ow_ok, count)
                for n in range(4):
                    m = pe.transpose(PS[0:64, b, n * P:(n + 1) * P], ow[:, b, n, :], ident_s[:, :])
                m.then_inc(owT_mm, 1)
                pe.wait_ge(owT_ok, q + 1)
                for n in range(4):
                    m = pe.matmul(PS[:, 2 + b, n * P:(n + 1) * P], owT[:, b, n * P:(n + 1) * P], tabA[:, :],
                                  start=True, stop=True)
                m.then_inc(z_mm, 1)

            def quad_out(q, b):
                pe.wait_ge(sz_ok, q + 1)
                for n in range(4):
                    m = pe.matmul(PS[0:64, 4 + b, 0:HID], ow[:, b, n, :], sz[:, b, n * P:(n + 1) * P],
                                  start=(n == 0), stop=(n == 3))
                m.then_inc(acc_mm, 1)

            with pe.Fori(0, QUADS // 2) as i:
                pe.wait_ge(racc_ok, 2 * i + 1)
                for b in range(2):
                    quad_in(2 * i + b, b)
                for b in range(2):
                    quad_out(2 * i + b, b)
            pe.wait_ge(gm_ok, 1)
            pe.transpose(PS[:, 6, 0:64], gm[:, :], ident_s[0:64, 0:64]).then_inc(gT_mm, 1)
            pe.wait_ge(gT_ok, 1)
            for e in range(NX):
                m = pe.matmul(PS[0:NX, 7, 0:E], gT[:, e * NX:(e + 1) * NX], w2_s[:, e, :],
                              start=(e == 0), stop=(e == NX - 1))
            m.then_inc(r8_mm, 1)
            pe.wait_ge(r8_ok, 1)

            def B1_qk(g, before):
                pe.wait_ge(x3T_a, g + 1)
                pe.wait_ge(x3T_v, g + 1)
                for c in range(C):
                    proj_T(4 + c, wat_s, c * P, xT1, Bq_mm)
                for c in range(C):
                    if before:
                        pe.wait_ge(h5_ok, TILES * (g - 2) + 2 * c + 2)
                    elif not first(g) and c == 1:
                        pe.wait_ge(h4_ok, 1)
                    proj_T(6 + c, wat_s, E + c * P, xT1, Bk_mm)

            def B1_v(g, tiles):
                for t in tiles:
                    if t == 0:
                        pe.wait_ge(Bk_out, 2 * g + 2)
                    for c in range(C):
                        m = pe.matmul(PS[:, (7, 5)[t // 2], (t % 2) * E:(t % 2 + 1) * E],
                                      xT1[:, c, t * P:(t + 1) * P], wat_s[:, c, 2 * E:3 * E],
                                      start=(c == 0), stop=(c == C - 1))
                    m.then_inc(Bv_mm, 1)

            def B2_scores(g, t):
                if t == 0:
                    pe.wait_ge(Bq_out, 4 * g + 4)
                    pe.wait_ge(Bk_out, 2 * g + 2)
                elif t == 2:
                    pe.wait_ge(f2_ok, TILES * g + 2)
                hb = (t % 2) * 256
                for i in range(4):
                    pe.matmul(PS[:, i, hb:hb + 256], identb[:, :], cmaskb[:, :, :], start=True, stop=False,
                              skip_group_check=True)
                image_scores(t, kT, qM, hb).then_inc(Bs_mm, 1)

            def B2_values(g, pair, banks):
                for t in (2 * pair, 2 * pair + 1):
                    pe.wait_ge(f2_ok, TILES * g + t + 1)
                    for hp in range(HP):
                        m = pe.matmul(PS[:, banks[t % 2], hp * L:(hp + 1) * L], F[:, t % 2, hp * P:(hp + 1) * P],
                                      V2[:, t, 2 * hp:2 * hp + 2, :, :], start=True, stop=True)
                    m.then_inc(Y_mm, 1)

            def B2_turn(g, t, bank):
                pe.wait_ge(Y_out, 2 * (TILES * g + t + 1))
                for b in range(2):
                    m = pe.transpose(PS[:, bank, (t % 2) * E + b * P:(t % 2) * E + (b + 1) * P],
                                     xn2[:, t, b * P:(b + 1) * P], ident_s[:, :])
                m.then_inc(yT_mm, 1)

            def B2_proj(g, pair, bank):
                pe.wait_ge(yT_out, 2 * g + pair + 1)
                for t in (2 * pair, 2 * pair + 1):
                    for e in range(2):
                        m = pe.matmul(PS[:, bank, (t % 2) * E:(t % 2 + 1) * E], xT2[:, e, t * P:(t + 1) * P],
                                      wpr_s[:, e, :], start=(e == 0), stop=(e == 1))
                m.then_inc(pr_mm, 1)

            def B3_up(g, nxt):
                if nxt:
                    B2_scores(g + 1, 1)
                pe.wait_ge(x4T_a, 2 * g + 2)
                pe.wait_ge(x4T_v, 2 * g + 2)
                if nxt:
                    pe.wait_ge(Bv_out, 8 * g + 16)
                for f in range(NF):
                    if f >= 4:
                        pe.wait_ge(g_ok, NF * g + f - 3)
                    for k, (part, c) in enumerate((part, c) for part in (x4_hi, x4_lo) for c in range(C)):
                        m = pe.matmul(PS[:, UP_BANKS[f % 4], :], wup_h[:, c, f * P:(f + 1) * P], part[:, c, :],
                                      start=(k == 0), stop=(k == 2 * C - 1))
                    m.then_inc(up_mm, 1)

            def B3_squares(g):
                pe.wait_ge(sqa_ok, (NF - 1) * (g + 1))
                for t in range(TILES):
                    m = pe.matmul(PS[:, 7, t:t + 1], sqa[:, t, :], ones[:, 0:1], start=True, stop=True)
                m.then_inc(ss_mm, 1)

            def B3_down(g, nxt):
                pe.wait_ge(gl_out, NF * g + NF)
                pe.wait_ge(msq_ok, g + 1)
                for t in range(TILES):
                    if t == 2 and nxt:
                        pe.wait_ge(h4_ok, 2 * (g + 1) + 1)
                    for k, (part, f) in enumerate((part, f) for part in (G_hi, G_lo) for f in range(NF)):
                        m = pe.matmul(PS[:, 6 + t // 2, (t % 2) * E:(t % 2 + 1) * E],
                                      part[:, f, t * P:(t + 1) * P], wdn_h[:, f, :],
                                      start=(k == 0), stop=(k == 2 * NF - 1))
                    m.then_inc(dn_mm, 1)

            def slot_B(g, prev, nxt):
                B2_scores(g, 2)
                B2_scores(g, 3)
                if prev:
                    pe.wait_ge(g_ok, NF * g)
                else:
                    pe.wait_ge(Bv_out, 8 * g + 8)
                B2_values(g, 0, (4, 5))
                B2_turn(g, 0, 6)
                if prev:
                    B3_squares(g - 1)
                B2_turn(g, 1, 6)
                if nxt:
                    transpose_in(g + 1, xn1, 4, xn3_ok, x3T_mm)
                if prev:
                    pe.wait_ge(msq_ok, g)
                B2_proj(g, 0, 7)
                if prev:
                    B3_down(g - 1, True)
                if nxt:
                    B1_qk(g + 1, prev)
                    pe.wait_ge(Bq_out, 4 * g + 8)
                B2_values(g, 1, (4, 5))
                if nxt:
                    pe.wait_ge(Bk_out, 2 * g + 3)
                else:
                    pe.wait_ge(h5_ok, TILES * g - 2)
                B2_turn(g, 2, 6)
                if nxt:
                    B1_v(g + 1, (0,))
                B2_turn(g, 3, 6)
                if nxt:
                    B1_v(g + 1, (1,))
                B2_proj(g, 1, 4)
                if nxt:
                    B1_v(g + 1, (2, 3))
                    B2_scores(g + 1, 0)
                    pe.wait_ge(Bv_out, 8 * g + 12)
                else:
                    pe.wait_ge(h5_ok, TILES * g)
                transpose_in(g, xn2, 6, xn4_ok, x4T_mm)
                B3_up(g, nxt)

            transpose_in(0, xn1, 4, xn3_ok, x3T_mm)
            B1_qk(0, False)
            pe.wait_ge(Bq_out, 4)
            B1_v(0, range(TILES))
            B2_scores(0, 0)
            B2_scores(0, 1)
            slot_B(0, False, True)
            with pe.Fori(1, LAST) as i:
                slot_B(i, True, True)
            slot_B(LAST, True, False)
            B3_squares(LAST)
            B3_down(LAST, False)

        @block.scalar
        def _(act):
            def a_A2(g):
                for c in range(C):
                    act.wait_ge(xT1_mm, 2 * g + c + 1)
                    act.activation(xT1[:, c, 0:TOK], PS[:, 4 + c, :], ACT.Copy).then_inc(xT1_a, 1)
                for c in range(C):
                    act.activation(xT1[:, c, TOK:TOK + L], PS[:, 4 + c, 0:L], ACT.Copy).then_inc(xT1_a, 1)
                for c in range(C):
                    act.wait_ge(q_mm, 2 * g + c + 1)
                    act.activation(qT[:, c, :], PS[:, 6 + c, :], ACT.Identity, bias=bqk_s[:, c:c + 1])\
                       .then_inc(q_out, 1)
                act.wait_ge(h1_mm, g + 1)
                act.activation(h1T[:, :], PS[0:64, 4, :], ACT.Relu, bias=rb1_s[:, :]).then_inc(h1_out, 1)
                act.wait_ge(rl_mm, g + 1)
                act.activation(t1[:, :], PS[:, 5, 0:L], ACT.Tanh, bias=rb2h[:, :], scale=0.5).then_inc(rt1, 1)
                act.wait_ge(rsg1, g + 1)
                act.activation(t2[:, :], sg1[:, :], ACT.Tanh, scale=0.5).then_inc(rt2, 1)

            def exps(g, pair):
                for t in (2 * pair, 2 * pair + 1):
                    act.wait_ge(p_sub, TILES * g + t + 1)
                    act.activation(Pm[:, t % 2, :], Pm[:, t % 2, :], ACT.Exp, scale=HD ** -0.5)\
                       .then_inc(p_exp, 1)

            def turns(g, pair):
                for t in (2 * pair, 2 * pair + 1):
                    for half in range(2):
                        act.wait_ge(pt_mm, 2 * (TILES * g + t) + half + 1)
                        act.activation(PT[:, t % 2, 4 * half:4 * half + 4, :], PS[:, 4 + half, :], ACT.Copy)\
                           .then_inc(pt_out, 1)

            def a_A4(g):
                for c in range(C):
                    act.wait_ge(xT2_mm, 2 * g + c + 1)
                    act.activation(xT2[:, c, :], PS[:, 6 + c, :], ACT.Copy).then_inc(xT2_a, 1)
                for c in range(C):
                    act.wait_ge(a_mm, 2 * g + c + 1)
                    act.activation(th[:, c * TOK:(c + 1) * TOK], PS[:, (5, 7)[c], :], ACT.Tanh, scale=0.5)\
                       .then_inc(th_ok, 1)

            act.wait_ge(loaded_A, 16 * len(loads_A))
            act.wait_ge(setup_v, SETUP_V)
            a_A2(0)
            exps(0, 0)
            with act.Fori(0, LAST) as i:
                turns(i, 0)
                exps(i, 1)
                turns(i, 1)
                a_A2(i + 1)
                a_A4(i)
                exps(i + 1, 0)
            act.wait_ge(loaded_B, 16 * len(loads_B))
            act.wait_ge(embed_mm, TILES * SLOTS)
            act.activation(spare[:, 0, :], wup_f, ACT.Abs, accum_out=sabs[:, 0:1]).then_inc(abs_ok, 1)
            act.activation(spare[:, 1, :], wdn_f, ACT.Abs, accum_out=sabs[:, 1:2]).then_inc(abs_ok, 1)
            turns(LAST, 0)
            exps(LAST, 1)
            turns(LAST, 1)
            a_A4(LAST)

            for n in range(2):
                act.wait_ge(tab_mm, n + 1)
                act.activation(AC[n][:, :], PS[:, n, 0:64], ACT.Copy).then_inc(tabT_ok, 1)
            for n in range(2):
                act.wait_ge(tab_t, n + 1)
                act.activation((tabA, tabC)[n][:, :], PS[0:64, 2 + n, 0:P], ACT.Copy).then_inc(tab_ok, 1)
            act.wait_ge(gl_ok, 1)
            act.activation(rs["ex"][:, :], rs["a"][:, :], ACT.Exp).then_inc(gex_ok, 1)
            with act.Fori(0, QUADS // 2) as i:
                for b in range(2):
                    act.wait_ge(owT_mm, 2 * i + b + 1)
                    act.activation(owT[:, b, :], PS[0:64, b, :], ACT.Copy).then_inc(owT_ok, 1)
                    act.wait_ge(z_mm, 2 * i + b + 1)
                    act.activation(tz[:, b, :], PS[:, 2 + b, :], ACT.Tanh, scale=0.5).then_inc(tz_ok, 1)
            act.wait_ge(gT_mm, 1)
            act.activation(gT[:, :], PS[:, 6, 0:64], ACT.Copy).then_inc(gT_ok, 1)

            def a_B1_k(g):
                act.wait_ge(x3T_mm, 2 * g + 1)
                act.activation(xT1[:, 0, 0:TOK], PS[:, 4, :], ACT.Copy).then_inc(x3T_a, 1)
                for c in range(C):
                    act.wait_ge(Bk_mm, 2 * g + c + 1)
                    act.activation(kT[:, c, :], PS[:, 6 + c, :], ACT.Copy).then_inc(Bk_out, 1)

            def a_B1_v(g):
                for t in range(TILES):
                    if t % 2 == 0:
                        act.wait_ge(Bv_mm, TILES * g + t + 2)
                    for b in range(2):
                        r = slice(b * L, (b + 1) * L)
                        act.activation(V2[r, t, :, b, :], PS[r, (7, 5)[t // 2], (t % 2) * E:(t % 2 + 1) * E]
                                       .rearrange("p (h d) -> p h d", d=HD), ACT.Copy).then_inc(Bv_out, 1)

            def relus(g, t):
                hb = (t % 2) * 256
                act.wait_ge(Bs_mm, TILES * g + 2 * (t // 2) + 2)
                act.activation(relu_s[t % 2][:, :], PS[:, 0:4, hb:hb + 256], ACT.Relu).then_inc(relu_ok, 1)

            def lins(g, t):
                hb = (t % 2) * 256
                act.activation(lin[t % 2][:, :], PS[:, 0:4, hb:hb + 256], ACT.Relu, scale=-0.01).then_inc(lin_ok, 1)

            def outs(g, tiles, banks):
                for t in tiles:
                    act.wait_ge(Y_mm, TILES * g + t + 1)
                    y = PS[:, banks[t % 2], :].rearrange("p (hp e b d) -> p hp e b d", hp=HP, e=2, b=2)
                    for e in range(2):
                        r = slice(e * L, (e + 1) * L)
                        act.activation(xn2[r, t, :].rearrange("p (b hp d) -> p b hp d", b=2, hp=HP),
                                       y[r, :, e, :, :].rearrange("p hp b d -> p b hp d"), ACT.Copy, scale=1e-3)\
                           .then_inc(Y_out, 1)

            def a_B3(g, nxt):
                for c in range(C):
                    act.wait_ge(x4T_mm, 2 * g + c + 1)
                    act.activation(x4_hi[:, c, :], PS[:, 6 + c, :], ACT.Copy).then_inc(x4T_a, 1)
                if nxt:
                    relus(g + 1, 0)
                    relus(g + 1, 1)
                    lins(g + 1, 0)
                for f in range(NF):
                    act.wait_ge(up_mm, NF * g + f + 1)
                    if f >= 4:
                        act.wait_ge(gl_out, NF * g + f - 3)
                    act.activation(g32[:, f % 4, :], PS[:, UP_BANKS[f % 4], :], ACT.Gelu).then_inc(g_ok, 1)
                    if f == 0 and nxt:
                        lins(g + 1, 1)
                    if f > 0:
                        square(g, f - 1)
                square(g, NF - 1)

            def square(g, f):
                act.wait_ge(g_ok, NF * g + f + 1)
                if f == 0:
                    if not first(g):
                        act.wait_ge(ss_mm, g)
                    act.activation(sqa, g32[:, 0, :], ACT.Square).then_inc(sq_ok, 1)
                else:
                    if f > 2:
                        act.wait_ge(sqa_ok, (NF - 1) * g + f - 2)
                    act.activation(sqt[f % 2], g32[:, f % 4, :], ACT.Square).then_inc(sq_ok, 1)

            def slot_B(g, prev, nxt):
                relus(g, 2)
                relus(g, 3)
                outs(g, (0, 1), (4, 5))
                lins(g, 2)
                lins(g, 3)
                if nxt:
                    a_B1_k(g + 1)
                outs(g, (2, 3), (4, 5))
                if nxt:
                    a_B1_v(g + 1)
                a_B3(g, nxt)

            act.wait_ge(V2_zero, 1)
            a_B1_k(0)
            a_B1_v(0)
            relus(0, 0)
            relus(0, 1)
            lins(0, 0)
            lins(0, 1)
            slot_B(0, False, True)
            with act.Fori(1, LAST) as i:
                slot_B(i, True, True)
            slot_B(LAST, True, False)

        @block.gpsimd
        def _(pool):
            def p_rstd(var_ok, n, src, dst, done):
                pool.wait_ge(var_ok, n)
                pool.tensor_tensor(dst[:, :], src[:, :], mhalf[:, :], ALU.pow).then_inc(done, 1)

            def p_mask(g):
                pool.wait_ge(bias_ok, g + 1)
                if not first(g):
                    pool.wait_ge(s_mm, TILES * g)
                pool.tensor_tensor(mb[:, :, :], bias[:, :].unsqueeze(1).broadcast_to([P, NH, L]),
                                   delta_s[:, :].unsqueeze(2).broadcast_to([P, NH, L]), ALU.mult)\
                    .then_inc(mb_ok, 1)

            pool.wait_ge(setup_v, 7)
            p_rstd(ve1_ok, 1, ve, rstd, rstd1_ok)
            pool.wait_ge(loaded_A, 16 * len(loads_A))
            p_mask(0)
            with pool.Fori(0, LAST) as i:
                p_rstd(ve1_ok, i + 2, ve, rstd, rstd1_ok)
                p_rstd(ve2_ok, i + 1, ve2, rstd2, rstd2_ok)
                p_mask(i + 1)
            p_rstd(ve2_ok, SLOTS, ve2, rstd2, rstd2_ok)

            def quads(g, t):
                pool.wait_ge(relu_ok, TILES * g + t + 1)
                v = relu_s[t % 2][:, :]
                pool.tensor_tensor(v, v, v, ALU.mult).then_inc(quad_even, 1)

            def p_ln4(g, pair):
                ts = slice(2 * pair, 2 * pair + 2)
                pool.wait_ge(ve4_ok, 4 * g + 2 * pair + 2)
                pool.tensor_tensor(rq[:, :, ts], vr[:, :, ts], pq[:, :, ts], ALU.pow).then_inc(rstd4_ok, 1)

            def p_rg(g):
                pool.wait_ge(msq_ok, g + 1)
                pool.tensor_tensor(rg[:, :], msq[:, :], phalf[:, :], ALU.pow).then_inc(rg_ok, 1)

            def p_B3(g, nxt):
                if nxt:
                    quads(g + 1, 0)
                for f in range(NF):
                    if f > 0:
                        pool.wait_ge(sq_ok, NF * g + f + 1)
                        if f > 1:
                            pool.wait_ge(sqa_ok, (NF - 1) * g + f - 1)
                        pool.tensor_tensor(sqa, sqa, sqt[f % 2], ALU.add).then_inc(sqa_ok, 1)

            def slot_B(g, prev, nxt):
                if nxt:
                    p_rstd(ve3_ok, g + 2, ve, rstd, rstd3_ok)
                quads(g, 2)
                if prev:
                    p_rg(g - 1)
                p_ln4(g, 0)
                p_ln4(g, 1)
                p_B3(g, nxt)

            p_rstd(ve3_ok, 1, ve, rstd, rstd3_ok)
            quads(0, 0)
            slot_B(0, False, True)
            with pool.Fori(1, LAST) as i:
                slot_B(i, True, True)
            slot_B(LAST, True, False)
            p_rg(LAST)

        @block.vector
        def _(dve):
            for buf, v in ((mhalf, -0.5), (phalf, 0.5), (ones, 1.0), (rW2_s, 0.0), (vbuf, 0.0)):
                dve.memset(buf[:], v).then_inc(setup_v, 1)
            for k, v in ((0, -0.5), (1, 0.5)):
                dve.memset(pq[:, k, :], v).then_inc(setup_v, 1)
            dve.wait_ge(setup_v, 7)
            for e in range(2):
                dve.memset(Vb[e * L:(e + 1) * L, :, :, :, e, HD:VW], 1.0).then_inc(setup_v, 1)
            dve.memset(msq[:, :], 0.0).then_inc(h3_ok, 1)

            def setup_A():
                dve.wait_ge(loaded_A, 16 * len(loads_A))
                for j in range(IMGS):
                    dve.tensor_copy(rW2_s[:, j, NH * j:NH * (j + 1)], rW2c[:, :]).then_inc(setup_v, 1)
                dve.tensor_scalar(rb2h[:, :], rb2_s[:, :], 0.5, None, ALU.mult).then_inc(setup_v, 1)
                dve.tensor_copy(selb[:, :, :], self_[:, :, :]).then_inc(setup_v, 1)

            def setup_B():
                dve.tensor_copy(identb[:, :], ident_s[:, :]).then_inc(setup_b, 1)
                dve.tensor_copy(cmaskb[:, :, :], cmask_s[:, :, :]).then_inc(setup_b, 1)
                dve.wait_ge(abs_mm, 1)
                dve.tensor_scalar(thr[:, :], PS[:, 4, 0:2], 0.5 / (E * FF), None, ALU.mult).then_inc(th_set, 1)
                dve.tensor_scalar(nthr[:, :], PS[:, 4, 0:2], -0.5 / (E * FF), None, ALU.mult).then_inc(th_set, 1)
                dve.wait_ge(th_set, 2)
                for n, (w, ternary) in enumerate(((wup_f, wup_t), (wdn_f, wdn_t))):
                    dve.tensor_scalar(spare[:, n, :], w, nthr[:, n:n + 1], None, ALU.is_lt).then_inc(th_neg, 1)
                    dve.wait_ge(th_neg, n + 1)
                    dve.scalar_tensor_tensor(out=ternary, in0=w, scalar=thr[:, n:n + 1], in1=spare[:, n, :],
                                             op0=ALU.is_gt, op1=ALU.subtract).then_inc(thr_ok, 1)

            def stats(g, st_, mv_, ve_, in_st, in_mv, in_ve, tiles=range(TILES)):
                for t in tiles:
                    dve.bn_stats(st_[:, t, :], H[:, TILES * g + t, :]).then_inc(in_st, 1)
                for t in tiles:
                    count = in_reg(dve, TILES * g + t + 1)
                    dve.wait_ge(setup_v, 1)
                    dve.wait_ge(in_st, count)
                    dve.bn_aggr(mv_[:, t, :], st_[:, t, :]).then_inc(in_mv, 1)
                dve.wait_ge(in_mv, TILES * g + tiles[-1] + 1)
                dve.tensor_scalar(ve_[:, tiles[0]:tiles[-1] + 1], mv_[:, tiles[0]:tiles[-1] + 1, 1], EPS, None, ALU.add).then_inc(in_ve, 1)

            def normalize(g, xn, mv_, scale, done, tiles=range(TILES)):
                for t in tiles:
                    dve.tensor_scalar(xn[:, t, :], H[:, TILES * g + t, :], mv_[:, t, 0:1], scale[:, t:t + 1],
                                      ALU.subtract, ALU.mult).then_inc(done, 1)

            def embed_h(g):
                for p in range(2):
                    dve.wait_ge(embed_mm, TILES * g + 2 * p + 2)
                    at = TILES * g + 2 * p
                    dve.tensor_tensor(H[:, bass.ds(at, 2), :], PS[:, 4 + p, :].rearrange("p (t n) -> p t n", t=2),
                                      tokb_s[:, :].unsqueeze(1).broadcast_to([P, 2, E]), ALU.add)\
                       .then_inc(embed_out, 1)
                count = in_reg(dve, 2 * g + 2)
                dve.wait_ge(setup_v, 1)
                dve.wait_ge(embed_out, count)
                stats(g, st, mv, ve, ve1_st, ve1_mv, ve1_ok)

            def norm1(g):
                dve.wait_ge(rstd1_ok, g + 1)
                normalize(g, xn1, mv, rstd, xn1_ok)

            def keys_in(g):
                for c in range(C):
                    dve.wait_ge(k_mm, 2 * g + c + 1)
                    for e in range(2):
                        dve.tensor_scalar(kM[:, c, e, :], PS[:, c, :], bqk_s[:, 2 + c:3 + c],
                                          par_s[:, e:e + 1], ALU.add, ALU.mult).then_inc(k_out, 1)

            def router_sigmoid(g):
                dve.wait_ge(rt1, g + 1)
                dve.tensor_scalar(sg1[:, :], t1[:, :], 0.5, 0.5, ALU.mult, ALU.add).then_inc(rsg1, 1)

            def values_to_blocks(g):
                bv3 = bv_s[:, :].rearrange("p (hp e d) -> p hp e d", e=2, d=HD)
                vp = PF[:, 0:8 * E].rearrange("p (n hp e d) -> p n hp e d", n=8, e=2, d=HD)

                def values_in(r, tiles, b, e, n0, n1):
                    n = n1 - n0
                    dve.tensor_tensor(Vb[r, tiles, :, b, e, 0:HD], vp[r, n0:n1, :, e, :],
                                      bv3[r, :, e, :].unsqueeze(1).broadcast_to([L, n, HP, HD]), ALU.add)\
                       .then_inc(v_out, 1)

                lo, hi = slice(0, L), slice(L, P)
                dve.wait_ge(v_mm, 8 * g + 4)
                values_in(lo, slice(0, 4), 0, 0, 4, 8)
                values_in(hi, slice(0, 4), 1, 1, 4, 8)
                dve.wait_ge(v_mm, 8 * g + 8)
                values_in(lo, slice(0, 4), 1, 0, 0, 4)
                values_in(hi, slice(1, 4), 0, 1, 0, 3)
                values_in(hi, slice(0, 1), 0, 1, 3, 4)

            def top_keys(g):
                dve.wait_ge(rt2, g + 1)
                dve.tensor_scalar(wk[0][:, :], t2[:, :], 0.5, 0.5, ALU.mult, ALU.add).then_inc(top_step, 1)
                for r in range(KEEP // 8):
                    count = in_reg(dve, TOP * g + 2 * r + 1)
                    dve.wait_ge(setup_v, 1)
                    dve.wait_ge(top_step, count)
                    dve.max(m8[r][:, :], wk[r % 3][:, :]).then_inc(top_step, 1)
                    count = in_reg(dve, TOP * g + 2 * r + 2)
                    dve.wait_ge(setup_v, 1)
                    dve.wait_ge(top_step, count)
                    dve.match_replace(wk[(r + 1) % 3][:, :], m8[r][:, :], wk[r % 3][:, :], TAKEN)\
                       .then_inc(top_step, 1)
                left = wk[(KEEP // 8) % 3]
                count = in_reg(dve, TOP * g + TOP - 3)
                dve.wait_ge(setup_v, 1)
                dve.wait_ge(top_step, count)
                dve.max(m8[3][:, :], left[:, :]).then_inc(top_step, 1)
                dve.wait_ge(top_step, TOP * g + TOP - 2)
                dve.scalar_tensor_tensor(out=cand[:, :], in0=left[:, :], scalar=m8[3][:, 0:1], in1=rev64_s[:, :],
                                         op0=ALU.is_equal, op1=ALU.mult).then_inc(top_step, 1)
                count = in_reg(dve, TOP * g + TOP - 1)
                dve.wait_ge(setup_v, 1)
                dve.wait_ge(top_step, count)
                dve.max(m8[4][:, :], cand[:, :]).then_inc(top_step, 1)
                dve.wait_ge(top_step, TOP * g + TOP)
                dve.tensor_scalar(selk[:, :], cand[:, :], m8[4][:, 0:1], None, ALU.is_equal)\
                   .then_inc(selk_ok, 1)
                dve.wait_ge(selk_ok, g + 1)
                dve.scalar_tensor_tensor(out=keep[:, :], in0=left[:, :], scalar=TAKEN, in1=selk[:, :],
                                         op0=ALU.is_equal, op1=ALU.add).then_inc(keep_ok, 1)
                dve.wait_ge(keep_ok, g + 1)
                if not first(g):
                    dve.wait_ge(mb_ok, g)
                dve.tensor_scalar(bias[:, :], keep[:, :], -1.0, -NEG, ALU.add, ALU.mult)\
                   .then_inc(bias_ok, 1)

            def soft(g, t):
                hb = (t % 2) * 256
                dve.wait_ge(s_mm, TILES * g + 2 * (t // 2) + 2)
                dve.tensor_reduce(mx[:, t % 2, :].rearrange("p (i h) -> p i h", i=4),
                                  PS[:, 0:4, hb:hb + 256].rearrange("p i (h k) -> p i h k", k=L), AX.X, ALU.max)\
                   .then_inc(smax, 1)
                dve.wait_ge(smax, TILES * g + t + 1)
                if not (first(g) and t < 2):
                    dve.wait_ge(pt_mm, 2 * (TILES * g + t - 1))
                dve.tensor_tensor(Pm[:, t % 2, :].rearrange("p (i h k) -> p i h k", i=4, k=L),
                                  PS[:, 0:4, hb:hb + 256].rearrange("p i (h k) -> p i h k", k=L),
                                  mx[:, t % 2, :].rearrange("p (i h) -> p i h", i=4).unsqueeze(3)
                                  .broadcast_to([P, 4, 4, L]), ALU.subtract).then_inc(p_sub, 1)

            def attend(g, t):
                dve.wait_ge(pv_mm, 2 * (TILES * g + t + 1))
                o = PF[:, PV0:PV0 + HP * 4 * VW].rearrange("p (hp b e v) -> p hp b e v", hp=HP, b=2, e=2)
                for b in range(2):
                    r = slice(b * L, (b + 1) * L)
                    dve.reciprocal(rden[r, :].rearrange("p (hp e) -> p hp e", e=2), o[r, :, b, :, HD])\
                       .then_inc(rden_ok, 1)
                for b in range(2):
                    r = slice(b * L, (b + 1) * L)
                    dve.wait_ge(rden_ok, 2 * (TILES * g + t) + b + 1)
                    dve.tensor_tensor(yn[r, :].rearrange("p (hp e d) -> p hp e d", hp=HP, e=2),
                                      o[r, :, b, :, 0:HD],
                                      rden[r, :].rearrange("p (hp e) -> p hp e", e=2).unsqueeze(3)
                                      .broadcast_to([L, HP, 2, HD]), ALU.mult).then_inc(y_out, 1)
                dve.wait_ge(y_out, 2 * (TILES * g + t + 1))
                dve.tensor_tensor(H[:, TILES * g + t, :], H[:, TILES * g + t, :], yn[:, :], ALU.add)\
                   .then_inc(h2_ok, 1)

            def stats2(g):
                count = in_reg(dve, TILES * g + TILES)
                dve.wait_ge(setup_v, 1)
                dve.wait_ge(h2_ok, count)
                stats(g, st2, mv2, ve2, ve2_st, ve2_mv, ve2_ok)

            def norm2(g):
                dve.wait_ge(rstd2_ok, g + 1)
                normalize(g, xn2, mv2, rstd2, xn2_ok)

            def v_A4(g):
                dve.wait_ge(gate_mm, g + 1)
                dve.tensor_copy(lg[:, bass.ds(TILES * g, TILES), :], PS[:, 4, 0:TILES * NX]
                                .rearrange("p (t e) -> p t e", e=NX)).then_inc(lg_ok, 1)
                for c in range(C):
                    cols = slice(c * TOK, (c + 1) * TOK)
                    dve.wait_ge(th_ok, 2 * g + c + 1)
                    dve.scalar_tensor_tensor(out=u[:, cols], in0=th[:, cols], scalar=1.0, in1=PS[:, (5, 7)[c], :],
                                             op0=ALU.add, op1=ALU.mult).then_inc(u_ok, 1)
                    dve.wait_ge(u_ok, 2 * g + c + 1)
                    dve.wait_ge(b_mm, 2 * g + c + 1)
                    dve.tensor_tensor(hs[:, cols], u[:, cols], PS[:, (6, 4)[c], :], ALU.mult)\
                       .then_inc(hs_ok, 1)

            def v_shared(g):
                for p in range(2):
                    dve.wait_ge(sh_mm, TILES * g + 2 * p + 2)
                    rows2 = H[:, bass.ds(TILES * g + 2 * p, 2), :]
                    dve.scalar_tensor_tensor(out=rows2, in0=PS[:, 5 + p, :].rearrange("p (t n) -> p t n", t=2),
                                             scalar=0.5, in1=rows2, op0=ALU.mult, op1=ALU.add)\
                       .then_inc(h3_ok, 1)

            def slot_in(g, between):
                between()
                keys_in(g)
                router_sigmoid(g)
                top_keys(g)
                values_to_blocks(g)

            dve.wait_ge(loaded_embed, 16 * len(loads_embed))
            embed_h(0)
            setup_A()
            norm1(0)
            slot_in(0, lambda: None)
            soft(0, 0)
            soft(0, 1)
            with dve.Fori(0, LAST) as i:
                attend(i, 0)
                soft(i, 2)
                attend(i, 1)
                soft(i, 3)
                embed_h(i + 1)
                norm1(i + 1)
                attend(i, 2)
                attend(i, 3)
                stats2(i)
                slot_in(i + 1, lambda: norm2(i))
                v_A4(i)
                soft(i + 1, 0)
                soft(i + 1, 1)
                v_shared(i)
            setup_B()
            for t in range(2):
                attend(LAST, t)
                soft(LAST, 2 + t)
            attend(LAST, 2)
            attend(LAST, 3)
            stats2(LAST)
            norm2(LAST)
            v_A4(LAST)
            v_shared(LAST)
            dve.wait_ge(h3_ok, 2 * SLOTS + 1)

            lg2 = lg[:, :, :].rearrange("p t e -> p (t e)")

            def each(v):
                return v[:, :].unsqueeze(2).broadcast_to([P, NT, NX])

            def experts(v):
                return v[:, :].unsqueeze(1).broadcast_to([P, NT, NX])

            dve.tensor_reduce(rsm["mx"][:, :], lg[:, :, :], AX.X, ALU.max).then_inc(routed_step, 1)
            dve.wait_ge(routed_step, after("routed"))
            dve.tensor_tensor(r3["a"], lg[:, :, :], each(rsm["mx"]), ALU.subtract).then_inc(gl_ok, 1)
            dve.wait_ge(gex_ok, 1)
            dve.tensor_reduce(rsm["sum"][:, :], r3["ex"], AX.X, ALU.add).then_inc(routed_step, 1)
            dve.wait_ge(routed_step, after("routed"))
            dve.reciprocal(rsm["inv"][:, :], rsm["sum"][:, :]).then_inc(routed_step, 1)
            dve.wait_ge(routed_step, after("routed"))
            dve.tensor_tensor(r3["pr"], r3["ex"], each(rsm["inv"]), ALU.mult).then_inc(routed_step, 1)
            dve.wait_ge(routed_step, after("routed"))
            dve.tensor_tensor(r3["s"], r3["pr"], experts(eb_s), ALU.add).then_inc(routed_step, 1)
            dve.wait_ge(routed_step, after("routed"))
            s4 = rs["s"][:, :].rearrange("p (t g x) -> p t g x", g=4, x=2)
            dve.tensor_tensor(gs[:, :, :], s4[:, :, :, 0], s4[:, :, :, 1], ALU.add).then_inc(routed_step, 1)
            dve.wait_ge(routed_step, after("routed"))
            for a in range(4):
                dve.memset(wins[:, :, a], float(a)).then_inc(routed_step, 1)
                dve.wait_ge(routed_step, after("routed"))
            for a in range(4):
                for b in range(a + 1, 4):
                    dve.tensor_tensor(cmp[:, :], gs[:, :, a], gs[:, :, b], ALU.is_ge).then_inc(routed_step, 1)
                    dve.wait_ge(routed_step, after("routed"))
                    dve.tensor_tensor(wins[:, :, a], wins[:, :, a], cmp[:, :], ALU.add).then_inc(routed_step, 1)
                    dve.wait_ge(routed_step, after("routed"))
                    dve.tensor_tensor(wins[:, :, b], wins[:, :, b], cmp[:, :], ALU.subtract).then_inc(routed_step, 1)
                    dve.wait_ge(routed_step, after("routed"))
            dve.tensor_scalar(gk[:, :, :], wins[:, :, :], 2.0, None, ALU.is_ge).then_inc(routed_step, 1)
            dve.wait_ge(routed_step, after("routed"))
            dve.tensor_scalar(gd[:, :, :], gk[:, :, :], -1.0, BIG, ALU.add, ALU.mult).then_inc(routed_step, 1)
            dve.wait_ge(routed_step, after("routed"))
            m4 = rs["m"][:, :].rearrange("p (t g x) -> p t g x", g=4, x=2)
            for xx in range(2):
                dve.tensor_tensor(m4[:, :, :, xx], s4[:, :, :, xx], gk[:, :, :], ALU.mult).then_inc(routed_step, 1)
                dve.wait_ge(routed_step, after("routed"))
                dve.tensor_tensor(m4[:, :, :, xx], m4[:, :, :, xx], gd[:, :, :], ALU.add).then_inc(routed_step, 1)
                dve.wait_ge(routed_step, after("routed"))
            for k, (src, oh, mxk, ck) in enumerate((("m", "oh1", "m1", "c1"), ("b", "oh2", "m2", "c2"))):
                dve.tensor_reduce(rsm[mxk][:, :], r3[src], AX.X, ALU.max).then_inc(routed_step, 1)
                dve.wait_ge(routed_step, after("routed"))
                dve.tensor_tensor(r3["a"], r3[src], each(rsm[mxk]), ALU.is_equal).then_inc(routed_step, 1)
                dve.wait_ge(routed_step, after("routed"))
                dve.tensor_tensor(r3["a"], r3["a"], experts(rev8_s), ALU.mult).then_inc(routed_step, 1)
                dve.wait_ge(routed_step, after("routed"))
                dve.tensor_reduce(rsm[ck][:, :], r3["a"], AX.X, ALU.max).then_inc(routed_step, 1)
                dve.wait_ge(routed_step, after("routed"))
                dve.tensor_tensor(r3[oh], r3["a"], each(rsm[ck]), ALU.is_equal).then_inc(routed_step, 1)
                dve.wait_ge(routed_step, after("routed"))
                if k == 0:
                    dve.scalar_tensor_tensor(out=rs["b"][:, :], in0=rs[oh][:, :], scalar=-BIG,
                                             in1=rs["m"][:, :], op0=ALU.mult, op1=ALU.add).then_inc(routed_step, 1)
                    dve.wait_ge(routed_step, after("routed"))
                cols = slice(k * NT, (k + 1) * NT)
                dve.tensor_scalar(ei[:, cols], rsm[ck][:, :], -1.0, float(NX), ALU.mult, ALU.add)\
                   .then_inc(routed_step, 1)
                dve.wait_ge(routed_step, after("routed"))
                dve.tensor_tensor(r3["a"], r3[oh], r3["pr"], ALU.mult).then_inc(routed_step, 1)
                dve.wait_ge(routed_step, after("routed"))
                dve.tensor_reduce(wt[:, cols], r3["a"], AX.X, ALU.add).then_inc(routed_step, 1)
                dve.wait_ge(routed_step, after("routed"))
            dve.tensor_tensor(rs["a"][:, :], rs["oh1"][:, :], rs["oh2"][:, :], ALU.add).then_inc(routed_step, 1)
            dve.wait_ge(routed_step, after("routed"))
            dve.tensor_reduce(cnt[:, :], rs["a"][:, :].rearrange("p (t e) -> p e t", e=NX), AX.X, ALU.add)\
               .then_inc(cnt_ok, 1)
            dve.wait_ge(cnt_mm, 1)
            dve.tensor_copy(off[:, :], PS[:, 4, 0:NX]).then_inc(routed_step, 1)
            dve.wait_ge(routed_step, after("routed"))
            for e in range(1, NX):
                dve.tensor_tensor(off[:, e:e + 1], off[:, e:e + 1], off[:, e - 1:e], ALU.add).then_inc(routed_step, 1)
                dve.wait_ge(routed_step, after("routed"))
            dve.tensor_scalar(gg[:, :], ridx_s[:, :], off[:, 0:1], None, ALU.is_ge).then_inc(routed_step, 1)
            dve.wait_ge(routed_step, after("routed"))
            for e in range(1, NX - 1):
                dve.scalar_tensor_tensor(out=gg[:, :], in0=ridx_s[:, :], scalar=off[:, e:e + 1],
                                         in1=gg[:, :], op0=ALU.is_ge, op1=ALU.add).then_inc(routed_step, 1)
                dve.wait_ge(routed_step, after("routed"))
            dve.scalar_tensor_tensor(out=code[:, :], in0=gg[:, :], scalar=float(NX), in1=ei[:, :],
                                     op0=ALU.mult, op1=ALU.add).then_inc(routed_step, 1)
            dve.wait_ge(routed_step, after("routed"))
            dve.memset(racc[:, :], 0.0).then_inc(racc_ok, 1)

            def quad_ow(q, b):
                for n in range(4):
                    at = 4 * q + n
                    dve.tensor_scalar(ow[:, b, n, :], iota_s[:, :], code[:, bass.ds(at, 1)],
                                      wt[:, bass.ds(at, 1)], ALU.is_equal, ALU.mult).then_inc(ow_ok, 1)

            with dve.Fori(0, QUADS // 2) as i:
                for b in range(2):
                    quad_ow(2 * i + b, b)
                for b in range(2):
                    dve.wait_ge(tz_ok, 2 * i + b + 1)
                    dve.scalar_tensor_tensor(out=sz[:, b, :], in0=tz[:, b, :], scalar=1.0, in1=PS[:, 2 + b, :],
                                             op0=ALU.add, op1=ALU.mult).then_inc(sz_ok, 1)
                for b in range(2):
                    dve.wait_ge(acc_mm, 2 * i + b + 1)
                    dve.wait_ge(racc_ok, 2 * i + b + 1)
                    dve.tensor_tensor(racc[:, :], racc[:, :], PS[0:64, 4 + b, 0:HID], ALU.add)\
                       .then_inc(racc_ok, 1)
            dve.wait_ge(racc_ok, QUADS + 1)
            dve.wait_ge(tab_ok, 2)
            dve.scalar_tensor_tensor(out=gm[:, :], in0=racc[:, :], scalar=0.5, in1=tabC[:, :], op0=ALU.mult,
                                     op1=ALU.mult).then_inc(gm_ok, 1)
            dve.wait_ge(r8_mm, 1)
            dve.tensor_tensor(H[0:NX, TILES * LAST, :], H[0:NX, TILES * LAST, :], PS[0:NX, 7, 0:E], ALU.add)\
               .then_inc(r8_ok, 1)
            dve.wait_ge(r8_ok, 1)

            def norm3(g):
                dve.wait_ge(rstd3_ok, g + 1)
                normalize(g, xn1, mv, rstd, xn3_ok)

            def v_B1(g):
                for c in range(C):
                    dve.wait_ge(Bq_mm, 2 * g + c + 1)
                    for e in range(2):
                        dve.tensor_scalar(qM[:, c, e, :], PS[:, 4 + c, :], par_s[:, 2 + e:3 + e], None, ALU.mult)\
                           .then_inc(Bq_out, 1)

            def v_x3T(g):
                dve.wait_ge(x3T_mm, 2 * g + 2)
                dve.tensor_copy(xT1[:, 1, 0:TOK], PS[:, 5, :]).then_inc(x3T_v, 1)

            def v_quads(g, t):
                dve.wait_ge(relu_ok, TILES * g + t + 1)
                v = relu_s[t % 2][:, :]
                dve.tensor_tensor(v, v, v, ALU.mult).then_inc(quad_odd, 1)

            def poly(g, t):
                hb = (t % 2) * 256
                dve.wait_ge(lin_ok, TILES * g + 2 * (t // 2) + 2)
                dve.wait_ge((quad_even, quad_odd)[t % 2], 2 * g + t // 2 + 1)
                dve.scalar_tensor_tensor(out=lin[t % 2][:, :], in0=lin[t % 2][:, :], scalar=1.0,
                                         in1=relu_s[t % 2][:, :], op0=ALU.add,
                                         op1=ALU.add).then_inc(f0_ok, 1)
                dve.wait_ge(f0_ok, TILES * g + t + 1)
                if not (first(g) and t < 2):
                    dve.wait_ge(Y_mm, TILES * g + t - 1)
                Fv = F[:, t % 2, :].rearrange("p (i n) -> p i n", i=4)
                dve.scalar_tensor_tensor(out=Fv, in0=PS[:, 0:4, hb:hb + 256], scalar=-100.0,
                                         in1=lin[t % 2][:, :].rearrange("p (i n) -> p i n", i=4), op0=ALU.is_ge,
                                         op1=ALU.mult).then_inc(f2_ok, 1)

            def turned(g, pair, bank):
                dve.wait_ge(yT_mm, TILES * g + 2 * pair + 2)
                for t in (2 * pair, 2 * pair + 1):
                    m = dve.tensor_copy(xT2[:, :, t * P:(t + 1) * P].rearrange("p e (b q) -> p e b q", b=2),
                                        PS[:, bank, (t % 2) * E:(t % 2 + 1) * E]
                                        .rearrange("p (b e q) -> p e b q", b=2, e=2))
                m.then_inc(yT_out, 1)

            def projected(g, pair, bank):
                dve.wait_ge(pr_mm, 2 * g + pair + 1)
                rows2 = H[:, bass.ds(TILES * g + 2 * pair, 2), :]
                dve.tensor_tensor(rows2, rows2, PS[:, bank, :].rearrange("p (t n) -> p t n", t=2), ALU.add)\
                   .then_inc(h4_ok, 1)

            def norm4(g, pair):
                tiles = range(2 * pair, 2 * pair + 2)
                ts = slice(2 * pair, 2 * pair + 2)
                count = in_reg(dve, 2 * g + pair + 1)
                dve.wait_ge(setup_v, 1)
                dve.wait_ge(h4_ok, count)
                stats(g, st2, mv2, vr[:, 0, :], ve4_st, ve4_mv, ve4_ok, tiles)
                dve.tensor_copy(vr[:, 1, ts], mv2[:, ts, 1]).then_inc(ve4_ok, 1)
                dve.wait_ge(rstd4_ok, 2 * g + pair + 1)
                n = 8 * g + 4 * pair
                dve.tensor_tensor(rr[:, ts], rq[:, 1, ts], rq[:, 0, ts], ALU.mult).then_inc(r4_step, 1)
                dve.wait_ge(r4_step, n + 1)
                dve.tensor_scalar(rr[:, ts], rr[:, ts], 1e-8, None, ALU.add).then_inc(r4_step, 1)
                dve.wait_ge(r4_step, n + 2)
                dve.reciprocal(rr[:, ts], rr[:, ts]).then_inc(r4_step, 1)
                dve.wait_ge(r4_step, n + 3)
                dve.tensor_tensor(r4[:, ts], rr[:, ts], rq[:, 0, ts], ALU.mult).then_inc(r4_step, 1)
                dve.wait_ge(r4_step, n + 4)
                normalize(g, xn2, mv2, r4, xn4_ok, tiles)

            def v_x4T(g):
                for c in range(C):
                    dve.wait_ge(x4T_a, 2 * g + c + 1)
                    dve.tensor_tensor(x4_lo[:, c, :], PS[:, 6 + c, :], x4_hi[:, c, :], ALU.subtract)\
                       .then_inc(x4T_v, 1)

            def g_parts(g, f0, f1):
                for f in range(f0, f1):
                    dve.wait_ge(g_ok, NF * g + f + 1)
                    dve.tensor_copy(G_hi[:, f, :], g32[:, f % 4, :]).then_inc(gh_out, 1)
                    dve.wait_ge(gh_out, NF * g + f + 1)
                    dve.tensor_tensor(G_lo[:, f, :], g32[:, f % 4, :], G_hi[:, f, :], ALU.subtract)\
                       .then_inc(gl_out, 1)

            def mean_squares(g):
                dve.wait_ge(ss_mm, g + 1)
                dve.tensor_scalar(msq[:, :], PS[:, 7, 0:TILES], 1.0 / FF, None, ALU.mult).then_inc(msq_ok, 1)

            def one_over_rms(g):
                dve.wait_ge(rg_ok, g + 1)
                dve.tensor_scalar(rge[:, :], rg[:, :], 1e-8, None, ALU.add).then_inc(rg_step, 1)
                dve.wait_ge(rg_step, 2 * g + 1)
                dve.reciprocal(rgi[:, :], rge[:, :]).then_inc(rg_step, 1)

            def ffn_out(g):
                dve.wait_ge(rg_step, 2 * g + 2)
                for t in range(TILES):
                    dve.wait_ge(dn_mm, TILES * g + 2 * (t // 2) + 2)
                    at = TILES * g + t
                    dve.scalar_tensor_tensor(out=H[:, at, :], in0=PS[:, 6 + t // 2, (t % 2) * E:(t % 2 + 1) * E],
                                             scalar=rgi[:, t:t + 1], in1=H[:, at, :], op0=ALU.mult, op1=ALU.add)\
                       .then_inc(h5_ok, 1)

            def stats3(g):
                stats(g, st, mv, ve, ve3_st, ve3_mv, ve3_ok)

            def slot_B(g, prev, nxt):
                if nxt:
                    stats3(g + 1)
                    norm3(g + 1)
                v_quads(g, 3)
                if prev:
                    mean_squares(g - 1)
                turned(g, 0, 6)
                if nxt:
                    v_x3T(g + 1)
                poly(g, 2)
                projected(g, 0, 7)
                if prev:
                    one_over_rms(g - 1)
                poly(g, 3)
                norm4(g, 0)
                if prev:
                    ffn_out(g - 1)
                if nxt:
                    v_B1(g + 1)
                turned(g, 1, 6)
                projected(g, 1, 4)
                norm4(g, 1)
                v_x4T(g)
                if nxt:
                    v_quads(g + 1, 1)
                g_parts(g, 0, 1)
                if nxt:
                    poly(g + 1, 0)
                    poly(g + 1, 1)
                g_parts(g, 1, NF)

            dve.memset(vbuf[:], 0.0).then_inc(V2_zero, 1)
            stats3(0)
            norm3(0)
            v_x3T(0)
            v_B1(0)
            v_quads(0, 1)
            poly(0, 0)
            poly(0, 1)
            slot_B(0, False, True)
            with dve.Fori(1, LAST) as i:
                slot_B(i, True, True)
            slot_B(LAST, True, False)
            mean_squares(LAST)
            one_over_rms(LAST)
            ffn_out(LAST)


def _layout(inputs):
    a = {k: np.asarray(v) for k, v in inputs.items()}

    def chunks(w):
        return w.reshape(-1, P, w.shape[1]).transpose(1, 0, 2)

    def rows(v):
        return np.broadcast_to(v[None, :], (P, v.shape[0]))

    x = a["x"].reshape(SLOTS, IMGS, 3, 8, 16, 8, 16).transpose(0, 2, 4, 6, 1, 3, 5).reshape(SLOTS, KP, P, TOK)
    x = np.roll(x, -1, axis=0).transpose(0, 2, 1, 3)
    order = np.concatenate([np.arange(HD) + HD * (4 * i + 2 * c + e)
                            for c in range(C) for i in range(4) for e in range(2)])
    qkv = a["L0_attn_qkv_w"].T
    qkv = np.concatenate([qkv[:, order], qkv[:, E + order], qkv[:, 2 * E:]], axis=1)
    qb = a["L0_attn_qkv_b"]
    bqk = np.stack([qb[order][:P], qb[order][P:], qb[E + order][:P], qb[E + order][P:]], axis=1)
    wat = a["L1_attn_W_attn"]
    wat = np.concatenate([wat[:, order], wat[:, E + order], wat[:, 2 * E:]], axis=1)
    wpr = a["L1_attn_W_proj"].reshape(HP, 2, HD, E).transpose(0, 2, 1, 3).reshape(P, 2, E)

    def hid(w):
        return w.reshape(NX, C, P, HID).transpose(2, 0, 1, 3)

    ident = np.eye(P)
    f = np.arange(P)
    even = ((f // HD) % 2 == 0).astype(np.float32)
    par = np.stack([even, 1 - even, HD ** -0.5 * even, HD ** -0.5 * (1 - even)], axis=1)
    sel = (f[:, None, None] // NH == 2 * np.arange(TILES)[None, :, None] + f[None, None, :] // L)
    delta = f[:, None] % NH == np.arange(NH)[None, :]
    rev64 = rows(np.arange(L, 0, -1))
    cm = np.where(f[:, None] % L > np.arange(L)[None, :], NEG, 0.0)
    cmask = np.broadcast_to(cm[:, None, :], (P, 4, L))
    slot = np.arange(SLOTS * TILES)
    tile0 = ((slot // TILES + 1) % SLOTS) * TILES + slot % TILES
    token = tile0[None, :] * P + f[:, None]
    ridx = np.concatenate([2 * token, 2 * token + 1], axis=1)
    maps = dict(
        x=x, tokW=chunks(a["L0_tok_W"]), tokb=rows(a["L0_tok_b"]), wqkv=chunks(qkv), bqk=bqk, bv=rows(qb[2 * E:]),
        rW1=chunks(a["L0_attn_r_w1"].T), rb1=a["L0_attn_r_b1"][:, None], rW2=a["L0_attn_r_w2"].T,
        rb2=np.tile(a["L0_attn_r_b2"], IMGS)[:, None], gateW=chunks(a["L0_ffn_w_gate"].T),
        eb=rows(a["L0_ffn_expert_bias"]), w1=hid(a["L0_ffn_w1"]), w3=hid(a["L0_ffn_w3"]),
        w2=a["L0_ffn_w2"].transpose(1, 0, 2), s1=chunks(a["L0_ffn_sw1"].T), s3=chunks(a["L0_ffn_sw3"].T),
        s2=chunks(a["L0_ffn_sw2"].T), wat=chunks(wat), wpr=wpr, wup=chunks(a["L1_ffn_w_up"].T),
        wdn=chunks(a["L1_ffn_w_down"].T), ident=ident, par=par, sel=sel, delta=delta, rev64=rev64, cmask=cmask,
        ridx=ridx, iota64=rows(np.arange(64)), rev8=rows(np.arange(NX, 0, -1)))
    consts = ("ident", "par", "sel", "delta", "rev64", "cmask", "ridx", "iota64", "rev8")
    return {k: np.ascontiguousarray(v.astype(np.float32) if k in consts else v) for k, v in maps.items()}


def kernel(**inputs):
    import concourse.bacc as _bacc
    from concourse.bass_utils import run_bass_kernel_spmd as _run

    nc = _bacc.Bacc("TRN2", target_bir_lowering=False, num_devices=1)
    arrays = _layout(inputs)
    args = {n: nc.dram_tensor("in_" + n, v.shape, F32, kind="ExternalInput").ap() for n, v in arrays.items()}
    out = nc.dram_tensor("out_0", (SLOTS, P, TILES, E), F32, kind="ExternalOutput").ap()
    build(nc, out=out, **args)
    r = _run(nc, [{"in_" + n: v for n, v in arrays.items()}], core_ids=[0])
    got = np.roll(np.asarray(r.results[0]["out_0"]), 1, axis=0)
    return np.ascontiguousarray(got.transpose(0, 2, 1, 3)).reshape(SLOTS * IMGS, L, E)
```

```python
from contextlib import ExitStack

import numpy as np

import concourse.bass as bass
from concourse import mybir

ALU = mybir.AluOpType
ACT = mybir.ActivationFunctionType
AX = mybir.AxisListType
F32 = mybir.dt.float32
BF16 = mybir.dt.bfloat16
F16 = mybir.dt.float16

P = 128
SLOTS = 8
IMGS = 8
L = 64
TILES = 4
TOK = IMGS * L
E = 256
C = E // P
NH = 16
HD = E // NH
HP = NH // 2
KEEP = int(L * 0.4)
KP = 6
NX = 8
HID = 128
FF = 1024
NF = FF // P
NEG = -1e30
EPS = 1e-5
VW = HD + 1
BIG = 3e38
WS = 1024.0
HS = 32.0
PV0 = 7 * 512 - 4 * 4 * VW
SETUP_V = 9 + IMGS + 4
TOP = 2 * (KEEP // 8) + 4
TAKEN = -4.0


def build(nc, x, tokW, tokb, wqkv, bqk, bv, rW1, rb1, rW2, rb2, gateW, eb, w1, w3, w2, s1, s3, s2,
          wat, wpr, wup, wdn, ident, par, sel, delta, rev64, cmask, ridx, iota64, rev8, out):
    with ExitStack() as ctx:
        def sb(name, shape, dt=F32):
            return ctx.enter_context(nc.sbuf_tensor(name, shape, dt))

        def sem(name):
            return ctx.enter_context(nc.semaphore(name))

        PS = ctx.enter_context(nc.psum_tensor("PS", [P, 8, 512], F32))
        PF = PS[:, :, :].rearrange("p b n -> p (b n)")

        def split_weights(name, *dims):
            return sb(name, [P, 2, *dims], F16)

        tokW_h = split_weights("tokW_h", KP, E); tokb_s = sb("tokb_s", [P, E])
        wqkv_h = split_weights("wqkv_h", C, 3 * E); bqk_s = sb("bqk_s", [P, 4]); bv_s = sb("bv_s", [P, E])
        rW1_h = split_weights("rW1_h", C, 64); rb1_s = sb("rb1_s", [64, 1])
        rW2_s = sb("rW2_s", [64, IMGS, P]); rW2c = sb("rW2c", [64, NH])
        rb2_s = sb("rb2_s", [P, 1]); rb2h = sb("rb2h", [P, 1])
        gateW_h = split_weights("gateW_h", C, NX); eb_s = sb("eb_s", [P, NX])
        s1_h = split_weights("s1_h", C, E); s3_h = split_weights("s3_h", C, E)
        w1_s = sb("w1_s", [P, NX, C, HID]); w3_s = sb("w3_s", [P, NX, C, HID]); w2_s = sb("w2_s", [P, NX, E])
        wat_h = split_weights("wat_h", C, 3 * E); wpr_s = sb("wpr_s", [P, C, E])
        wup_s = sb("wup_s", [P, C, FF]); wdn_s = sb("wdn_s", [P, NF, E])
        ident_s = sb("ident_s", [P, P]); identb = sb("identb", [P, P], BF16); identh = sb("identh", [P, P], F16)
        par_s = sb("par_s", [P, 4])
        late = sb("late", [P, NH * L])
        self_ = late[:, 0:TILES * P].rearrange("p (t m) -> p t m", t=TILES)
        s2_h = late[:, TILES * P:TILES * P + C * E].bitcast(F16).rearrange("p (k c n) -> p k c n", k=2, c=C)
        selb = sb("selb", [P, TILES, P], BF16)
        delta_s = sb("delta_s", [P, NH]); rev64_s = sb("rev64_s", [P, L])
        cmask_s = sb("cmask_s", [P, 4, L]); cmaskb = sb("cmaskb", [P, 4, L], BF16)
        ridx_s = sb("ridx_s", [P, 64]); iota_s = sb("iota_s", [P, 64]); rev8_s = sb("rev8_s", [P, NX])
        ones = sb("ones", [P, P]); mhalf = sb("mhalf", [P, 4]); phalf = sb("phalf", [P, 4])

        H = sb("H", [P, SLOTS * TILES, E])
        work = sb("work", [P, NF, TOK])
        patch = work[:, 0:KP, :]
        st = sb("st", [P, TILES, 6]); mv = sb("mv", [P, TILES, 2])
        st2 = sb("st2", [P, TILES, 6]); mv2 = sb("mv2", [P, TILES, 2])
        ve = sb("ve", [P, TILES]); rstd = sb("rstd", [P, TILES])
        ve2 = sb("ve2", [P, TILES]); rstd2 = sb("rstd2", [P, TILES])
        xn1 = sb("xn1", [P, TILES, E]); xn2 = sb("xn2", [P, TILES, E])
        xT1 = sb("xT1", [P, C, TOK + L]); xT2 = sb("xT2", [P, C, TOK])
        qT = sb("qT", [P, C, TOK]); kM = sb("kM", [P, C, 2, TOK])
        vbuf = sb("vbuf", [P, TILES * HP * 2 * 2 * VW])
        Vb = vbuf[:, :].rearrange("p (t hp b e v) -> p t hp b e v", t=TILES, hp=HP, b=2, e=2)
        V2 = vbuf[:, 0:TILES * NH * 2 * HD].rearrange("p (t h b d) -> p t h b d", t=TILES, h=NH, b=2)
        h1T = sb("h1T", [64, TOK])
        t1 = sb("t1", [P, L]); sg1 = sb("sg1", [P, L]); t2 = sb("t2", [P, L]); sg2 = sb("sg2", [P, L])
        wk = [sb(f"wk{i}", [P, L]) for i in range(3)]
        m8 = [sb(f"m8_{i}", [P, 8]) for i in range(5)]
        cand = sb("cand", [P, L]); selk = sb("selk", [P, L]); keep = sb("keep", [P, L]); bias = sb("bias", [P, L])
        mb = sb("mb", [P, NH, L], BF16)
        mx = sb("mx", [P, 2, NH])
        Pm = sb("Pm", [P, 2, NH * L]); PT = sb("PT", [P, 2, HP, P])
        rden = sb("rden", [P, NH]); yn = sb("yn", [P, E])
        th = sb("th", [P, C * TOK]); u = sb("u", [P, C * TOK]); hs = sb("hs", [P, C * TOK])
        sabs = sb("sabs", [P, 2]); thr = sb("thr", [P, 2]); nthr = sb("nthr", [P, 2])
        vr = sb("vr", [P, 2, TILES]); rq = sb("rq", [P, 2, TILES]); pq = sb("pq", [P, 2, TILES])
        rr = sb("rr", [P, TILES]); r4 = sb("r4", [P, TILES])
        msq = sb("msq", [P, TILES]); rg = sb("rg", [P, TILES])
        rge = sb("rge", [P, TILES]); rgi = sb("rgi", [P, TILES])
        lg = sb("lg", [P, SLOTS * TILES, NX])


        NT = SLOTS * TILES
        CH = 2 * NT
        RB = CH // 4
        flat = wup_s[:, :, :].rearrange("p c n -> p (c n)")
        rs = {n: flat[:, k * NT * NX:(k + 1) * NT * NX]
              for k, n in enumerate(("ex", "pr", "s", "m", "a", "b", "oh1", "oh2"))}
        r3 = {n: v[:, :].rearrange("p (t e) -> p t e", e=NX) for n, v in rs.items()}
        rsm = {n: sb("rv_" + n, [P, NT]) for n in ("mx", "sum", "inv", "m1", "c1", "m2", "c2")}
        gs, wins, gk, gd = (wdn_s[:, :, :].rearrange("p f n -> p (f n)")[:, k * NT * 4:(k + 1) * NT * 4]
                            .rearrange("p (t g) -> p t g", g=4) for k in range(4))
        cmp = sb("cmp", [P, NT])
        wt = sb("wt", [P, CH]); ei = sb("ei", [P, 2 * NT]); gg = sb("gg", [P, 2 * NT])
        code = sb("code", [P, CH + RB])
        cnt = sb("cnt", [P, NX]); off = sb("off", [P, NX])
        AC = [sb("AT", [P, 64]), sb("CT", [P, 64])]
        tabA = sb("tabA", [64, 2, HID], F16); tabC = sb("tabC", [64, HID])
        one_hot = s1_h[:, :, :, :].rearrange("p k c n -> p (k c n)").rearrange("p (k e) -> p k e", k=RB)
        one_hot_prev = s3_h[:, :, :, :].rearrange("p k c n -> p (k c n)").rearrange("p (k e) -> p k e", k=RB)
        one_hot_T = w1_s[0:64, :, :, :].rearrange("p e c h -> p (e c h)")[:, NH * L:2 * NH * L].bitcast(F16)
        wz = wup_s[:, :, :].rearrange("p c n -> p (c n)")
        tz = wdn_s[:, :, :].rearrange("p f n -> p (f n)")
        halves = tz.bitcast(F16)
        silu_hi, silu_lo = (halves[:, k * RB * HID:(k + 1) * RB * HID].rearrange("p (k n) -> p k n", k=RB)
                            for k in range(2))
        PH = PS[:, 0:2, :].rearrange("p b n -> p (b n)").bitcast(F16)
        racc = sb("racc", [64, HID]); gm = sb("gm", [64, HID]); gT = sb("gT", [P, 64])
        UP_BANKS = (4, 6, 7, 5)

        spare = work[:, 0:NF, :].rearrange("p (n k) t -> p n (k t)", n=2)
        wup_f = wup_s[:, :, :].rearrange("p c n -> p (c n)")
        wdn_f = wdn_s[:, :, :].rearrange("p f n -> p (f n)")
        half_q = wqkv_h[:, :, :, :].rearrange("p h c n -> p (h c n)")[:, 0:C * FF]
        half_t = tokW_h[:, :, :, :].rearrange("p h k n -> p (h k n)")[:, 0:NF * E]
        wup_t, wdn_t = half_q, half_t
        wup_h = half_q.rearrange("p (c n) -> p c n", c=C)
        wdn_h = half_t.rearrange("p (f n) -> p f n", f=NF)

        w2_f = w2_s[:, :, :].rearrange("p e n -> p (e n)")
        raw, splits, at = [], [], 0
        for area, group in ((w2_f, ((tokW_h, tokW),)), (wup_f, ((wqkv_h, wqkv),)),
                            (wdn_f, ((s1_h, s1), (s3_h, s3), (s2_h, s2), (rW1_h, rW1), (gateW_h, gateW))),
                            (w2_f, ((wat_h, wat),))):
            at = 0
            for dst, src in group:
                n = src.shape[1] * src.shape[2]
                raw.append((area[:, at:at + n].rearrange("p (c n) -> p c n", c=src.shape[1]), src))
                splits.append((raw[-1][0], dst[:, 0, :, :], dst[:, 1, :, :]))
                at += n
        p_hi, p_lo = (w[:, :, :, :].rearrange("p e c h -> p (e c h)")[:, 0:KP * TOK // 2].bitcast(F16)
                      .rearrange("p (k n) -> p k n", k=KP) for w in (w1_s, w3_s))
        x1b = xT1[:, :, :].bitcast(F16)
        x1_hi, x1_lo = x1b[:, :, 0:TOK + L], x1b[:, :, TOK + L:2 * (TOK + L)]
        thb = th[:, :].bitcast(F16).rearrange("p (c k n) -> p c k n", c=C, k=2)
        hs_hi, hs_lo = thb[:, :, 0, :], thb[:, :, 1, :]
        x8 = sb("x8", [P, C, NX])

        kT = qT
        qM = kM
        F = Pm
        relu_s = (th, hs)
        lin = (u, late)
        sqt = (PT[:, 0, 0:4, :], PT[:, 0, 4:8, :])
        sqa = PT[:, 1, 0:4, :]
        Gb = work[:, :, :].bitcast(F16)
        G_hi, G_lo = Gb[:, :, 0:TOK], Gb[:, :, TOK:2 * TOK]
        x4b = xT2[:, :, :].bitcast(F16)
        x4_hi, x4_lo = x4b[:, :, 0:TOK], x4b[:, :, TOK:2 * TOK]
        g_areas = (w3_s[:, :, :, :].rearrange("p e c h -> p (e c h)"),
                   w1_s[:, :, :, :].rearrange("p e c h -> p (e c h)")[:, 0:2 * TOK],
                   wqkv_h[:, :, :, :].rearrange("p h c n -> p (h c n)")[:, C * FF:C * FF + 2 * TOK].bitcast(F32),
                   tokW_h[:, :, :, :].rearrange("p h k n -> p (h k n)")[:, NF * E:NF * E + 2 * TOK].bitcast(F32))
        g32 = [area[:, k * TOK:(k + 1) * TOK] for area in g_areas for k in range(area.shape[1] // TOK)]

        def sems(names):
            return (sem(n) for n in names.split())

        a_mm, abs_mm, abs_ok, acc_mm, b_mm, bias_ok, Bk_mm = sems("a_mm abs_mm abs_ok acc_mm b_mm bias_ok Bk_mm")
        Bk_out, Bq_mm, Bq_out, Bs_mm, Bv_mm, Bv_out = sems("Bk_out Bq_mm Bq_out Bs_mm Bv_mm Bv_out")
        cnt_mm, cnt_ok, dn_mm, embed_mm, embed_out, f0_ok = sems("cnt_mm cnt_ok dn_mm embed_mm embed_out f0_ok")
        f2_ok, g_ok, gate_mm, gex_ok, gh_out, gl_ok = sems("f2_ok g_ok gate_mm gex_ok gh_out gl_ok")
        gl_out, gm_ok, gT_mm, gT_ok, h1_mm, h1_out, h2_ok = sems("gl_out gm_ok gT_mm gT_ok h1_mm h1_out h2_ok")
        h3_ok, h4_ok, h5_ok, high_w, hs_ok, hs_split, k_mm = sems("h3_ok h4_ok h5_ok high_w hs_ok hs_split k_mm")
        k_out, keep_ok, lg_ok, lin_ok, loaded_A, loaded_B = sems("k_out keep_ok lg_ok lin_ok loaded_A loaded_B")
        loaded_embed, loaded_experts, loaded_wat, low_w = sems("loaded_embed loaded_experts loaded_wat low_w")
        mb_ok, msq_ok, oh_ok, oh_prev_ok, ohT_mm, ohT_ok = sems("mb_ok msq_ok oh_ok oh_prev_ok ohT_mm ohT_ok")
        p_exp, p_hi_ok, p_lo_ok, p_sub, patch_in, pr_mm = sems("p_exp p_hi_ok p_lo_ok p_sub patch_in pr_mm")
        pt_mm, pt_out, pv_mm, q_mm, q_out, quad_even = sems("pt_mm pt_out pv_mm q_mm q_out quad_even")
        quad_odd, r4_step, r8_mm, r8_ok, racc_ok, rden_ok = sems("quad_odd r4_step r8_mm r8_ok racc_ok rden_ok")
        relu_ok, rg_ok, rg_step, rl_mm, routed_step = sems("relu_ok rg_ok rg_step rl_mm routed_step")
        routed_zero, rsg1, rstd1_ok, rstd2_ok, rstd3_ok = sems("routed_zero rsg1 rstd1_ok rstd2_ok rstd3_ok")
        rstd4_ok, rt1, rt2, s_mm, selk_ok, setup_b = sems("rstd4_ok rt1 rt2 s_mm selk_ok setup_b")
        setup_v, sh_mm, silu_hi_ok, silu_lo_ok, silu_ok = sems("setup_v sh_mm silu_hi_ok silu_lo_ok silu_ok")
        silu_step, smax, sq_ok, sqa_ok, ss_mm, stored = sems("silu_step smax sq_ok sqa_ok ss_mm stored")
        tab_lo_ok, tab_mm, tab_ok, tab_t, tabT_ok, th_neg = sems("tab_lo_ok tab_mm tab_ok tab_t tabT_ok th_neg")
        th_ok, th_set, thr_ok, top_step, tz_ok, u_ok = sems("th_ok th_set thr_ok top_step tz_ok u_ok")
        up_mm, V2_zero, v_mm, v_out, ve1_mv, ve1_ok = sems("up_mm V2_zero v_mm v_out ve1_mv ve1_ok")
        ve1_st, ve2_mv, ve2_ok, ve2_st, ve3_mv, ve3_ok = sems("ve1_st ve2_mv ve2_ok ve2_st ve3_mv ve3_ok")
        ve3_st, ve4_mv, ve4_ok, ve4_st, wz_ok, x3T_a = sems("ve3_st ve4_mv ve4_ok ve4_st wz_ok x3T_a")
        x3T_mm, x3T_v, x4T_a, x4T_mm, x4T_v, x8_ok, xn1_ok = sems("x3T_mm x3T_v x4T_a x4T_mm x4T_v x8_ok xn1_ok")
        xn2_ok, xn3_ok, xn4_ok, xT1_a, xT1_mm, xT1_v = sems("xn2_ok xn3_ok xn4_ok xT1_a xT1_mm xT1_v")
        xT1_w, xT2_a, xT2_mm, xT2_v, Y_mm, y_out, Y_out = sems("xT1_w xT2_a xT2_mm xT2_v Y_mm y_out Y_out")
        yT_mm, yT_out, z_mm = sems("yT_mm yT_out z_mm")

        def first(g):
            return isinstance(g, int) and g == 0

        def in_reg(eng, value):
            return value if isinstance(value, int) else eng.to_reg(value)

        steps = {}

        def after(chain, n=1):
            steps[chain] = steps.get(chain, 0) + n
            return steps[chain]

        loads_embed = [raw[0], (ident_s, ident), (tokb_s, tokb)]
        loads_A = [raw[1], (bqk_s, bqk), (par_s, par), (rb1_s, rb1), (rW2c, rW2), (rb2_s, rb2),
                   (rev64_s, rev64), (bv_s, bv), (delta_s, delta), (self_, sel)] + raw[2:7]
        loads_wat = raw[7:]
        loads_B = [(cmask_s, cmask), (eb_s, eb), (rev8_s, rev8), (ridx_s, ridx), (iota_s, iota64), (wpr_s, wpr),
                   (wup_s, wup), (wdn_s, wdn), (w2_s, w2)]
        loads_experts = [(w1_s, w1), (w3_s, w3)]
        LAST = SLOTS - 1
        block = ctx.enter_context(nc.Block())

        @block.sync
        def _(sp):
            def load_patches(g):
                sp.dma_start(patch, x[g, :, :, :]).then_inc(patch_in, 16)

            load_patches(0)
            for dst, src in loads_embed:
                sp.dma_start(dst[:], src).then_inc(loaded_embed, 16)
            for dst, src in loads_A:
                sp.dma_start(dst[:], src).then_inc(loaded_A, 16)
            sp.wait_ge(low_w, 1)
            for dst, src in loads_wat:
                sp.dma_start(dst[:], src).then_inc(loaded_wat, 16)
            sp.wait_ge(p_lo_ok, 2)
            load_patches(1)
            sp.wait_ge(low_w, len(splits))
            for dst, src in loads_B:
                sp.dma_start(dst[:], src).then_inc(loaded_B, 16)
            with sp.Fori(1, LAST) as i:
                sp.wait_ge(p_lo_ok, 2 * i + 2)
                load_patches(i + 1)
            sp.wait_ge(embed_mm, TILES * SLOTS)
            for dst, src in loads_experts:
                sp.dma_start(dst[:], src).then_inc(loaded_experts, 16)
            with sp.Fori(0, SLOTS) as i:
                sp.wait_ge(h5_ok, TILES * i + TILES)
                sp.dma_start(out[i, :, :, :], H[:, bass.ds(TILES * i, TILES), :]).then_inc(stored, 16)
            sp.wait_ge(stored, 16 * SLOTS)

        @block.tensor
        def _(pe):
            PASSES = ((0, 0), (1, 0), (0, 1))

            def rows_product(dst, halves_, rows, w, cols, chunks):
                for n, ((wi, xi), k) in enumerate((pa, k) for pa in PASSES for k in range(chunks)):
                    m = pe.matmul(dst, halves_[xi][:, k, rows], w[:, wi, k, cols],
                                  start=(n == 0), stop=(n == 3 * chunks - 1))
                return m

            def embed(g, tiles=range(TILES)):
                if 0 in tiles:
                    pe.wait_ge(p_hi_ok, 2 * g + 2)
                    pe.wait_ge(p_lo_ok, 2 * g + 2)
                for t in tiles:
                    rows_product(PS[:, 4 + t // 2, (t % 2) * E:(t % 2 + 1) * E], (p_hi, p_lo),
                                 slice(t * P, (t + 1) * P), tokW_h, slice(0, E), KP).then_inc(embed_mm, 1)

            def transpose_chunk(g, c, xn, bank, ready, done):
                for t in range(TILES):
                    if c == 0:
                        pe.wait_ge(ready, TILES * g + t + 1)
                    m = pe.transpose(PS[:, bank, t * P:(t + 1) * P], xn[:, t, c * P:(c + 1) * P], ident_s[:, :])
                m.then_inc(done, 1)

            def transpose_in(g, xn, bank, ready, done):
                for c in range(C):
                    transpose_chunk(g, c, xn, bank + c, ready, done)

            def proj_T(bank, w, col, x, done, cols=P):
                for n, ((wi, xi), c) in enumerate((pa, c) for pa in PASSES for c in range(C)):
                    m = pe.matmul(PS[0:cols, bank, :], w[:, wi, c, col:col + cols], x[xi][:, c, 0:TOK],
                                  start=(n == 0), stop=(n == 3 * C - 1))
                m.then_inc(done, 1)

            def two_T(outs_, x, hi_sem, lo_sem, g):
                for c in range(C):
                    for wi, xi in PASSES:
                        if wi == 0:
                            pe.wait_ge((hi_sem, lo_sem)[xi], 2 * g + c + 1)
                        for bank, w, col, done in outs_:
                            m = pe.matmul(PS[:, bank, :], w[:, wi, c, col:col + P], x[xi][:, c, 0:TOK],
                                          start=(c == 0 and wi + xi == 0), stop=(c == C - 1 and xi == 1))
                            if c == C - 1 and xi == 1:
                                m.then_inc(done, 1)

            def A2(g, turn=lambda: None):
                if not first(g):
                    pe.wait_ge(y_out, 2 * TILES * g)
                two_T([(6 + o, wqkv_h, o * P, q_mm) for o in range(C)], (x1_hi, x1_lo), xT1_a, xT1_v, g)
                proj_T(4, rW1_h, 0, (x1_hi, x1_lo), h1_mm, 64)
                if not first(g):
                    pe.wait_ge(p_sub, TILES * g)
                for c in range(C):
                    proj_T(c, wqkv_h, E + c * P, (x1_hi, x1_lo), k_mm)
                pe.wait_ge(h1_out, g + 1)
                for j in range(IMGS):
                    m = pe.matmul(PS[:, 5, 0:L], rW2_s[:, j, :], h1T[:, j * L:(j + 1) * L],
                                  start=(j == 0), stop=(j == IMGS - 1))
                m.then_inc(rl_mm, 1)
                for n in range(TILES):
                    value_rows(2 + n // 2, n % 2, n * P)
                turn()
                pe.wait_ge(xT1_w, 2 * g + 2)
                pe.wait_ge(k_out, 4 * g + 4)
                for n in range(TILES):
                    value_rows(n // 2, n % 2, n * P + L)

            def value_rows(bank, half, at):
                rows_product(PS[:, bank, half * E:(half + 1) * E], (x1_hi, x1_lo), slice(at, at + P), wqkv_h,
                             slice(2 * E, 3 * E), C).then_inc(v_mm, 1)

            def image_scores(t, left, right, hb):
                for b in range(2):
                    for c in range(C):
                        for i in range(4):
                            at, r = t * P + b * L, slice(32 * i, 32 * i + 32)
                            m = pe.matmul(PS[b * L:(b + 1) * L, i, hb + c * P:hb + (c + 1) * P],
                                          left[r, c, at:at + L], right[r, c, :, at:at + L],
                                          start=False, stop=True, tile_position=(32 * i, b * L),
                                          skip_group_check=True)
                return m

            def scores(g, pair):
                if pair == 0:
                    pe.wait_ge(mb_ok, g + 1)
                    pe.wait_ge(q_out, 2 * g + 2)
                    pe.wait_ge(v_out, 5 * g + 5)
                else:
                    pe.wait_ge(p_sub, TILES * g + 2)
                for t in (2 * pair, 2 * pair + 1):
                    hb = (t % 2) * 256
                    for i in range(4):
                        pe.matmul(PS[:, i, hb:hb + 256], selb[:, t, :], mb[:, 4 * i:4 * i + 4, :],
                                  start=True, stop=False, skip_group_check=True)
                    image_scores(t, qT, kM, hb).then_inc(s_mm, 1)

            def weights_T(g, t, half):
                if half == 0:
                    pe.wait_ge(p_exp, TILES * g + t + 1)
                if t % 2:
                    pe.wait_ge(pt_out, 2 * (TILES * g + t) + half - 1)
                for hp in range(4):
                    at = (4 * half + hp) * P
                    m = pe.transpose(PS[:, 4 + half, hp * P:(hp + 1) * P], Pm[:, t % 2, at:at + P], ident_s[:, :])
                m.then_inc(pt_mm, 1)

            def values(g, t, half):
                pe.wait_ge(pt_out, 2 * (TILES * g + t) + half + 1)
                if t and half == 0:
                    pe.wait_ge(y_out, 2 * (TILES * g + t))
                for hp in range(4 * half, 4 * half + 4):
                    at = PV0 + hp * 4 * VW
                    m = pe.matmul(PF[:, at:at + 4 * VW], PT[:, t % 2, hp, :], Vb[:, t, hp, :, :, :],
                                  start=True, stop=True)
                m.then_inc(pv_mm, 1)

            def attend_first(g, nxt):
                weights_T(g, 0, 0)
                weights_T(g, 0, 1)
                values(g, 0, 0)
                weights_T(g, 1, 0)
                values(g, 0, 1)
                weights_T(g, 1, 1)
                if nxt:
                    pe.wait_ge(pt_out, 2 * (TILES * g + 1) + 1)
                    embed(g + 1, (0,))
                values(g, 1, 0)
                values(g, 1, 1)
                if nxt:
                    embed(g + 1, (1, 2, 3))
                    pe.wait_ge(embed_out, 2 * g + 3)

            def attend_second(g, turn):
                weights_T(g, 2, 0)
                if not isinstance(g, int):
                    pe.wait_ge(embed_out, 2 * g + 4)
                weights_T(g, 2, 1)
                values(g, 2, 0)
                weights_T(g, 3, 0)
                values(g, 2, 1)
                weights_T(g, 3, 1)
                pe.wait_ge(pt_out, 2 * (TILES * g + 3) + 1)
                turn(0)
                values(g, 3, 0)
                values(g, 3, 1)
                turn(1)

            def turn2(g, last):
                if last:
                    pe.wait_ge(Bk_out, 2)
                else:
                    pe.wait_ge(q_out, 2 * g + 4)
                transpose_in(g, xn2, 6, xn2_ok, xT2_mm)

            def A4(g, last):
                if last:
                    pe.wait_ge(Bq_out, 4)
                else:
                    pe.wait_ge(rt1, g + 2)
                pe.wait_ge(xT2_v, 2 * g + 1)
                if last:
                    pe.wait_ge(x8_ok, 2)
                two_T([(5, s1_h, 0, a_mm), (6, s3_h, 0, b_mm)], (x4_hi, x4_lo), xT2_a, xT2_v, g)
                if not last:
                    pe.wait_ge(h1_out, g + 2)
                for t in range(TILES):
                    m = rows_product(PS[:, 4, t * NX:(t + 1) * NX], (x4_hi, x4_lo), slice(t * P, (t + 1) * P),
                                     gateW_h, slice(0, NX), C)
                m.then_inc(gate_mm, 1)
                proj_T(7, s1_h, P, (x4_hi, x4_lo), a_mm)
                pe.wait_ge(lg_ok, g + 1)
                proj_T(4, s3_h, P, (x4_hi, x4_lo), b_mm)
                if not last:
                    scores(g + 1, 0)
                pe.wait_ge(hs_split, 4 * g + 4)
                for t in range(TILES):
                    rows_product(PS[:, 5 + t // 2, (t % 2) * E:(t % 2 + 1) * E], (hs_hi, hs_lo),
                                 slice(t * P, (t + 1) * P), s2_h, slice(0, E), C).then_inc(sh_mm, 1)

            pe.wait_ge(loaded_embed, 16 * len(loads_embed))
            pe.wait_ge(low_w, 1)
            embed(0)
            pe.wait_ge(loaded_A, 16 * len(loads_A))
            pe.wait_ge(setup_v, SETUP_V)
            transpose_in(0, xn1, 4, xn1_ok, xT1_mm)
            pe.wait_ge(low_w, 7)
            A2(0)
            scores(0, 0)
            with pe.Fori(0, LAST) as i:
                scores(i, 1)
                pe.wait_ge(h3_ok, 2 * i + 1)
                attend_first(i, True)
                attend_second(i, lambda c: transpose_chunk(i + 1, c, xn1, 4 + c, xn1_ok, xT1_mm))
                A2(i + 1, lambda: turn2(i, False))
                A4(i, False)
            def routed_tables():
                pe.wait_ge(loaded_experts, 16 * len(loads_experts))
                pe.wait_ge(x8_ok, 2)
                for n, w in enumerate((w1_s, w3_s)):
                    for e in range(NX):
                        for c in range(C):
                            m = pe.matmul(PS[:, 4 + 2 * n, e * NX:(e + 1) * NX], w[:, e, c, :], x8[:, c, :],
                                          start=(c == 0), stop=(c == C - 1))
                    m.then_inc(tab_mm, 1)
                for n in range(2):
                    pe.wait_ge(tabT_ok, n + 1)
                    pe.transpose(PS[0:64, 4 + 2 * n, 0:P], AC[n][:, :], ident_s[:, :]).then_inc(tab_t, 1)

            def routed_count():
                pe.wait_ge(Bv_out, 4)
                pe.wait_ge(cnt_ok, 1)
                pe.matmul(PS[:, 7, 0:NX], ones[:, :], cnt[:, :], start=True, stop=True).then_inc(cnt_mm, 1)

            def routed_sums(g):
                i = g - 1
                pe.wait_ge(f2_ok, TILES * g + TILES)
                pe.wait_ge(silu_hi_ok, i + 1)
                pe.wait_ge(silu_lo_ok, i + 1)
                pe.wait_ge(oh_prev_ok, i + 1)
                for k in range(RB):
                    for part in (silu_hi, silu_lo):
                        m = pe.matmul(PS[0:64, 2, 0:HID], one_hot_prev[:, k, :], part[:, k, :],
                                      start=(k == 0 and part is silu_hi), stop=(k == RB - 1 and part is silu_lo))
                m.then_inc(acc_mm, 1)

            def routed_turn(g):
                i = g - 1
                count = in_reg(pe, i + 1)
                pe.wait_ge(setup_v, 1)
                pe.wait_ge(oh_ok, count)
                for k in range(RB):
                    m = pe.transpose(PH[0:64, k * P:(k + 1) * P], one_hot[:, k, :], identh[:, :])
                m.then_inc(ohT_mm, 1)

            def routed_gates(g):
                i = g - 1
                pe.wait_ge(racc_ok, i + 2)
                pe.wait_ge(ohT_ok, i + 1)
                for k in range(RB):
                    for part in range(2):
                        m = pe.matmul(PS[:, (2, 3, 0, 1)[k // 4], (k % 4) * P:(k % 4 + 1) * P],
                                      one_hot_T[:, k * P:(k + 1) * P], tabA[:, part, :],
                                      start=(part == 0), stop=(part == 1))
                    if k == RB // 2 - 1 or k == RB - 1:
                        m.then_inc(z_mm, 1)

            def routed_out():
                pe.wait_ge(gm_ok, 1)
                pe.transpose(PS[:, 0, 0:64], gm[:, :], ident_s[0:64, 0:64]).then_inc(gT_mm, 1)
                pe.wait_ge(gT_ok, 1)
                for e in range(NX):
                    m = pe.matmul(PS[0:NX, 1, 0:E], gT[:, e * NX:(e + 1) * NX], w2_s[:, e, :],
                                  start=(e == 0), stop=(e == NX - 1))
                m.then_inc(r8_mm, 1)

            def B1_qk(g, before):
                pe.wait_ge(x3T_a, 2 * g + 2)
                pe.wait_ge(x3T_v, 2 * g + 2)
                for c in range(C):
                    proj_T(4 + c, wat_h, c * P, (x1_hi, x1_lo), Bq_mm)
                for c in range(C):
                    if before:
                        pe.wait_ge(h5_ok, TILES * (g - 2) + 2 * c + 2)
                    elif not first(g) and c == 1:
                        pe.wait_ge(h4_ok, 1)
                    proj_T(6 + c, wat_h, E + c * P, (x1_hi, x1_lo), Bk_mm)

            def B1_v(g, tiles):
                for t in tiles:
                    if t == 0:
                        pe.wait_ge(Bk_out, 2 * g + 2)
                    rows_product(PS[:, (7, 5)[t // 2], (t % 2) * E:(t % 2 + 1) * E], (x1_hi, x1_lo),
                                 slice(t * P, (t + 1) * P), wat_h, slice(2 * E, 3 * E), C).then_inc(Bv_mm, 1)

            def B2_scores(g, t):
                if t == 0:
                    pe.wait_ge(Bq_out, 4 * g + 4)
                    pe.wait_ge(Bk_out, 2 * g + 2)
                elif t == 2:
                    pe.wait_ge(f2_ok, TILES * g + 2)
                hb = (t % 2) * 256
                for i in range(4):
                    pe.matmul(PS[:, i, hb:hb + 256], identb[:, :], cmaskb[:, :, :], start=True, stop=False,
                              skip_group_check=True)
                image_scores(t, kT, qM, hb).then_inc(Bs_mm, 1)

            def B2_values(g, pair, banks):
                for t in (2 * pair, 2 * pair + 1):
                    pe.wait_ge(f2_ok, TILES * g + t + 1)
                    for hp in range(HP):
                        m = pe.matmul(PS[:, banks[t % 2], hp * L:(hp + 1) * L], F[:, t % 2, hp * P:(hp + 1) * P],
                                      V2[:, t, 2 * hp:2 * hp + 2, :, :], start=True, stop=True)
                    m.then_inc(Y_mm, 1)

            def B2_turn(g, t, bank):
                pe.wait_ge(Y_out, 2 * (TILES * g + t + 1))
                for b in range(2):
                    m = pe.transpose(PS[:, bank, (t % 2) * E + b * P:(t % 2) * E + (b + 1) * P],
                                     xn2[:, t, b * P:(b + 1) * P], ident_s[:, :])
                m.then_inc(yT_mm, 1)

            def B2_proj(g, pair, bank):
                pe.wait_ge(yT_out, 2 * g + pair + 1)
                for t in (2 * pair, 2 * pair + 1):
                    for e in range(2):
                        m = pe.matmul(PS[:, bank, (t % 2) * E:(t % 2 + 1) * E], xT2[:, e, t * P:(t + 1) * P],
                                      wpr_s[:, e, :], start=(e == 0), stop=(e == 1))
                m.then_inc(pr_mm, 1)

            def B3_up(g, nxt):
                pe.wait_ge(x4T_a, 2 * g + 2)
                pe.wait_ge(x4T_v, 2 * g + 2)
                for f in range(NF):
                    if f == 3 and nxt:
                        pe.wait_ge(Bv_out, 8 * g + 16)
                    if f >= 4:
                        pe.wait_ge(g_ok, NF * g + f - 3)
                    for k, (part, c) in enumerate((part, c) for part in (x4_hi, x4_lo) for c in range(C)):
                        m = pe.matmul(PS[:, UP_BANKS[f % 4], :], wup_h[:, c, f * P:(f + 1) * P], part[:, c, :],
                                      start=(k == 0), stop=(k == 2 * C - 1))
                    m.then_inc(up_mm, 1)

            def B3_squares(g):
                pe.wait_ge(sqa_ok, (NF - 1) * (g + 1))
                for t in range(TILES):
                    m = pe.matmul(PS[:, 7, t:t + 1], sqa[:, t, :], ones[:, 0:1], start=True, stop=True)
                m.then_inc(ss_mm, 1)

            def B3_down(g):
                pe.wait_ge(gl_out, NF * g + NF)
                pe.wait_ge(msq_ok, g + 1)
                for t in range(TILES):
                    if t == 2:
                        pe.wait_ge(h4_ok, 2 * (g + 1) + 1)
                    for k, (part, f) in enumerate((part, f) for part in (G_hi, G_lo) for f in range(NF)):
                        m = pe.matmul(PS[:, 6 + t // 2, (t % 2) * E:(t % 2 + 1) * E],
                                      part[:, f, t * P:(t + 1) * P], wdn_h[:, f, :],
                                      start=(k == 0), stop=(k == 2 * NF - 1))
                    m.then_inc(dn_mm, 1)

            def B3_down_last(g):
                for f in range(NF):
                    pe.wait_ge(gl_out, NF * g + f + 1)
                    for t in range(TILES):
                        for part in (G_hi, G_lo):
                            m = pe.matmul(PS[:, t, 0:E], part[:, f, t * P:(t + 1) * P], wdn_h[:, f, :],
                                          start=(f == 0 and part is G_hi), stop=(f == NF - 1 and part is G_lo))
                        if f == NF - 1:
                            m.then_inc(dn_mm, 1)

            def slot_B(g, prev, nxt, routed=None):
                B2_scores(g, 2)
                if not prev:
                    routed_count()
                B2_scores(g, 3)
                if prev:
                    pe.wait_ge(g_ok, NF * g)
                else:
                    pe.wait_ge(Bv_out, 8 * g + 8)
                    pe.wait_ge(tab_ok, 2)
                    pe.wait_ge(tab_lo_ok, 1)
                    pe.wait_ge(racc_ok, 1)
                B2_values(g, 0, (4, 5))
                B2_turn(g, 0, 6)
                if prev:
                    B3_squares(g - 1)
                B2_turn(g, 1, 6)
                if nxt:
                    transpose_in(g + 1, xn1, 4, xn3_ok, x3T_mm)
                if prev:
                    pe.wait_ge(msq_ok, g)
                B2_proj(g, 0, 7)
                if prev:
                    B3_down(g - 1)
                if routed:
                    routed_sums(g)
                if routed == "batch":
                    routed_turn(g)
                if nxt:
                    B1_qk(g + 1, prev)
                if routed == "batch":
                    routed_gates(g)
                elif routed:
                    routed_out()
                if nxt:
                    pe.wait_ge(Bq_out, 4 * g + 8)
                B2_values(g, 1, (4, 5))
                if nxt:
                    pe.wait_ge(Bk_out, 2 * g + 3)
                else:
                    pe.wait_ge(h5_ok, TILES * g - 2)
                B2_turn(g, 2, 6)
                if nxt:
                    B1_v(g + 1, (0,))
                B2_turn(g, 3, 6)
                if nxt:
                    B1_v(g + 1, (1,))
                B2_proj(g, 1, 4)
                if nxt:
                    if routed == "batch":
                        pe.wait_ge(wz_ok, 2 * g)
                    elif routed:
                        pe.wait_ge(r8_ok, 1)
                    B2_scores(g + 1, 0)
                    B2_scores(g + 1, 1)
                    pe.wait_ge(Bv_out, 8 * g + 12)
                else:
                    pe.wait_ge(h5_ok, TILES * g)
                transpose_in(g, xn2, 6, xn4_ok, x4T_mm)
                if nxt:
                    B1_v(g + 1, (2, 3))
                B3_up(g, nxt)

            scores(LAST, 1)
            pe.wait_ge(abs_ok, 2)
            pe.wait_ge(h3_ok, 2 * LAST + 1)
            pe.matmul(PS[:, 4, 0:2], ones[:, :], sabs[:, :], start=True, stop=True).then_inc(abs_mm, 1)
            pe.wait_ge(th_set, 2)
            attend_first(LAST, False)
            pe.wait_ge(pt_out, 2 * (TILES * LAST + 2))
            attend_second(LAST, lambda c: transpose_chunk(0, c, xn1, 4 + c, xn3_ok, x3T_mm))
            pe.wait_ge(setup_b, 3)
            pe.wait_ge(low_w, len(splits))
            pe.wait_ge(y_out, 2 * TILES * SLOTS)
            B1_qk(0, False)
            turn2(LAST, True)
            A4(LAST, True)
            pe.wait_ge(h3_ok, 2 * SLOTS + 1)
            B1_v(0, range(TILES))
            B2_scores(0, 0)
            B2_scores(0, 1)
            routed_tables()
            slot_B(0, False, True)
            with pe.Fori(1, LAST - 2) as i:
                slot_B(i, True, True, routed="batch")
            slot_B(LAST - 2, True, True, routed="last")
            slot_B(LAST - 1, True, True)
            slot_B(LAST, True, False)
            B3_down_last(LAST)
            B3_squares(LAST)

        @block.scalar
        def _(act):
            def a_A2(g, last_x4=lambda: None):
                for c in range(C):
                    act.wait_ge(xT1_mm, 2 * g + c + 1)
                    act.activation(x1_hi[:, c, 0:TOK], PS[:, 4 + c, :], ACT.Copy).then_inc(xT1_a, 1)
                for c in range(C):
                    act.wait_ge(q_mm, 2 * g + c + 1)
                    act.activation(qT[:, c, :], PS[:, 6 + c, :], ACT.Identity, bias=bqk_s[:, c:c + 1], scale=1 / WS)\
                       .then_inc(q_out, 1)
                act.wait_ge(h1_mm, g + 1)
                act.activation(h1T[:, :], PS[0:64, 4, :], ACT.Relu, bias=rb1_s[:, :], scale=1 / WS).then_inc(h1_out, 1)
                act.wait_ge(rl_mm, g + 1)
                act.activation(t1[:, :], PS[:, 5, 0:L], ACT.Tanh, bias=rb2h[:, :], scale=0.5).then_inc(rt1, 1)
                act.wait_ge(rsg1, g + 1)
                act.activation(t2[:, :], sg1[:, :], ACT.Tanh, scale=0.5).then_inc(rt2, 1)
                last_x4()

            def exps(g, pair):
                for t in (2 * pair, 2 * pair + 1):
                    act.wait_ge(p_sub, TILES * g + t + 1)
                    act.activation(Pm[:, t % 2, :], Pm[:, t % 2, :], ACT.Exp, scale=HD ** -0.5)\
                       .then_inc(p_exp, 1)

            def turns(g, pair):
                for t in (2 * pair, 2 * pair + 1):
                    for half in range(2):
                        act.wait_ge(pt_mm, 2 * (TILES * g + t) + half + 1)
                        act.activation(PT[:, t % 2, 4 * half:4 * half + 4, :], PS[:, 4 + half, :], ACT.Copy)\
                           .then_inc(pt_out, 1)

            def x4_high(g):
                for c in range(C):
                    act.wait_ge(xT2_mm, 2 * g + c + 1)
                    act.activation(x4_hi[:, c, :], PS[:, 6 + c, :], ACT.Copy).then_inc(xT2_a, 1)

            def a_A4(g):
                for c in range(C):
                    act.wait_ge(a_mm, 2 * g + c + 1)
                    act.activation(th[:, c * TOK:(c + 1) * TOK], PS[:, (5, 7)[c], :], ACT.Tanh, scale=0.5 / WS)\
                       .then_inc(th_ok, 1)

            def high_weights(n0, n1):
                for w, hi, lo in splits[n0:n1]:
                    act.activation(hi, w, ACT.Copy, scale=WS).then_inc(high_w, 1)

            def high_patches(g):
                act.wait_ge(patch_in, 16 * g + 16)
                if not first(g):
                    act.wait_ge(embed_mm, TILES * g)
                for k in range(2):
                    ks = slice(k * KP // 2, (k + 1) * KP // 2)
                    act.activation(p_hi[:, ks, :], patch[:, ks, :], ACT.Copy).then_inc(p_hi_ok, 1)

            act.wait_ge(loaded_embed, 16 * len(loads_embed))
            high_weights(0, 1)
            high_patches(0)
            act.wait_ge(loaded_A, 16 * len(loads_A))
            high_weights(1, 7)
            act.wait_ge(setup_v, SETUP_V)
            a_A2(0)
            act.wait_ge(loaded_wat, 16 * len(loads_wat))
            high_weights(7, 8)
            exps(0, 0)
            with act.Fori(0, LAST) as i:
                high_patches(i + 1)
                turns(i, 0)
                exps(i, 1)
                turns(i, 1)
                a_A2(i + 1, lambda: x4_high(i))
                a_A4(i)
                exps(i + 1, 0)
            def routed_tables():
                for n in range(2):
                    act.wait_ge(tab_mm, n + 1)
                    act.activation(AC[n][:, :], PS[:, 4 + 2 * n, 0:64], ACT.Copy).then_inc(tabT_ok, 1)
                for n, dst in enumerate((tabA[:, 0, :], tabC[:, :])):
                    act.wait_ge(tab_t, n + 1)
                    act.activation(dst, PS[0:64, 4 + 2 * n, 0:P], ACT.Copy).then_inc(tab_ok, 1)

            def one_hot_turned(g):
                act.wait_ge(ohT_mm, g)
                act.activation(one_hot_T, PH[0:64, :], ACT.Copy).then_inc(ohT_ok, 1)
                act.activation(one_hot_prev, one_hot, ACT.Copy).then_inc(oh_prev_ok, 1)

            def routed_tanh(g, k):
                cols = slice(k * RB * HID // 2, (k + 1) * RB * HID // 2)
                act.wait_ge(wz_ok, 2 * g - 1 + k)
                act.activation(tz[:, cols], wz[:, cols], ACT.Tanh, scale=0.5).then_inc(tz_ok, 1)

            def routed_hi(g):
                act.wait_ge(silu_ok, 2 * g)
                act.activation(silu_hi, wz, ACT.Copy).then_inc(silu_hi_ok, 1)

            def a_B1_x(g):
                for c in range(C):
                    act.wait_ge(x3T_mm, 2 * g + c + 1)
                    act.activation(x1_hi[:, c, 0:TOK], PS[:, 4 + c, :], ACT.Copy).then_inc(x3T_a, 1)

            def a_B1_k(g):
                for c in range(C):
                    act.wait_ge(Bk_mm, 2 * g + c + 1)
                    act.activation(kT[:, c, :], PS[:, 6 + c, :], ACT.Copy, scale=1 / WS).then_inc(Bk_out, 1)

            def a_B1_v(g, half):
                for t in (2 * half, 2 * half + 1):
                    if t % 2 == 0:
                        act.wait_ge(Bv_mm, TILES * g + t + 2)
                    for b in range(2):
                        r = slice(b * L, (b + 1) * L)
                        act.activation(V2[r, t, :, b, :], PS[r, (7, 5)[t // 2], (t % 2) * E:(t % 2 + 1) * E]
                                       .rearrange("p (h d) -> p h d", d=HD), ACT.Copy, scale=1 / WS).then_inc(Bv_out, 1)

            def relus(g, t):
                hb = (t % 2) * 256
                act.wait_ge(Bs_mm, TILES * g + 2 * (t // 2) + 2)
                act.activation(relu_s[t % 2][:, :], PS[:, 0:4, hb:hb + 256], ACT.Relu).then_inc(relu_ok, 1)

            def lins(g, t):
                hb = (t % 2) * 256
                act.activation(lin[t % 2][:, :], PS[:, 0:4, hb:hb + 256], ACT.Relu, scale=-0.01).then_inc(lin_ok, 1)

            def outs(g, tiles, banks):
                for t in tiles:
                    act.wait_ge(Y_mm, TILES * g + t + 1)
                    y = PS[:, banks[t % 2], :].rearrange("p (hp e b d) -> p hp e b d", hp=HP, e=2, b=2)
                    for e in range(2):
                        r = slice(e * L, (e + 1) * L)
                        act.activation(xn2[r, t, :].rearrange("p (b hp d) -> p b hp d", b=2, hp=HP),
                                       y[r, :, e, :, :].rearrange("p hp b d -> p b hp d"), ACT.Copy, scale=1e-3)\
                           .then_inc(Y_out, 1)

            def a_B3(g, nxt):
                for c in range(C):
                    act.wait_ge(x4T_mm, 2 * g + c + 1)
                    act.activation(x4_hi[:, c, :], PS[:, 6 + c, :], ACT.Copy).then_inc(x4T_a, 1)
                if nxt:
                    relus(g + 1, 0)
                    relus(g + 1, 1)
                    lins(g + 1, 0)
                for f in range(NF):
                    act.wait_ge(up_mm, NF * g + f + 1)
                    if f == 0 and not first(g):
                        act.wait_ge(gl_out, NF * g)
                    act.activation(g32[f], PS[:, UP_BANKS[f % 4], :], ACT.Gelu).then_inc(g_ok, 1)
                    if f == 0 and nxt:
                        lins(g + 1, 1)
                        a_B1_v(g + 1, 1)
                    if f > 0:
                        square(g, f - 1)
                square(g, NF - 1)

            def square(g, f):
                act.wait_ge(g_ok, NF * g + f + 1)
                if f == 0:
                    if not first(g):
                        act.wait_ge(ss_mm, g)
                    act.activation(sqa, g32[0], ACT.Square).then_inc(sq_ok, 1)
                else:
                    if f > 2:
                        act.wait_ge(sqa_ok, (NF - 1) * g + f - 2)
                    act.activation(sqt[f % 2], g32[f], ACT.Square).then_inc(sq_ok, 1)

            def slot_B(g, prev, nxt, routed=None):
                relus(g, 2)
                relus(g, 3)
                outs(g, (0, 1), (4, 5))
                lins(g, 2)
                lins(g, 3)
                if nxt:
                    a_B1_x(g + 1)
                if routed == "batch":
                    one_hot_turned(g)
                if nxt:
                    a_B1_k(g + 1)
                if routed == "last":
                    act.wait_ge(gT_mm, 1)
                    act.activation(gT[:, :], PS[:, 0, 0:64], ACT.Copy).then_inc(gT_ok, 1)
                for k in range(2):
                    if routed == "batch":
                        routed_tanh(g, k)
                    outs(g, (2 + k,), (4, 5))
                if nxt:
                    a_B1_v(g + 1, 0)
                a_B3(g, nxt)
                if routed == "batch":
                    routed_hi(g)

            act.wait_ge(loaded_B, 16 * len(loads_B))
            act.wait_ge(embed_mm, TILES * SLOTS)
            act.activation(spare[:, 0, :], wup_f, ACT.Abs, accum_out=sabs[:, 0:1]).then_inc(abs_ok, 1)
            act.activation(spare[:, 1, :], wdn_f, ACT.Abs, accum_out=sabs[:, 1:2]).then_inc(abs_ok, 1)
            turns(LAST, 0)
            exps(LAST, 1)
            turns(LAST, 1)
            a_B1_x(0)
            a_B1_k(0)
            x4_high(LAST)
            a_A4(LAST)
            act.wait_ge(gl_ok, 1)
            act.activation(rs["ex"][:, :], rs["a"][:, :], ACT.Exp).then_inc(gex_ok, 1)
            act.wait_ge(V2_zero, 1)
            a_B1_v(0, 0)
            a_B1_v(0, 1)
            relus(0, 0)
            relus(0, 1)
            lins(0, 0)
            lins(0, 1)
            routed_tables()
            slot_B(0, False, True)
            with act.Fori(1, LAST - 2) as i:
                slot_B(i, True, True, routed="batch")
            slot_B(LAST - 2, True, True, routed="last")
            slot_B(LAST - 1, True, True)
            slot_B(LAST, True, False)

        @block.gpsimd
        def _(pool):
            def p_rstd(var_ok, n, src, dst, done):
                pool.wait_ge(var_ok, n)
                pool.tensor_tensor(dst[:, :], src[:, :], mhalf[:, :], ALU.pow).then_inc(done, 1)

            def p_mask(g):
                pool.wait_ge(bias_ok, g + 1)
                if not first(g):
                    pool.wait_ge(s_mm, TILES * g)
                pool.tensor_tensor(mb[:, :, :], bias[:, :].unsqueeze(1).broadcast_to([P, NH, L]),
                                   delta_s[:, :].unsqueeze(2).broadcast_to([P, NH, L]), ALU.mult)\
                    .then_inc(mb_ok, 1)

            pool.wait_ge(setup_v, 7)
            def low_patches(g):
                for k in range(2):
                    ks = slice(k * KP // 2, (k + 1) * KP // 2)
                    pool.wait_ge(p_hi_ok, 2 * g + k + 1)
                    pool.tensor_tensor(p_lo[:, ks, :], patch[:, ks, :], p_hi[:, ks, :], ALU.subtract)\
                        .then_inc(p_lo_ok, 1)

            p_rstd(ve1_ok, 1, ve, rstd, rstd1_ok)
            pool.wait_ge(loaded_A, 16 * len(loads_A))
            p_mask(0)
            with pool.Fori(0, LAST) as i:
                low_patches(i + 1)
                p_rstd(ve1_ok, i + 2, ve, rstd, rstd1_ok)
                p_rstd(ve2_ok, i + 1, ve2, rstd2, rstd2_ok)
                p_mask(i + 1)
            p_rstd(ve3_ok, 1, ve, rstd, rstd3_ok)
            p_rstd(ve2_ok, SLOTS, ve2, rstd2, rstd2_ok)

            def quads(g, t):
                pool.wait_ge(relu_ok, TILES * g + t + 1)
                v = relu_s[t % 2][:, :]
                pool.tensor_tensor(v, v, v, ALU.mult).then_inc(quad_even, 1)

            def p_ln4(g, pair):
                ts = slice(2 * pair, 2 * pair + 2)
                pool.wait_ge(ve4_ok, 4 * g + 2 * pair + 2)
                pool.tensor_tensor(rq[:, :, ts], vr[:, :, ts], pq[:, :, ts], ALU.pow).then_inc(rstd4_ok, 1)

            def p_rg(g):
                pool.wait_ge(msq_ok, g + 1)
                pool.tensor_tensor(rg[:, :], msq[:, :], phalf[:, :], ALU.pow).then_inc(rg_ok, 1)

            def p_B3(g, nxt):
                if nxt:
                    quads(g + 1, 0)
                for f in range(NF):
                    if f > 0:
                        pool.wait_ge(sq_ok, NF * g + f + 1)
                        if f > 1:
                            pool.wait_ge(sqa_ok, (NF - 1) * g + f - 1)
                        pool.tensor_tensor(sqa, sqa, sqt[f % 2], ALU.add).then_inc(sqa_ok, 1)

            def routed_lo(g):
                pool.wait_ge(silu_hi_ok, g)
                pool.tensor_tensor(silu_lo, wz.rearrange("p (k n) -> p k n", k=RB), silu_hi, ALU.subtract)\
                    .then_inc(silu_lo_ok, 1)

            def slot_B(g, prev, nxt, routed=None):
                if nxt:
                    p_rstd(ve3_ok, g + 2, ve, rstd, rstd3_ok)
                quads(g, 2)
                if prev:
                    p_rg(g - 1)
                if routed:
                    routed_lo(g)
                p_ln4(g, 0)
                p_ln4(g, 1)
                p_B3(g, nxt)

            quads(0, 0)
            pool.wait_ge(cnt_ok, 1)
            for buf in (wz, halves, one_hot_prev):
                pool.memset(buf, 0.0).then_inc(routed_zero, 1)
            slot_B(0, False, True)
            with pool.Fori(1, LAST - 2) as i:
                slot_B(i, True, True, routed="batch")
            slot_B(LAST - 2, True, True, routed="last")
            slot_B(LAST - 1, True, True)
            slot_B(LAST, True, False)
            p_rg(LAST)

        @block.vector
        def _(dve):
            for buf, v in ((mhalf, -0.5), (phalf, 0.5), (ones, 1.0), (rW2_s, 0.0), (vbuf, 0.0)):
                dve.memset(buf[:], v).then_inc(setup_v, 1)
            for k, v in ((0, -0.5), (1, 0.5)):
                dve.memset(pq[:, k, :], v).then_inc(setup_v, 1)
            dve.wait_ge(setup_v, 7)
            for e in range(2):
                dve.memset(Vb[e * L:(e + 1) * L, :, :, :, e, HD:VW], WS).then_inc(setup_v, 1)
            dve.memset(msq[:, :], 0.0).then_inc(h3_ok, 1)

            def setup_A():
                dve.wait_ge(loaded_A, 16 * len(loads_A))
                for j in range(IMGS):
                    dve.tensor_copy(rW2_s[:, j, NH * j:NH * (j + 1)], rW2c[:, :]).then_inc(setup_v, 1)
                dve.tensor_scalar(rb2h[:, :], rb2_s[:, :], 0.5, None, ALU.mult).then_inc(setup_v, 1)
                dve.tensor_scalar(bqk_s[:, 2:4], bqk_s[:, 2:4], WS, None, ALU.mult).then_inc(setup_v, 1)
                dve.tensor_scalar(bv_s[:, :], bv_s[:, :], WS, None, ALU.mult).then_inc(setup_v, 1)
                dve.tensor_copy(selb[:, :, :], self_[:, :, :]).then_inc(setup_v, 1)

            def low_weights(n0, n1):
                for n, (w, hi, lo) in list(enumerate(splits))[n0:n1]:
                    dve.wait_ge(high_w, n + 1)
                    dve.scalar_tensor_tensor(out=lo, in0=w, scalar=WS, in1=hi, op0=ALU.mult, op1=ALU.subtract)\
                       .then_inc(low_w, 1)

            def setup_B():
                dve.tensor_copy(identb[:, :], ident_s[:, :]).then_inc(setup_b, 1)
                dve.tensor_copy(identh[:, :], ident_s[:, :]).then_inc(setup_b, 1)
                dve.tensor_copy(cmaskb[:, :, :], cmask_s[:, :, :]).then_inc(setup_b, 1)
                dve.wait_ge(abs_mm, 1)
                dve.tensor_scalar(thr[:, :], PS[:, 4, 0:2], 0.5 / (E * FF), None, ALU.mult).then_inc(th_set, 1)
                dve.tensor_scalar(nthr[:, :], PS[:, 4, 0:2], -0.5 / (E * FF), None, ALU.mult).then_inc(th_set, 1)
                dve.wait_ge(th_set, 2)
                for n, (w, ternary) in enumerate(((wup_f, wup_t), (wdn_f, wdn_t))):
                    dve.tensor_scalar(spare[:, n, :], w, nthr[:, n:n + 1], None, ALU.is_lt).then_inc(th_neg, 1)
                    dve.wait_ge(th_neg, n + 1)
                    dve.scalar_tensor_tensor(out=ternary, in0=w, scalar=thr[:, n:n + 1], in1=spare[:, n, :],
                                             op0=ALU.is_gt, op1=ALU.subtract).then_inc(thr_ok, 1)

            def stats(g, st_, mv_, ve_, in_st, in_mv, in_ve, tiles=range(TILES)):
                for t in tiles:
                    dve.bn_stats(st_[:, t, :], H[:, TILES * g + t, :]).then_inc(in_st, 1)
                for t in tiles:
                    count = in_reg(dve, TILES * g + t + 1)
                    dve.wait_ge(setup_v, 1)
                    dve.wait_ge(in_st, count)
                    dve.bn_aggr(mv_[:, t, :], st_[:, t, :]).then_inc(in_mv, 1)
                dve.wait_ge(in_mv, TILES * g + tiles[-1] + 1)
                ts = slice(tiles[0], tiles[-1] + 1)
                dve.tensor_scalar(ve_[:, ts], mv_[:, ts, 1], EPS, None, ALU.add).then_inc(in_ve, 1)

            def normalize(g, xn, mv_, scale, done, tiles=range(TILES)):
                for t in tiles:
                    dve.tensor_scalar(xn[:, t, :], H[:, TILES * g + t, :], mv_[:, t, 0:1], scale[:, t:t + 1],
                                      ALU.subtract, ALU.mult).then_inc(done, 1)

            def embed_h(g):
                for p in range(2):
                    dve.wait_ge(embed_mm, TILES * g + 2 * p + 2)
                    at = TILES * g + 2 * p
                    dve.scalar_tensor_tensor(out=H[:, bass.ds(at, 2), :], scalar=1 / WS,
                                             in0=PS[:, 4 + p, :].rearrange("p (t n) -> p t n", t=2),
                                             in1=tokb_s[:, :].unsqueeze(1).broadcast_to([P, 2, E]),
                                             op0=ALU.mult, op1=ALU.add).then_inc(embed_out, 1)
                count = in_reg(dve, 2 * g + 2)
                dve.wait_ge(setup_v, 1)
                dve.wait_ge(embed_out, count)
                stats(g, st, mv, ve, ve1_st, ve1_mv, ve1_ok)

            def norm1(g):
                dve.wait_ge(rstd1_ok, g + 1)
                normalize(g, xn1, mv, rstd, xn1_ok)

            def x1_low(g):
                for c in range(C):
                    dve.wait_ge(xT1_a, 2 * g + c + 1)
                    dve.tensor_tensor(x1_lo[:, c, 0:TOK], PS[:, 4 + c, :], x1_hi[:, c, 0:TOK], ALU.subtract)\
                       .then_inc(xT1_v, 1)

            def x1_wrap(g):
                dve.tensor_copy(x1_hi[:, :, TOK:TOK + L], x1_hi[:, :, 0:L]).then_inc(xT1_w, 1)
                dve.wait_ge(xT1_v, 2 * g + 2)
                dve.tensor_copy(x1_lo[:, :, TOK:TOK + L], x1_lo[:, :, 0:L]).then_inc(xT1_w, 1)

            def keys_in(g):
                for c in range(C):
                    dve.wait_ge(k_mm, 2 * g + c + 1)
                    for e in range(2):
                        dve.tensor_scalar(kM[:, c, e, :], PS[:, c, :], bqk_s[:, 2 + c:3 + c],
                                          par_s[:, e:e + 1], ALU.add, ALU.mult).then_inc(k_out, 1)

            def router_sigmoid(g):
                dve.wait_ge(rt1, g + 1)
                dve.tensor_scalar(sg1[:, :], t1[:, :], 0.5, 0.5, ALU.mult, ALU.add).then_inc(rsg1, 1)

            def values_to_blocks(g):
                bv3 = bv_s[:, :].rearrange("p (hp e d) -> p hp e d", e=2, d=HD)
                vp = PF[:, 0:8 * E].rearrange("p (n hp e d) -> p n hp e d", n=8, e=2, d=HD)

                def values_in(r, tiles, b, e, n0, n1):
                    n = n1 - n0
                    dve.tensor_tensor(Vb[r, tiles, :, b, e, 0:HD], vp[r, n0:n1, :, e, :],
                                      bv3[r, :, e, :].unsqueeze(1).broadcast_to([L, n, HP, HD]), ALU.add)\
                       .then_inc(v_out, 1)

                lo, hi = slice(0, L), slice(L, P)
                dve.wait_ge(v_mm, 8 * g + 4)
                values_in(lo, slice(0, 4), 0, 0, 4, 8)
                values_in(hi, slice(0, 4), 1, 1, 4, 8)
                dve.wait_ge(v_mm, 8 * g + 8)
                values_in(lo, slice(0, 4), 1, 0, 0, 4)
                values_in(hi, slice(1, 4), 0, 1, 0, 3)
                values_in(hi, slice(0, 1), 0, 1, 3, 4)

            def top_keys(g, last_x4):
                dve.wait_ge(rt2, g + 1)
                dve.tensor_scalar(wk[0][:, :], t2[:, :], 0.5, 0.5, ALU.mult, ALU.add).then_inc(top_step, 1)
                for r in range(KEEP // 8):
                    count = in_reg(dve, TOP * g + 2 * r + 1)
                    dve.wait_ge(setup_v, 1)
                    dve.wait_ge(top_step, count)
                    dve.max(m8[r][:, :], wk[r % 3][:, :]).then_inc(top_step, 1)
                    count = in_reg(dve, TOP * g + 2 * r + 2)
                    dve.wait_ge(setup_v, 1)
                    dve.wait_ge(top_step, count)
                    dve.match_replace(wk[(r + 1) % 3][:, :], m8[r][:, :], wk[r % 3][:, :], TAKEN)\
                       .then_inc(top_step, 1)
                last_x4()
                left = wk[(KEEP // 8) % 3]
                count = in_reg(dve, TOP * g + TOP - 3)
                dve.wait_ge(setup_v, 1)
                dve.wait_ge(top_step, count)
                dve.max(m8[3][:, :], left[:, :]).then_inc(top_step, 1)
                dve.wait_ge(top_step, TOP * g + TOP - 2)
                dve.scalar_tensor_tensor(out=cand[:, :], in0=left[:, :], scalar=m8[3][:, 0:1], in1=rev64_s[:, :],
                                         op0=ALU.is_equal, op1=ALU.mult).then_inc(top_step, 1)
                count = in_reg(dve, TOP * g + TOP - 1)
                dve.wait_ge(setup_v, 1)
                dve.wait_ge(top_step, count)
                dve.max(m8[4][:, :], cand[:, :]).then_inc(top_step, 1)
                dve.wait_ge(top_step, TOP * g + TOP)
                dve.tensor_scalar(selk[:, :], cand[:, :], m8[4][:, 0:1], None, ALU.is_equal)\
                   .then_inc(selk_ok, 1)
                dve.wait_ge(selk_ok, g + 1)
                dve.scalar_tensor_tensor(out=keep[:, :], in0=left[:, :], scalar=TAKEN, in1=selk[:, :],
                                         op0=ALU.is_equal, op1=ALU.add).then_inc(keep_ok, 1)
                dve.wait_ge(keep_ok, g + 1)
                if not first(g):
                    dve.wait_ge(mb_ok, g)
                dve.tensor_scalar(bias[:, :], keep[:, :], -1.0, -NEG, ALU.add, ALU.mult)\
                   .then_inc(bias_ok, 1)

            def soft(g, t):
                hb = (t % 2) * 256
                dve.wait_ge(s_mm, TILES * g + 2 * (t // 2) + 2)
                dve.tensor_reduce(mx[:, t % 2, :].rearrange("p (i h) -> p i h", i=4),
                                  PS[:, 0:4, hb:hb + 256].rearrange("p i (h k) -> p i h k", k=L), AX.X, ALU.max)\
                   .then_inc(smax, 1)
                dve.wait_ge(smax, TILES * g + t + 1)
                if not (first(g) and t < 2):
                    dve.wait_ge(pt_mm, 2 * (TILES * g + t - 1))
                dve.tensor_tensor(Pm[:, t % 2, :].rearrange("p (i h k) -> p i h k", i=4, k=L),
                                  PS[:, 0:4, hb:hb + 256].rearrange("p i (h k) -> p i h k", k=L),
                                  mx[:, t % 2, :].rearrange("p (i h) -> p i h", i=4).unsqueeze(3)
                                  .broadcast_to([P, 4, 4, L]), ALU.subtract).then_inc(p_sub, 1)

            def attend(g, t):
                dve.wait_ge(pv_mm, 2 * (TILES * g + t + 1))
                o = PF[:, PV0:PV0 + HP * 4 * VW].rearrange("p (hp b e v) -> p hp b e v", hp=HP, b=2, e=2)
                for b in range(2):
                    r = slice(b * L, (b + 1) * L)
                    dve.reciprocal(rden[r, :].rearrange("p (hp e) -> p hp e", e=2), o[r, :, b, :, HD])\
                       .then_inc(rden_ok, 1)
                for b in range(2):
                    r = slice(b * L, (b + 1) * L)
                    dve.wait_ge(rden_ok, 2 * (TILES * g + t) + b + 1)
                    dve.tensor_tensor(yn[r, :].rearrange("p (hp e d) -> p hp e d", hp=HP, e=2),
                                      o[r, :, b, :, 0:HD],
                                      rden[r, :].rearrange("p (hp e) -> p hp e", e=2).unsqueeze(3)
                                      .broadcast_to([L, HP, 2, HD]), ALU.mult).then_inc(y_out, 1)
                dve.wait_ge(y_out, 2 * (TILES * g + t + 1))
                dve.tensor_tensor(H[:, TILES * g + t, :], H[:, TILES * g + t, :], yn[:, :], ALU.add)\
                   .then_inc(h2_ok, 1)

            def stats2(g):
                count = in_reg(dve, TILES * g + TILES)
                dve.wait_ge(setup_v, 1)
                dve.wait_ge(h2_ok, count)
                stats(g, st2, mv2, ve2, ve2_st, ve2_mv, ve2_ok)

            def norm2(g):
                dve.wait_ge(rstd2_ok, g + 1)
                normalize(g, xn2, mv2, rstd2, xn2_ok)

            def x2_low(g):
                for c in range(C):
                    dve.wait_ge(xT2_a, 2 * g + c + 1)
                    dve.tensor_tensor(x4_lo[:, c, :], PS[:, 6 + c, :], x4_hi[:, c, :], ALU.subtract)\
                       .then_inc(xT2_v, 1)

            def v_A4(g):
                dve.wait_ge(gate_mm, g + 1)
                dve.tensor_scalar(lg[:, bass.ds(TILES * g, TILES), :], PS[:, 4, 0:TILES * NX]
                                  .rearrange("p (t e) -> p t e", e=NX), 1 / WS, None, ALU.mult).then_inc(lg_ok, 1)
                for c in range(C):
                    cols = slice(c * TOK, (c + 1) * TOK)
                    dve.wait_ge(th_ok, 2 * g + c + 1)
                    dve.scalar_tensor_tensor(out=u[:, cols], in0=th[:, cols], scalar=1.0, in1=PS[:, (5, 7)[c], :],
                                             op0=ALU.add, op1=ALU.mult).then_inc(u_ok, 1)
                    dve.wait_ge(u_ok, 2 * g + c + 1)
                    dve.wait_ge(b_mm, 2 * g + c + 1)
                    dve.scalar_tensor_tensor(out=hs[:, cols], in0=u[:, cols], scalar=HS / WS ** 2,
                                             in1=PS[:, (6, 4)[c], :], op0=ALU.mult, op1=ALU.mult)\
                       .then_inc(hs_ok, 1)
                    dve.wait_ge(hs_ok, 2 * g + c + 1)
                    dve.tensor_copy(hs_hi[:, c, :], hs[:, cols]).then_inc(hs_split, 1)
                    dve.wait_ge(hs_split, 4 * g + 2 * c + 1)
                    dve.tensor_tensor(hs_lo[:, c, :], hs[:, cols], hs_hi[:, c, :], ALU.subtract)\
                       .then_inc(hs_split, 1)

            def v_shared(g):
                for p in range(2):
                    dve.wait_ge(sh_mm, TILES * g + 2 * p + 2)
                    rows2 = H[:, bass.ds(TILES * g + 2 * p, 2), :]
                    dve.scalar_tensor_tensor(out=rows2, in0=PS[:, 5 + p, :].rearrange("p (t n) -> p t n", t=2),
                                             scalar=0.5 / (HS * WS), in1=rows2, op0=ALU.mult, op1=ALU.add)\
                       .then_inc(h3_ok, 1)

            def slot_in(g, last_norm=lambda: None, last_x4=lambda: None):
                last_norm()
                keys_in(g)
                router_sigmoid(g)
                top_keys(g, last_x4)
                values_to_blocks(g)

            dve.wait_ge(loaded_embed, 16 * len(loads_embed))
            low_weights(0, 1)
            for k in range(2):
                ks = slice(k * KP // 2, (k + 1) * KP // 2)
                dve.wait_ge(p_hi_ok, k + 1)
                dve.tensor_tensor(p_lo[:, ks, :], patch[:, ks, :], p_hi[:, ks, :], ALU.subtract).then_inc(p_lo_ok, 1)
            setup_A()
            low_weights(1, 7)
            embed_h(0)
            norm1(0)
            x1_low(0)
            x1_wrap(0)
            slot_in(0)
            dve.wait_ge(loaded_wat, 16 * len(loads_wat))
            low_weights(7, 8)
            soft(0, 0)
            soft(0, 1)
            with dve.Fori(0, LAST) as i:
                attend(i, 0)
                soft(i, 2)
                attend(i, 1)
                soft(i, 3)
                embed_h(i + 1)
                norm1(i + 1)
                attend(i, 2)
                attend(i, 3)
                x1_low(i + 1)
                x1_wrap(i + 1)
                stats2(i)
                slot_in(i + 1, lambda: norm2(i), lambda: x2_low(i))
                v_A4(i)
                soft(i + 1, 0)
                soft(i + 1, 1)
                v_shared(i)

            def each(v):
                return v[:, :].unsqueeze(2).broadcast_to([P, NT, NX])

            def experts(v):
                return v[:, :].unsqueeze(1).broadcast_to([P, NT, NX])

            def expert_logits():
                dve.tensor_reduce(rsm["mx"][:, :], lg[:, :, :], AX.X, ALU.max).then_inc(routed_step, 1)
                dve.wait_ge(routed_step, after("routed"))
                dve.tensor_tensor(r3["a"], lg[:, :, :], each(rsm["mx"]), ALU.subtract).then_inc(gl_ok, 1)

            def expert_choice(between):
                dve.wait_ge(gex_ok, 1)
                dve.tensor_reduce(rsm["sum"][:, :], r3["ex"], AX.X, ALU.add).then_inc(routed_step, 1)
                dve.wait_ge(routed_step, after("routed"))
                dve.reciprocal(rsm["inv"][:, :], rsm["sum"][:, :]).then_inc(routed_step, 1)
                dve.wait_ge(routed_step, after("routed"))
                dve.tensor_tensor(r3["pr"], r3["ex"], each(rsm["inv"]), ALU.mult).then_inc(routed_step, 1)
                dve.wait_ge(routed_step, after("routed"))
                dve.tensor_tensor(r3["s"], r3["pr"], experts(eb_s), ALU.add).then_inc(routed_step, 1)
                dve.wait_ge(routed_step, after("routed"))
                s4 = rs["s"][:, :].rearrange("p (t g x) -> p t g x", g=4, x=2)
                dve.tensor_tensor(gs[:, :, :], s4[:, :, :, 0], s4[:, :, :, 1], ALU.add).then_inc(routed_step, 1)
                dve.wait_ge(routed_step, after("routed"))
                for a in range(4):
                    dve.memset(wins[:, :, a], float(a)).then_inc(routed_step, 1)
                    dve.wait_ge(routed_step, after("routed"))
                for a in range(4):
                    for b in range(a + 1, 4):
                        dve.tensor_tensor(cmp[:, :], gs[:, :, a], gs[:, :, b], ALU.is_ge).then_inc(routed_step, 1)
                        dve.wait_ge(routed_step, after("routed"))
                        dve.tensor_tensor(wins[:, :, a], wins[:, :, a], cmp[:, :], ALU.add).then_inc(routed_step, 1)
                        dve.wait_ge(routed_step, after("routed"))
                        dve.tensor_tensor(wins[:, :, b], wins[:, :, b], cmp[:, :], ALU.subtract).then_inc(routed_step, 1)
                        dve.wait_ge(routed_step, after("routed"))
                dve.tensor_scalar(gk[:, :, :], wins[:, :, :], 2.0, None, ALU.is_ge).then_inc(routed_step, 1)
                dve.wait_ge(routed_step, after("routed"))
                dve.tensor_scalar(gd[:, :, :], gk[:, :, :], -1.0, BIG, ALU.add, ALU.mult).then_inc(routed_step, 1)
                dve.wait_ge(routed_step, after("routed"))
                m4 = rs["m"][:, :].rearrange("p (t g x) -> p t g x", g=4, x=2)
                for xx in range(2):
                    dve.tensor_tensor(m4[:, :, :, xx], s4[:, :, :, xx], gk[:, :, :], ALU.mult).then_inc(routed_step, 1)
                    dve.wait_ge(routed_step, after("routed"))
                    dve.tensor_tensor(m4[:, :, :, xx], m4[:, :, :, xx], gd[:, :, :], ALU.add).then_inc(routed_step, 1)
                    dve.wait_ge(routed_step, after("routed"))
                for k, (src, oh, mxk, ck) in enumerate((("m", "oh1", "m1", "c1"), ("b", "oh2", "m2", "c2"))):
                    dve.tensor_reduce(rsm[mxk][:, :], r3[src], AX.X, ALU.max).then_inc(routed_step, 1)
                    dve.wait_ge(routed_step, after("routed"))
                    dve.tensor_tensor(r3["a"], r3[src], each(rsm[mxk]), ALU.is_equal).then_inc(routed_step, 1)
                    dve.wait_ge(routed_step, after("routed"))
                    dve.tensor_tensor(r3["a"], r3["a"], experts(rev8_s), ALU.mult).then_inc(routed_step, 1)
                    dve.wait_ge(routed_step, after("routed"))
                    dve.tensor_reduce(rsm[ck][:, :], r3["a"], AX.X, ALU.max).then_inc(routed_step, 1)
                    dve.wait_ge(routed_step, after("routed"))
                    dve.tensor_tensor(r3[oh], r3["a"], each(rsm[ck]), ALU.is_equal).then_inc(routed_step, 1)
                    dve.wait_ge(routed_step, after("routed"))
                    if k == 0:
                        dve.scalar_tensor_tensor(out=rs["b"][:, :], in0=rs[oh][:, :], scalar=-BIG,
                                                 in1=rs["m"][:, :], op0=ALU.mult, op1=ALU.add).then_inc(routed_step, 1)
                        dve.wait_ge(routed_step, after("routed"))
                    cols = slice(k * NT, (k + 1) * NT)
                    dve.tensor_scalar(ei[:, cols], rsm[ck][:, :], -1.0, float(NX), ALU.mult, ALU.add)\
                       .then_inc(routed_step, 1)
                    dve.wait_ge(routed_step, after("routed"))
                    dve.tensor_tensor(r3["a"], r3[oh], r3["pr"], ALU.mult).then_inc(routed_step, 1)
                    dve.wait_ge(routed_step, after("routed"))
                    dve.tensor_reduce(wt[:, cols], r3["a"], AX.X, ALU.add).then_inc(routed_step, 1)
                    dve.wait_ge(routed_step, after("routed"))
                    if k == 0:
                        between()
                dve.tensor_tensor(rs["a"][:, :], rs["oh1"][:, :], rs["oh2"][:, :], ALU.add).then_inc(routed_step, 1)
                dve.wait_ge(routed_step, after("routed"))
                dve.tensor_reduce(cnt[:, :], rs["a"][:, :].rearrange("p (t e) -> p e t", e=NX), AX.X, ALU.add)\
                   .then_inc(cnt_ok, 1)

            def row_codes():
                dve.wait_ge(cnt_mm, 1)
                dve.tensor_copy(off[:, :], PS[:, 7, 0:NX]).then_inc(routed_step, 1)
                dve.wait_ge(routed_step, after("routed"))
                for e in range(1, NX):
                    dve.tensor_tensor(off[:, e:e + 1], off[:, e:e + 1], off[:, e - 1:e], ALU.add).then_inc(routed_step, 1)
                    dve.wait_ge(routed_step, after("routed"))
                dve.tensor_scalar(gg[:, :], ridx_s[:, :], off[:, 0:1], None, ALU.is_ge).then_inc(routed_step, 1)
                dve.wait_ge(routed_step, after("routed"))
                for e in range(1, NX - 1):
                    dve.scalar_tensor_tensor(out=gg[:, :], in0=ridx_s[:, :], scalar=off[:, e:e + 1],
                                             in1=gg[:, :], op0=ALU.is_ge, op1=ALU.add).then_inc(routed_step, 1)
                    dve.wait_ge(routed_step, after("routed"))
                dve.scalar_tensor_tensor(out=code[:, 0:CH], in0=gg[:, :], scalar=float(NX), in1=ei[:, :],
                                         op0=ALU.mult, op1=ALU.add).then_inc(routed_step, 1)
                dve.wait_ge(routed_step, after("routed"))
                dve.memset(code[:, CH:CH + RB], 0.0).then_inc(routed_zero, 1)
                dve.wait_ge(routed_zero, 4)
                dve.memset(racc[:, :], 0.0).then_inc(racc_ok, 1)
                dve.memset(cmp[:, 0:1], 0.0).then_inc(silu_hi_ok, 1)
                dve.memset(cmp[:, 1:2], 0.0).then_inc(oh_prev_ok, 1)

            def one_hots(g):
                if not first(g):
                    dve.wait_ge(oh_prev_ok, g + 1)
                dve.tensor_tensor(one_hot, iota_s[:, :].unsqueeze(1).broadcast_to([P, RB, 64]),
                                  code[:, bass.ds(RB * g, RB)].unsqueeze(2).broadcast_to([P, RB, 64]),
                                  ALU.is_equal).then_inc(oh_ok, 1)

            def sums_in(g):
                dve.wait_ge(acc_mm, g)
                dve.wait_ge(racc_ok, g)
                dve.tensor_tensor(racc[:, :], racc[:, :], PS[0:64, 2, 0:HID], ALU.add).then_inc(racc_ok, 1)

            def weighted(k, g):
                return wt[:, bass.ds(RB * (g - 1) + k * RB // 2, RB // 2)].unsqueeze(2)\
                    .broadcast_to([P, RB // 2, HID])

            def half_batch(k):
                return wz[:, k * RB * HID // 2:(k + 1) * RB * HID // 2].rearrange("p (k n) -> p k n", n=HID)

            def gates_in(g):
                for k in range(2):
                    dve.wait_ge(z_mm, 2 * g - 1 + k)
                    z = PS[:, 2 - 2 * k:4 - 2 * k, :].rearrange("p b (k n) -> p (b k) n", n=HID)
                    dve.tensor_tensor(half_batch(k), z, weighted(k, g), ALU.mult).then_inc(wz_ok, 1)

            def silus(g):
                for k in range(2):
                    cols = slice(k * RB * HID // 2, (k + 1) * RB * HID // 2)
                    dve.wait_ge(tz_ok, 2 * g - 1 + k)
                    dve.scalar_tensor_tensor(out=wz[:, cols], in0=tz[:, cols], scalar=1.0, in1=wz[:, cols],
                                             op0=ALU.add, op1=ALU.mult).then_inc(silu_step, 1)

            def weighted_silus(g):
                for k in range(2):
                    dve.wait_ge(silu_step, 2 * g - 1 + k)
                    dve.tensor_tensor(half_batch(k), half_batch(k), weighted(k, g), ALU.mult).then_inc(silu_ok, 1)

            def gated_sums():
                dve.wait_ge(racc_ok, LAST - 1)
                dve.scalar_tensor_tensor(out=gm[:, :], in0=racc[:, :], scalar=0.5, in1=tabC[:, :], op0=ALU.mult,
                                         op1=ALU.mult).then_inc(gm_ok, 1)

            def routed_rows_in():
                dve.wait_ge(r8_mm, 1)
                dve.tensor_tensor(H[0:NX, TILES * LAST, :], H[0:NX, TILES * LAST, :], PS[0:NX, 1, 0:E], ALU.add)\
                   .then_inc(r8_ok, 1)
                dve.wait_ge(r8_ok, 1)

            def norm3(g):
                dve.wait_ge(rstd3_ok, g + 1)
                normalize(g, xn1, mv, rstd, xn3_ok)

            def v_B1(g):
                for c in range(C):
                    dve.wait_ge(Bq_mm, 2 * g + c + 1)
                    for e in range(2):
                        dve.tensor_scalar(qM[:, c, e, :], PS[:, 4 + c, :], par_s[:, 2 + e:3 + e], None, ALU.mult)\
                           .then_inc(Bq_out, 1)

            def v_x3T(g):
                for c in range(C):
                    dve.wait_ge(x3T_a, 2 * g + c + 1)
                    dve.tensor_tensor(x1_lo[:, c, 0:TOK], PS[:, 4 + c, :], x1_hi[:, c, 0:TOK], ALU.subtract)\
                       .then_inc(x3T_v, 1)

            def v_quads(g, t):
                dve.wait_ge(relu_ok, TILES * g + t + 1)
                v = relu_s[t % 2][:, :]
                dve.tensor_tensor(v, v, v, ALU.mult).then_inc(quad_odd, 1)

            def poly(g, t):
                hb = (t % 2) * 256
                dve.wait_ge(lin_ok, TILES * g + 2 * (t // 2) + 2)
                dve.wait_ge((quad_even, quad_odd)[t % 2], 2 * g + t // 2 + 1)
                dve.scalar_tensor_tensor(out=lin[t % 2][:, :], in0=lin[t % 2][:, :], scalar=1.0,
                                         in1=relu_s[t % 2][:, :], op0=ALU.add,
                                         op1=ALU.add).then_inc(f0_ok, 1)
                dve.wait_ge(f0_ok, TILES * g + t + 1)
                if not (first(g) and t < 2):
                    dve.wait_ge(Y_mm, TILES * g + t - 1)
                Fv = F[:, t % 2, :].rearrange("p (i n) -> p i n", i=4)
                dve.scalar_tensor_tensor(out=Fv, in0=PS[:, 0:4, hb:hb + 256], scalar=-100.0,
                                         in1=lin[t % 2][:, :].rearrange("p (i n) -> p i n", i=4), op0=ALU.is_ge,
                                         op1=ALU.mult).then_inc(f2_ok, 1)

            def turned(g, pair, bank):
                dve.wait_ge(yT_mm, TILES * g + 2 * pair + 2)
                for t in (2 * pair, 2 * pair + 1):
                    m = dve.tensor_copy(xT2[:, :, t * P:(t + 1) * P].rearrange("p e (b q) -> p e b q", b=2),
                                        PS[:, bank, (t % 2) * E:(t % 2 + 1) * E]
                                        .rearrange("p (b e q) -> p e b q", b=2, e=2))
                m.then_inc(yT_out, 1)

            def projected(g, pair, bank):
                dve.wait_ge(pr_mm, 2 * g + pair + 1)
                rows2 = H[:, bass.ds(TILES * g + 2 * pair, 2), :]
                dve.tensor_tensor(rows2, rows2, PS[:, bank, :].rearrange("p (t n) -> p t n", t=2), ALU.add)\
                   .then_inc(h4_ok, 1)

            def norm4(g, pair):
                tiles = range(2 * pair, 2 * pair + 2)
                ts = slice(2 * pair, 2 * pair + 2)
                count = in_reg(dve, 2 * g + pair + 1)
                dve.wait_ge(setup_v, 1)
                dve.wait_ge(h4_ok, count)
                stats(g, st2, mv2, vr[:, 0, :], ve4_st, ve4_mv, ve4_ok, tiles)
                dve.tensor_copy(vr[:, 1, ts], mv2[:, ts, 1]).then_inc(ve4_ok, 1)
                dve.wait_ge(rstd4_ok, 2 * g + pair + 1)
                n = 8 * g + 4 * pair
                dve.tensor_tensor(rr[:, ts], rq[:, 1, ts], rq[:, 0, ts], ALU.mult).then_inc(r4_step, 1)
                dve.wait_ge(r4_step, n + 1)
                dve.tensor_scalar(rr[:, ts], rr[:, ts], 1e-8, None, ALU.add).then_inc(r4_step, 1)
                dve.wait_ge(r4_step, n + 2)
                dve.reciprocal(rr[:, ts], rr[:, ts]).then_inc(r4_step, 1)
                dve.wait_ge(r4_step, n + 3)
                dve.tensor_tensor(r4[:, ts], rr[:, ts], rq[:, 0, ts], ALU.mult).then_inc(r4_step, 1)
                dve.wait_ge(r4_step, n + 4)
                normalize(g, xn2, mv2, r4, xn4_ok, tiles)

            def v_x4T(g):
                for c in range(C):
                    dve.wait_ge(x4T_a, 2 * g + c + 1)
                    dve.tensor_tensor(x4_lo[:, c, :], PS[:, 6 + c, :], x4_hi[:, c, :], ALU.subtract)\
                       .then_inc(x4T_v, 1)

            def g_parts(g, f0, f1):
                for f in range(f0, f1):
                    dve.wait_ge(g_ok, NF * g + f + 1)
                    dve.tensor_copy(G_hi[:, f, :], g32[f]).then_inc(gh_out, 1)
                    dve.wait_ge(gh_out, NF * g + f + 1)
                    dve.tensor_tensor(G_lo[:, f, :], g32[f], G_hi[:, f, :], ALU.subtract)\
                       .then_inc(gl_out, 1)

            def mean_squares(g):
                dve.wait_ge(ss_mm, g + 1)
                dve.tensor_scalar(msq[:, :], PS[:, 7, 0:TILES], 1.0 / FF, None, ALU.mult).then_inc(msq_ok, 1)

            def one_over_rms(g):
                dve.wait_ge(rg_ok, g + 1)
                dve.tensor_scalar(rge[:, :], rg[:, :], 1e-8, None, ALU.add).then_inc(rg_step, 1)
                dve.wait_ge(rg_step, 2 * g + 1)
                dve.reciprocal(rgi[:, :], rge[:, :]).then_inc(rg_step, 1)

            def ffn_out(g, last=False):
                dve.wait_ge(rg_step, 2 * g + 2)
                for t in range(TILES):
                    dve.wait_ge(dn_mm, TILES * g + 2 * (t // 2) + 2)
                    at = TILES * g + t
                    rows = PS[:, t, 0:E] if last else PS[:, 6 + t // 2, (t % 2) * E:(t % 2 + 1) * E]
                    dve.scalar_tensor_tensor(out=H[:, at, :], in0=rows, scalar=rgi[:, t:t + 1], in1=H[:, at, :],
                                             op0=ALU.mult, op1=ALU.add).then_inc(h5_ok, 1)

            def stats3(g):
                stats(g, st, mv, ve, ve3_st, ve3_mv, ve3_ok)

            def slot_B(g, prev, nxt, routed=None):
                if nxt:
                    stats3(g + 1)
                    norm3(g + 1)
                v_quads(g, 3)
                if prev:
                    mean_squares(g - 1)
                turned(g, 0, 6)
                if nxt:
                    v_x3T(g + 1)
                poly(g, 2)
                projected(g, 0, 7)
                if prev:
                    one_over_rms(g - 1)
                poly(g, 3)
                if not prev:
                    v_B1(g + 1)
                norm4(g, 0)
                if prev:
                    ffn_out(g - 1)
                if routed:
                    sums_in(g)
                if routed == "last":
                    gated_sums()
                if nxt and prev:
                    v_B1(g + 1)
                if routed == "batch":
                    gates_in(g)
                    silus(g)
                elif routed:
                    routed_rows_in()
                turned(g, 1, 6)
                if routed == "batch":
                    weighted_silus(g)
                projected(g, 1, 4)
                norm4(g, 1)
                v_x4T(g)
                if nxt:
                    v_quads(g + 1, 1)
                g_parts(g, 0, 1)
                if nxt:
                    poly(g + 1, 0)
                    poly(g + 1, 1)
                g_parts(g, 1, NF)
                if routed == "batch" or not prev:
                    one_hots(g)

            setup_B()
            attend(LAST, 0)
            soft(LAST, 2)
            attend(LAST, 1)
            soft(LAST, 3)
            stats3(0)
            norm3(0)
            attend(LAST, 2)
            attend(LAST, 3)
            v_x3T(0)
            stats2(LAST)
            norm2(LAST)
            v_B1(0)
            dve.memset(vbuf[:], 0.0).then_inc(V2_zero, 1)
            x2_low(LAST)
            for c in range(C):
                dve.tensor_copy(x8[:, c, :], PS[:, 6 + c, 0:NX]).then_inc(x8_ok, 1)
            v_A4(LAST)
            expert_logits()
            v_shared(LAST)
            def first_polys():
                v_quads(0, 1)
                poly(0, 0)
                poly(0, 1)

            expert_choice(first_polys)
            dve.wait_ge(tab_ok, 1)
            dve.tensor_tensor(tabA[:, 1, :], PS[0:64, 4, 0:P], tabA[:, 0, :], ALU.subtract).then_inc(tab_lo_ok, 1)
            row_codes()
            slot_B(0, False, True)
            with dve.Fori(1, LAST - 2) as i:
                slot_B(i, True, True, routed="batch")
            slot_B(LAST - 2, True, True, routed="last")
            slot_B(LAST - 1, True, True)
            slot_B(LAST, True, False)
            mean_squares(LAST)
            one_over_rms(LAST)
            ffn_out(LAST, last=True)


def _layout(inputs):
    a = {k: np.asarray(v) for k, v in inputs.items()}

    def chunks(w):
        return w.reshape(-1, P, w.shape[1]).transpose(1, 0, 2)

    def rows(v):
        return np.broadcast_to(v[None, :], (P, v.shape[0]))

    x = a["x"].reshape(SLOTS, IMGS, 3, 8, 16, 8, 16).transpose(0, 2, 4, 6, 1, 3, 5).reshape(SLOTS, KP, P, TOK)
    x = np.roll(x, -1, axis=0).transpose(0, 2, 1, 3)
    order = np.concatenate([np.arange(HD) + HD * (4 * i + 2 * c + e)
                            for c in range(C) for i in range(4) for e in range(2)])
    qkv = a["L0_attn_qkv_w"].T
    qkv = np.concatenate([qkv[:, order], qkv[:, E + order], qkv[:, 2 * E:]], axis=1)
    qb = a["L0_attn_qkv_b"]
    bqk = np.stack([qb[order][:P], qb[order][P:], qb[E + order][:P], qb[E + order][P:]], axis=1)
    wat = a["L1_attn_W_attn"]
    wat = np.concatenate([wat[:, order], wat[:, E + order], wat[:, 2 * E:]], axis=1)
    wpr = a["L1_attn_W_proj"].reshape(HP, 2, HD, E).transpose(0, 2, 1, 3).reshape(P, 2, E)

    def hid(w):
        return w.reshape(NX, C, P, HID).transpose(2, 0, 1, 3)

    ident = np.eye(P)
    f = np.arange(P)
    even = ((f // HD) % 2 == 0).astype(np.float32)
    par = np.stack([even, 1 - even, HD ** -0.5 * even, HD ** -0.5 * (1 - even)], axis=1) / WS
    sel = (f[:, None, None] // NH == 2 * np.arange(TILES)[None, :, None] + f[None, None, :] // L)
    delta = f[:, None] % NH == np.arange(NH)[None, :]
    rev64 = rows(np.arange(L, 0, -1))
    cm = np.where(f[:, None] % L > np.arange(L)[None, :], NEG, 0.0)
    cmask = np.broadcast_to(cm[:, None, :], (P, 4, L))
    slot = np.arange(SLOTS * TILES)
    tile0 = ((slot // TILES + 1) % SLOTS) * TILES + slot % TILES
    token = tile0[None, :] * P + f[:, None]
    ridx = np.concatenate([2 * token, 2 * token + 1], axis=1)
    maps = dict(
        x=x, tokW=chunks(a["L0_tok_W"]), tokb=rows(a["L0_tok_b"]), wqkv=chunks(qkv), bqk=bqk, bv=rows(qb[2 * E:]),
        rW1=chunks(a["L0_attn_r_w1"].T), rb1=a["L0_attn_r_b1"][:, None], rW2=a["L0_attn_r_w2"].T,
        rb2=np.tile(a["L0_attn_r_b2"], IMGS)[:, None], gateW=chunks(a["L0_ffn_w_gate"].T),
        eb=rows(a["L0_ffn_expert_bias"]), w1=hid(a["L0_ffn_w1"]), w3=hid(a["L0_ffn_w3"]),
        w2=a["L0_ffn_w2"].transpose(1, 0, 2), s1=chunks(a["L0_ffn_sw1"].T), s3=chunks(a["L0_ffn_sw3"].T),
        s2=chunks(a["L0_ffn_sw2"].T), wat=chunks(wat), wpr=wpr, wup=chunks(a["L1_ffn_w_up"].T),
        wdn=chunks(a["L1_ffn_w_down"].T), ident=ident, par=par, sel=sel, delta=delta, rev64=rev64, cmask=cmask,
        ridx=ridx, iota64=rows(np.arange(64)), rev8=rows(np.arange(NX, 0, -1)))
    consts = ("ident", "par", "sel", "delta", "rev64", "cmask", "ridx", "iota64", "rev8")
    return {k: np.ascontiguousarray(v.astype(np.float32) if k in consts else v) for k, v in maps.items()}


def kernel(**inputs):
    import concourse.bacc as _bacc
    from concourse.bass_utils import run_bass_kernel_spmd as _run

    nc = _bacc.Bacc("TRN2", target_bir_lowering=False, num_devices=1)
    arrays = _layout(inputs)
    args = {n: nc.dram_tensor("in_" + n, v.shape, F32, kind="ExternalInput").ap() for n, v in arrays.items()}
    out = nc.dram_tensor("out_0", (SLOTS, P, TILES, E), F32, kind="ExternalOutput").ap()
    build(nc, out=out, **args)
    r = _run(nc, [{"in_" + n: v for n, v in arrays.items()}], core_ids=[0])
    got = np.roll(np.asarray(r.results[0]["out_0"]), 1, axis=0)
    return np.ascontiguousarray(got.transpose(0, 2, 1, 3)).reshape(SLOTS * IMGS, L, E)
```
